# Optimizing a Trainium2 kernel written in Bass

```python
import numpy as np
import jax
import jax.numpy as jnp

def _softmax(x, axis=-1):
    return jax.nn.softmax(x, axis=axis)

def _gelu(x):
    return jax.nn.gelu(x, approximate=True)

def _silu(x):
    return jax.nn.silu(x)

def _sigmoid(x):
    return jax.nn.sigmoid(x)

def _layernorm(x, axis=-1, eps=1e-05):
    m = jnp.mean(x, axis=axis, keepdims=True)
    v = jnp.var(x, axis=axis, keepdims=True)
    return (x - m) / jnp.sqrt(v + eps)

def _scatter_add(tgt, idx, src, axis=0):
    return tgt.at[idx].add(src)

def _segment_sum(src, seg, n):
    return jax.ops.segment_sum(src, seg, n)
kernel_name = 'mk_conv_seq_d2_conv_nhwc384_r2_1a9451'

def setup_inputs(seed: int=0):
    np.random.seed(seed)
    _w = jnp.asarray

    def _rec_inputs():
        import jax
        import jax.numpy as jnp
        _gk = jax.random.key(seed)
        x = -0.0004039 + 1 * jax.random.normal(jax.random.fold_in(_gk, 1), (8, 32, 32, 192), jnp.float32)
        return x
    x = _rec_inputs()

    def _L0_conv_setup():
        import jax, jax.numpy as jnp
        import numpy as np
        DIM = 192
        H = 32
        W = 32
        NB = 8
        BS = DIM // NB
        WF = W // 2 + 1
        EPS = 1e-05

        def _layernorm(x, g, b):
            mu = jnp.mean(x, axis=-1, keepdims=True)
            var = jnp.mean(jnp.square(x - mu), axis=-1, keepdims=True)
            return (x - mu) * jax.lax.rsqrt(var + EPS) * g + b
        key = jax.random.key(seed)
        ks = jax.random.split(key, 8)
        scale = 0.02
        x = jax.random.normal(ks[0], (8, H, W, DIM), dtype=jnp.float32)
        w1 = scale * jax.random.normal(ks[1], (H, WF, NB, BS, BS, 2), dtype=jnp.float32)
        b1 = scale * jax.random.normal(ks[2], (H, WF, NB, BS, 2), dtype=jnp.float32)
        norm1_w = jnp.ones((DIM,), jnp.float32)
        norm1_b = jnp.zeros((DIM,), jnp.float32)
        norm2_w = jnp.ones((DIM,), jnp.float32)
        norm2_b = jnp.zeros((DIM,), jnp.float32)
        lim1 = 1.0 / np.sqrt(DIM)
        lim2 = 1.0 / np.sqrt(4 * DIM)
        mlp_w1 = jax.random.uniform(ks[3], (DIM, 4 * DIM), jnp.float32, -lim1, lim1)
        mlp_b1 = jax.random.uniform(ks[4], (4 * DIM,), jnp.float32, -lim1, lim1)
        mlp_w2 = jax.random.uniform(ks[5], (4 * DIM, DIM), jnp.float32, -lim2, lim2)
        mlp_b2 = jax.random.uniform(ks[6], (DIM,), jnp.float32, -lim2, lim2)
        return {'x': x, 'w1': w1, 'b1': b1, 'norm1_w': norm1_w, 'norm1_b': norm1_b, 'norm2_w': norm2_w, 'norm2_b': norm2_b, 'mlp_w1': mlp_w1, 'mlp_b1': mlp_b1, 'mlp_w2': mlp_w2, 'mlp_b2': mlp_b2}
    _L0_conv_all = _L0_conv_setup()
    _L0_conv_in = {k: v for k, v in _L0_conv_all.items() if k in ('w1', 'b1', 'norm1_w', 'norm1_b', 'norm2_w', 'norm2_b', 'mlp_w1', 'mlp_b1', 'mlp_w2', 'mlp_b2')}
    del _L0_conv_all

    def _L1_conv_setup():
        import jax, jax.numpy as jnp
        import numpy as np
        B, H, W, C, T = (16, 32, 32, 192, 8)
        HID = int(4.0 * C)
        EPS = 1e-06

        def _ln(x, scale, bias):
            mu = jnp.mean(x, axis=-1, keepdims=True)
            var = jnp.mean(jnp.square(x - mu), axis=-1, keepdims=True)
            return (x - mu) * jax.lax.rsqrt(var + EPS) * scale + bias
        key = jax.random.key(seed)
        ks = jax.random.split(key, 8)
        w = lambda k, shape: jax.random.normal(k, shape, jnp.float32) * 0.02
        return {'x': jax.random.normal(ks[0], (B, H, W, C), jnp.float32), 'norm1_scale': jnp.ones((C,), jnp.float32), 'norm1_bias': jnp.zeros((C,), jnp.float32), 'Wu': w(ks[1], (C, C)), 'bu': jnp.zeros((C,), jnp.float32), 'Wg': w(ks[2], (C, C)), 'bg': jnp.zeros((C,), jnp.float32), 'A': w(ks[3], (C, C)), 'norm2_scale': jnp.ones((C,), jnp.float32), 'norm2_bias': jnp.zeros((C,), jnp.float32), 'mlp_w1': w(ks[4], (C, HID)), 'mlp_b1': jnp.zeros((HID,), jnp.float32), 'mlp_w2': w(ks[5], (HID, C)), 'mlp_b2': jnp.zeros((C,), jnp.float32)}
    _L1_conv_all = _L1_conv_setup()
    _L1_conv_in = {k: v for k, v in _L1_conv_all.items() if k in ('norm1_scale', 'norm1_bias', 'Wu', 'bu', 'Wg', 'bg', 'A', 'norm2_scale', 'norm2_bias', 'mlp_w1', 'mlp_b1', 'mlp_w2', 'mlp_b2')}
    del _L1_conv_all
    return {'x': x, 'L0_conv_w1': _L0_conv_in['w1'], 'L0_conv_b1': _L0_conv_in['b1'], 'L0_conv_norm1_w': _L0_conv_in['norm1_w'], 'L0_conv_norm1_b': _L0_conv_in['norm1_b'], 'L0_conv_norm2_w': _L0_conv_in['norm2_w'], 'L0_conv_norm2_b': _L0_conv_in['norm2_b'], 'L0_conv_mlp_w1': _L0_conv_in['mlp_w1'], 'L0_conv_mlp_b1': _L0_conv_in['mlp_b1'], 'L0_conv_mlp_w2': _L0_conv_in['mlp_w2'], 'L0_conv_mlp_b2': _L0_conv_in['mlp_b2'], 'L1_conv_norm1_scale': _L1_conv_in['norm1_scale'], 'L1_conv_norm1_bias': _L1_conv_in['norm1_bias'], 'L1_conv_Wu': _L1_conv_in['Wu'], 'L1_conv_bu': _L1_conv_in['bu'], 'L1_conv_Wg': _L1_conv_in['Wg'], 'L1_conv_bg': _L1_conv_in['bg'], 'L1_conv_A': _L1_conv_in['A'], 'L1_conv_norm2_scale': _L1_conv_in['norm2_scale'], 'L1_conv_norm2_bias': _L1_conv_in['norm2_bias'], 'L1_conv_mlp_w1': _L1_conv_in['mlp_w1'], 'L1_conv_mlp_b1': _L1_conv_in['mlp_b1'], 'L1_conv_mlp_w2': _L1_conv_in['mlp_w2'], 'L1_conv_mlp_b2': _L1_conv_in['mlp_b2']}

def reference(x, L0_conv_w1, L0_conv_b1, L0_conv_norm1_w, L0_conv_norm1_b, L0_conv_norm2_w, L0_conv_norm2_b, L0_conv_mlp_w1, L0_conv_mlp_b1, L0_conv_mlp_w2, L0_conv_mlp_b2, L1_conv_norm1_scale, L1_conv_norm1_bias, L1_conv_Wu, L1_conv_bu, L1_conv_Wg, L1_conv_bg, L1_conv_A, L1_conv_norm2_scale, L1_conv_norm2_bias, L1_conv_mlp_w1, L1_conv_mlp_b1, L1_conv_mlp_w2, L1_conv_mlp_b2):
    import jax
    import jax.numpy as jnp

    def _L0_conv_ref(x, w1, b1, norm1_w, norm1_b, norm2_w, norm2_b, mlp_w1, mlp_b1, mlp_w2, mlp_b2):
        import jax, jax.numpy as jnp
        import numpy as np
        DIM = 192
        H = 32
        W = 32
        NB = 8
        BS = DIM // NB
        WF = W // 2 + 1
        EPS = 1e-05

        def _layernorm(x, g, b):
            mu = jnp.mean(x, axis=-1, keepdims=True)
            var = jnp.mean(jnp.square(x - mu), axis=-1, keepdims=True)
            return (x - mu) * jax.lax.rsqrt(var + EPS) * g + b
        B, h, w, C = x.shape
        residual = x
        xn = _layernorm(x, norm1_w, norm1_b)
        xf = jnp.fft.rfft2(xn.astype(jnp.float32), axes=(1, 2), norm='ortho')
        xf = xf.reshape(B, h, w // 2 + 1, NB, BS)
        w1c = jax.lax.complex(w1[..., 0], w1[..., 1])
        b1c = jax.lax.complex(b1[..., 0], b1[..., 1])
        o1 = jnp.einsum('bhwni,hwnio->bhwno', xf, w1c) + b1c
        o1 = jax.lax.complex(jax.nn.relu(o1.real), jax.nn.relu(o1.imag))
        o1 = o1.reshape(B, h, w // 2 + 1, C)
        xs = jnp.fft.irfft2(o1, s=(h, w), axes=(1, 2), norm='ortho')
        xm = _layernorm(xs, norm2_w, norm2_b)
        hdn = jax.nn.gelu(xm @ mlp_w1 + mlp_b1, approximate=False)
        mlp_out = hdn @ mlp_w2 + mlp_b2
        return xs + residual + mlp_out

    def _L1_conv_ref(x, norm1_scale, norm1_bias, Wu, bu, Wg, bg, A, norm2_scale, norm2_bias, mlp_w1, mlp_b1, mlp_w2, mlp_b2):
        import jax, jax.numpy as jnp
        import numpy as np
        B, H, W, C, T = (16, 32, 32, 192, 8)
        HID = int(4.0 * C)
        EPS = 1e-06

        def _ln(x, scale, bias):
            mu = jnp.mean(x, axis=-1, keepdims=True)
            var = jnp.mean(jnp.square(x - mu), axis=-1, keepdims=True)
            return (x - mu) * jax.lax.rsqrt(var + EPS) * scale + bias
        xn = _ln(x, norm1_scale, norm1_bias)
        u = jnp.einsum('bhwc,cd->bhwd', xn, Wu) + bu
        g = jax.nn.sigmoid(jnp.einsum('bhwc,cd->bhwd', xn, Wg) + bg)

        def step(h, _):
            h = g * jnp.einsum('bhwc,cd->bhwd', h, A) + (1.0 - g) * u
            return (h, None)
        h_last, _ = jax.lax.scan(step, jnp.zeros_like(u), None, length=T)
        x = x + h_last
        xn2 = _ln(x, norm2_scale, norm2_bias)
        m = jax.nn.gelu(jnp.einsum('bhwc,cf->bhwf', xn2, mlp_w1) + mlp_b1)
        m = jnp.einsum('bhwf,fc->bhwc', m, mlp_w2) + mlp_b2
        return x + m

    def _gn(v, G=32, eps=1e-05):
        B_, H_, W_, C_ = v.shape
        g = v.reshape(B_, H_, W_, G, C_ // G)
        m = jnp.mean(g, axis=(1, 2, 4), keepdims=True)
        s = jnp.var(g, axis=(1, 2, 4), keepdims=True)
        return ((g - m) / jnp.sqrt(s + eps)).reshape(v.shape)

    def _ln_c(v, eps=1e-06):
        m = jnp.mean(v, axis=-1, keepdims=True)
        s = jnp.var(v, axis=-1, keepdims=True)
        return (v - m) / jnp.sqrt(s + eps)

    def _ln_t(v, eps=1e-05):
        m = jnp.mean(v, axis=-1, keepdims=True)
        s = jnp.var(v, axis=-1, keepdims=True)
        return (v - m) / jnp.sqrt(s + eps)

    def _to_tokens(v):
        B_, H_, W_, C_ = v.shape
        return v.reshape(B_, H_ * W_, C_)

    def _from_tokens(t, like):
        return t.reshape(like.shape)
    x = _L0_conv_ref(x, L0_conv_w1, L0_conv_b1, L0_conv_norm1_w, L0_conv_norm1_b, L0_conv_norm2_w, L0_conv_norm2_b, L0_conv_mlp_w1, L0_conv_mlp_b1, L0_conv_mlp_w2, L0_conv_mlp_b2)
    x = _L1_conv_ref(x, L1_conv_norm1_scale, L1_conv_norm1_bias, L1_conv_Wu, L1_conv_bu, L1_conv_Wg, L1_conv_bg, L1_conv_A, L1_conv_norm2_scale, L1_conv_norm2_bias, L1_conv_mlp_w1, L1_conv_mlp_b1, L1_conv_mlp_w2, L1_conv_mlp_b2)
    return x

_drawn_inputs = setup_inputs


def setup_inputs(seed=0):
    import zlib

    import numpy as np

    out = dict(_drawn_inputs(seed))
    spreads = {'L0_conv_norm1_w': (1.0, 0.2),
     'L0_conv_norm1_b': (0.0, 0.417),
     'L0_conv_norm2_w': (1.0, 0.2),
     'L0_conv_norm2_b': (0.0, 0.378),
     'L1_conv_norm1_scale': (1.0, 0.595),
     'L1_conv_norm1_bias': (0.0, 0.55),
     'L1_conv_bu': (0.0, 0.1),
     'L1_conv_bg': (0.0, 0.8),
     'L1_conv_norm2_scale': (1.0, 0.6),
     'L1_conv_norm2_bias': (0.0, 0.8),
     'L1_conv_mlp_b1': (0.0, 0.295),
     'L1_conv_mlp_b2': (0.0, 0.1)}
    factors = {'L0_conv_mlp_b1': 3.903, 'L0_conv_mlp_b2': 2.671, 'L1_conv_Wg': 2.778, 'L1_conv_A': 2.748}
    for name, (base, spread) in spreads.items():
        noise = np.random.default_rng([zlib.crc32(name.encode()), seed]).standard_normal(out[name].shape)
        drawn = base * np.exp(spread * noise) if base else spread * noise
        out[name] = jnp.asarray(drawn.astype(out[name].dtype))
    for name, factor in factors.items():
        out[name] = (out[name] * factor).astype(out[name].dtype)
    return out
```

```python
import itertools
from contextlib import ExitStack

import numpy as np

import concourse.bass as bass
from concourse import mybir

F32 = mybir.dt.float32
F32R = mybir.dt.float32r
ALU = mybir.AluOpType
ACT = mybir.ActivationFunctionType

P = 128
B, H, W, C = 8, 32, 32, 192
WF = W // 2 + 1
NB, BS = 8, 24
HID = 4 * C
TOK = B * H * W
NT = TOK // P
TPB = NT // B
HH = P // W
HALF = C // 2
NH = NB // 2
NG = WF // 2
GT = 4
NGRP = NT // GT
GTOK = GT * P
MT = HID // P
C1 = C - P
STEPS = 8
EPS0, EPS1 = 1e-5, 1e-6


def dft_tables():
    h = np.arange(H)
    th = 2 * np.pi * np.outer(h, h) / H
    co, si = np.cos(th) / np.sqrt(H), np.sin(th) / np.sqrt(H)
    fw, iw = np.zeros((W, W)), np.zeros((W, W))
    for k in range(W // 2):
        fw[:, 2 * k] = co[:, k]
        iw[2 * k, :] = co[k] * (1 if k == 0 else 2)
        if k:
            fw[:, 2 * k + 1] = -si[:, k]
            iw[2 * k + 1, :] = -2 * si[k]
    fw[:, 1], iw[1, :] = co[:, W // 2], co[W // 2]
    eye = np.eye(HH)
    fwd_w, inv_w = np.kron(eye, fw), np.kron(eye, iw)
    fc = np.block([[co, -si], [si, co]])
    ic = np.block([[co, si], [-si, co]])
    z = np.zeros((2 * H, 2 * H))
    fwd_h = np.block([[fc, z], [z, fc]])
    inv_h = np.block([[ic, z], [z, ic]])
    fwd_h0 = np.zeros((P, 3 * 2 * H))
    fwd_h0[0:H, 0:2 * H] = fc[0:H]
    fwd_h0[2 * H:, 2 * H:4 * H] = fc
    fwd_h0[H:2 * H, 4 * H:] = fc[0:H]
    return [a.astype(np.float32) for a in (fwd_w, inv_w, fwd_h, fwd_h0, inv_h)]


def block_ones():
    s = np.zeros((NH, 2, NH, B, 2 * H))
    for n in range(NH):
        s[n, 0, n] = 1
    return s.reshape(NH, -1).astype(np.float32)


def passed(eng, sem, value):
    if not isinstance(value, int) or value > 0:
        eng.wait_ge(sem, value)


def words(tile_):
    return itertools.cycle([tile_[:, k:k + 1] for k in range(tile_.shape[1])])


def held(nc, dve, scratch, sem, value):
    passed(dve, sem, value)
    nc.vector.memset(next(scratch), 0.0)


def rolled(eng, count, body, head=1, tail=2):
    for i in range(head):
        body(i)
    with eng.Fori(head, count - tail) as i:
        body(i)
    for i in range(count - tail, count):
        body(i)


def build(nc, t, out):
    ctx = ExitStack()
    with ctx:
        X = ctx.enter_context(nc.sbuf_tensor("X", [P, NT, C], F32))
        mv = ctx.enter_context(nc.sbuf_tensor("mv", [P, NT, 2], F32))
        ident = ctx.enter_context(nc.sbuf_tensor("ident", [P, P], F32))
        F1 = nc.dram_tensor("rows_spectrum", [W, H, B, C], F32, kind="Internal").ap()
        F2 = nc.dram_tensor("rows_mixed", [B, H, W, C], F32, kind="Internal").ap()
        fourier(nc, t, X, F1, F2)
        with nc.sbuf_tensor("XS", [P, NT, C], F32) as XS:
            inverse_rows(nc, t, X, XS, mv, ident, F2)
            mlp(nc, t, "L0_conv_", "norm2_w", "norm2_b", ACT.Gelu, EPS0, XS, X, mv, ident, None)
        gated_scan(nc, t, X, mv, ident)
        mlp(nc, t, "L1_conv_", "norm2_scale", "norm2_bias", ACT.Gelu_apprx_tanh, EPS1, X, X, mv, ident, out)


def fourier(nc, t, X, F1, F2):
    with ExitStack() as ctx:
        def sb(name, shape, dt=F32):
            return ctx.enter_context(nc.sbuf_tensor(name, shape, dt))

        def sem(name):
            return ctx.enter_context(nc.semaphore(name))

        fwd_w = sb("fwd_w", [P, P])
        fwd_h = sb("fwd_h", [P, P])
        fwd_h0 = sb("fwd_h0", [P, 6 * H])
        inv_h = sb("inv_h", [P, P])
        gamma = sb("gamma", [HALF, 2])
        beta = sb("beta", [HALF, 2])
        dc = sb("dc", [HALF, 2])
        st = sb("st", [P, TPB, 6])
        mvb = sb("mvb", [P, TPB, 2])
        scratch = words(sb("scratch", [P, 16]))
        sd = sb("sd", [P, TPB])
        rs = sb("rs", [P, TPB])
        xn = [sb(f"xn{s}", [P, TPB, C]) for s in range(2)]
        d1 = [sb(f"d1{s}", [P, TPB, C]) for s in range(2)]
        d2 = sb("d2", [P, B, C])
        xh = [sb(f"xh{s}", [HALF, 2, B, 2 * H]) for s in range(2)]
        x16 = [sb(f"x16{s}", [HALF, 2, B, H]) for s in range(2)]
        S = [sb(f"S{s}", [HALF + NH, 2 * NH * B, 2 * H]) for s in range(2)]
        Wt = [sb(f"Wt{s}", [HALF + NH, 2, H, 2 * BS]) for s in range(2)]
        cross = [sb(f"cross{s}", [P, 8, BS]) for s in range(2)]
        Y = sb("Y", [P, H, BS])
        Yt = sb("Yt", [P, BS, H])
        Z = sb("Z", [P, B, 2, HALF])
        d3 = sb("d3", [P, B * C])
        ps = ctx.enter_context(nc.psum_tensor("psF", [P, 8, 512], F32))

        consts, zeroed, ones_in = sem("consts"), sem("zeroed"), sem("ones_in")
        x_in = [sem(f"x_in{s}") for s in range(2)]
        stats, aggr, eps_in, rooted, recip, normed = (sem(n) for n in ("stats", "aggr", "eps_in", "rooted", "recip", "normed"))
        rows_done, d1_done, dc_done = sem("rows_done"), sem("d1_done"), sem("dc_done")
        f1_out = [sem(f"f1_out{s}") for s in range(2)]
        d2_in, hdft, xh_done, k16_dft, k16_done = sem("d2_in"), sem("hdft"), sem("xh_done"), sem("k16_dft"), sem("k16_done")
        s_in = [sem(f"s_in{s}") for s in range(2)]
        w_in = [sem(f"w_in{s}") for s in range(2)]
        mixed, crossed, summed, turned, relu = sem("mixed"), sem("crossed"), sem("summed"), sem("turned"), sem("relu")
        inv_done, d3_done, f2_out = sem("inv_done"), sem("d3_done"), sem("f2_out")

        x_v = t["x"].rearrange("b (t hh) w c -> b (hh w) t c", hh=HH)
        f1_w = F1.rearrange("k (t hh) b c -> hh b k t c", hh=HH)
        f1_r = F1.rearrange("(g q) h b c -> g (q h) (b c)", q=4)
        f2_w = F2.rearrange("b h k c -> k h b c")
        w_v = t["L0_conv_w1"].rearrange("h k (s n) i o r -> s k (n i) h (o r)", s=2)
        b_v = t["L0_conv_b1"].rearrange("h k (s n) o r -> s k n h (o r)", s=2)
        N_CONST = 4 + 4
        UNITS = 2 * (NG + 1)

        block = ctx.enter_context(nc.Block())

        def load_weights(eng, g, s, bins=2):
            for k in range(bins):
                eng.dma_start(Wt[s][0:HALF, k], w_v[s, 2 * g + k]).then_inc(w_in[s], 16)
                eng.dma_start(Wt[s][HALF:HALF + NH, k], b_v[s, 2 * g + k]).then_inc(w_in[s], 16)

        def expand(eng, s, src, bins=2):
            for n in range(NH):
                rows = slice(n * BS, (n + 1) * BS)
                dst = S[s][rows].rearrange("p (r n b) f -> p r n b f", r=2, n=NH)[:, :, n, :, 0:bins * H]
                if bins == 2:
                    eng.dma_start(dst, src[rows]).then_inc(s_in[s], 16)
                else:
                    for r in range(2):
                        eng.dma_start(dst[:, r], src[rows, r]).then_inc(s_in[s], 16)

        @block.sync
        def _(sp):
            sp.dma_start(fwd_w[:, :], t["fwd_w"]).then_inc(consts, 16)
            sp.dma_start(fwd_h[:, :], t["fwd_h"]).then_inc(consts, 16)
            sp.dma_start(fwd_h0[:, :], t["fwd_h0"]).then_inc(consts, 16)
            sp.dma_start(inv_h[:, :], t["inv_h"]).then_inc(consts, 16)
            for s in range(2):
                sp.dma_start(gamma[:, s:s + 1], t["L0_conv_norm1_w"].rearrange("(s c o) -> s c o", s=2, o=1)[s]).then_inc(consts, 16)
                sp.dma_start(beta[:, s:s + 1], t["L0_conv_norm1_b"].rearrange("(s c o) -> s c o", s=2, o=1)[s]).then_inc(consts, 16)

            def image(i, s):
                b = 2 * i + s
                passed(sp, x_in[s], 16 * i)
                sp.dma_start(X[:, bass.ds(b * TPB, TPB), :], x_v[b]).then_inc(x_in[s], 16)

            def store_rows(i, s):
                b = 2 * i + s
                sp.wait_ge(d1_done, (b + 1) * 4)
                for hh in range(HH):
                    sp.dma_start(f1_w[hh, b], d1[s][hh * W:(hh + 1) * W]).then_inc(f1_out[s], 16)

            for s in range(2):
                image(0, s)
            with sp.Fori(1, B // 2) as i:
                for s in range(2):
                    image(i, s)
                    store_rows(i - 1, s)
            for s in range(2):
                store_rows(B // 2 - 1, s)
            for s in range(2):
                sp.wait_ge(f1_out[s], 16 * HH * B // 2)

            def spectrum_rows(g):
                sp.dma_start(d2[:, :, :], f1_r[g]).then_inc(d2_in, 16)

            def store_mixed(g):
                sp.wait_ge(d3_done, 4 * (g + 1))
                for q in range(4):
                    if not (isinstance(g, int) and g == 0 and q == 1):
                        sp.dma_start(f2_w[4 * g + q], d3[q * H:(q + 1) * H, :].rearrange("p (b c) -> p b c", b=B)).then_inc(f2_out, 16)

            spectrum_rows(0)
            sp.wait_ge(zeroed, 3)
            for s in range(2):
                sp.dma_start(S[s][HALF:HALF + NH].rearrange("p a f -> p (a f)"), t["block_ones"]).then_inc(ones_in, 16)
            for s in range(2):
                sp.wait_ge(xh_done, 4 * (s + 1))
                expand(sp, s, xh[s])
            sp.wait_ge(k16_dft, 2)
            spectrum_rows(1)

            def group(g, last=False):
                for s in range(2):
                    sp.wait_ge(mixed, 4 * (2 * g + s + 1))
                    if last:
                        load_weights(sp, g + 1, s, 1)
                        expand(sp, s, x16[s], 1)
                    else:
                        load_weights(sp, g + 1, s)
                        sp.wait_ge(xh_done, 4 * (2 * (g + 1) + s + 1))
                        expand(sp, s, xh[s])
                    if s == 0 and not (isinstance(g, int) and g == 0):
                        store_mixed(g - 1)
                if not last and not (isinstance(g, int) and g == NG - 2):
                    sp.wait_ge(hdft, 2 * 2 * (g + 2))
                    spectrum_rows(g + 2)

            group(0)
            group(1)
            with sp.Fori(2, NG - 2) as g:
                group(g)
            group(NG - 2)
            group(NG - 1, True)
            store_mixed(NG - 1)
            sp.wait_ge(d3_done, 4 * (NG + 1))
            sp.dma_start(f2_w[1], d3[0:H, :].rearrange("p (b c) -> p b c", b=B)).then_inc(f2_out, 16)
            sp.wait_ge(f2_out, 16 * 4 * NG)

        @block.gpsimd
        def _(pool):
            nc.gpsimd.memset(S[0][:, :, :], 0.0).then_inc(zeroed, 1)

        @block.scalar
        def _(act):
            for s in range(2):
                load_weights(act, 0, s)

            def root(b):
                act.wait_ge(eps_in, b + 1)
                nc.scalar.activation(sd[:, :], mvb[:, :, 1], ACT.Sqrt).then_inc(rooted, 1)

            def rows_out(i, s):
                b = 2 * i + s
                for q in range(4):
                    act.wait_ge(rows_done, 4 * b + q + 1)
                    if q == 0:
                        passed(act, f1_out[s], 16 * HH * i)
                    nc.scalar.activation(d1[s][:, 2 * q:2 * q + 2, :],
                                         ps[:, 4 * s + q, 0:2 * C].rearrange("p (t c) -> p t c", t=2),
                                         ACT.Copy).then_inc(d1_done, 1)

            def pair(i, last=False):
                root(2 * i + 1)
                rows_out(i, 0)
                if not last:
                    root(2 * i + 2)
                rows_out(i, 1)

            root(0)
            pair(0)
            with act.Fori(1, B // 2 - 1) as i:
                pair(i)
            pair(B // 2 - 1, True)

            def unit(u, bins=2):
                for j in range(4):
                    act.wait_ge(mixed, 4 * u + j + 1)
                    passed(act, summed, 4 * u + j - 1)
                    v = ps[:, j, 0:8 * 2 * BS].rearrange("p (h o r) -> p h o r", h=8, r=2)
                    for k in range(bins):
                        re, im = 2 * k * H, (2 * k + 1) * H
                        nc.scalar.activation(cross[j % 2][re:re + H], v[im:im + H, :, :, 1], ACT.Copy,
                                             scale=-1.0).then_inc(crossed, 1)
                        nc.scalar.activation(cross[j % 2][im:im + H], v[re:re + H, :, :, 1],
                                             ACT.Copy).then_inc(crossed, 1)

            unit(0)
            with act.Fori(1, 2 * NG) as u:
                unit(u)
            for u in range(2 * NG, UNITS):
                unit(u, 1)

        @block.vector
        def _(dve):
            nc.vector.memset(S[1][:, :, :], 0.0).then_inc(zeroed, 1)
            nc.vector.memset(Y[:, :, :], 0.0).then_inc(zeroed, 1)
            dve.wait_ge(consts, 16 * N_CONST)
            nc.vector.tensor_scalar(dc[:, :], beta[:, :], float(np.sqrt(H * W)), None, ALU.mult).then_inc(dc_done, 1)

            def measure(i, s):
                b = 2 * i + s
                dve.wait_ge(x_in[s], 16 * (i + 1))
                held(nc, dve, scratch, aggr, TPB * b)
                for k in range(TPB):
                    nc.vector.bn_stats(st[:, k, :], X[:, b * TPB + k, :]).then_inc(stats, 1)
                passed(dve, normed, TPB * b)
                held(nc, dve, scratch, stats, TPB * (b + 1))
                for k in range(TPB):
                    nc.vector.bn_aggr(mvb[:, k, :], st[:, k, :]).then_inc(aggr, 1)
                dve.wait_ge(aggr, TPB * (b + 1))
                nc.vector.tensor_scalar(mvb[:, :, 1], mvb[:, :, 1], EPS0, None, ALU.add).then_inc(eps_in, 1)

            def normalise(i, s):
                b = 2 * i + s
                dve.wait_ge(rooted, b + 1)
                nc.vector.reciprocal(rs[:, :], sd[:, :]).then_inc(recip, 1)
                dve.wait_ge(recip, b + 1)
                passed(dve, rows_done, 4 * (b - 1))
                for k in range(TPB):
                    nc.vector.tensor_scalar(xn[s][:, k, :], X[:, b * TPB + k, :], mvb[:, k, 0:1], rs[:, k:k + 1],
                                            ALU.subtract, ALU.mult).then_inc(normed, 1)

            def pair(i):
                for s in range(2):
                    measure(i, s)
                    normalise(i, s)

            pair(0)
            with dve.Fori(1, B // 2) as i:
                pair(i)

            def channels_out(u, s, g0=False):
                for q in range(2):
                    dve.wait_ge(hdft, 2 * u + q + 1)
                    if q == 0 and not g0:
                        dve.wait_ge(s_in[s], 16 * NH * (u // 2 if isinstance(u, int) else (u - s) // 2))
                    v = ps[0:HALF, 4 + q, :].rearrange("p (b k r h) -> p r b k h", b=4, k=2, r=2)
                    for r in range(2):
                        nc.vector.tensor_scalar(
                            xh[s][:, r, 4 * q:4 * q + 4, :].rearrange("p b (k h) -> p b k h", k=2),
                            v[:, r], gamma[:, s:s + 1], None, ALU.mult).then_inc(xh_done if not g0 else k16_done, 1)

            for s in range(2):
                channels_out(s, s, True)
                dve.wait_ge(k16_done, 7 * s + 4)
                dve.wait_ge(dc_done, 1)
                nc.vector.tensor_scalar(xh[s][:, 0, :, 0], xh[s][:, 0, :, 0], dc[:, s:s + 1], None,
                                        ALU.add).then_inc(xh_done, 4)
                dve.wait_ge(k16_dft, s + 1)
                v = ps[0:HALF, 6 + s, :].rearrange("p (b r h) -> p r b h", b=B, r=2)
                for r in range(2):
                    nc.vector.tensor_scalar(x16[s][:, r], v[:, r], gamma[:, s:s + 1], None,
                                            ALU.mult).then_inc(k16_done, 1)
                if s == 0:
                    nc.vector.tensor_scalar(dc[:, 0:1], dc[:, 0:1], 1.0, None, ALU.mult).then_inc(k16_done, 1)

            def unit(u, s, g, bins=2):
                for j in range(4):
                    dve.wait_ge(crossed, (16 * u + 4 * (j + 1)) if bins == 2 else
                                16 * 2 * NG + 8 * (u - 2 * NG) + 2 * (j + 1))
                    if j == 0:
                        passed(dve, turned, u)
                    v = ps[:, j, 0:8 * 2 * BS].rearrange("p (h o r) -> p h o r", h=8, r=2)
                    n = 2 * H * bins
                    nc.vector.tensor_tensor(Y[0:n, 8 * j:8 * j + 8, :], v[0:n, :, :, 0], cross[j % 2][0:n],
                                            ALU.add).then_inc(summed, 1)
                dve.wait_ge(summed, 4 * (u + 1))
                passed(dve, relu, u)
                nc.vector.transpose(Yt[:, :, :], Y[:, :, :].rearrange("p h o -> p o h")).then_inc(turned, 1)
                dve.wait_ge(turned, u + 1)
                passed(dve, inv_done, 4 * g)
                nc.vector.tensor_scalar(
                    Z[:, :, s, :].rearrange("p b (n o) -> p b n o", n=NH),
                    Yt[:, :, :].rearrange("p o (n b) -> p b n o", n=NH), 0.0, None, ALU.max).then_inc(relu, 1)

            def inverse_out(g):
                for j in range(4):
                    dve.wait_ge(inv_done, 4 * g + j + 1)
                    if j == 0:
                        passed(dve, f2_out, 16 * (4 * g - 1))
                    nc.vector.tensor_copy(d3[:, 384 * j:384 * j + 384], ps[:, 6 + j % 2, 0:384]).then_inc(d3_done, 1)

            def group(g):
                for s in range(2):
                    if not (isinstance(g, int) and g == NG - 1):
                        channels_out(2 * (g + 1) + s, s)
                    if s == 0 and not (isinstance(g, int) and g == 0):
                        inverse_out(g - 1)
                    unit(2 * g + s, s, g)

            group(0)
            group(1)
            with dve.Fori(2, NG - 1) as g:
                group(g)
            group(NG - 1)
            inverse_out(NG - 1)
            for s in range(2):
                unit(2 * NG + s, s, NG, 1)
            for j in range(4):
                dve.wait_ge(inv_done, 4 * NG + j + 1)
                if j == 0:
                    dve.wait_ge(f2_out, 16 * (4 * NG - 1))
                nc.vector.tensor_copy(d3[0:H, 384 * j:384 * j + 384], ps[0:H, 6 + j % 2, 0:384]).then_inc(d3_done, 1)

        @block.tensor
        def _(pe):
            pe.wait_ge(consts, 16 * N_CONST)

            def rows(i, s):
                b = 2 * i + s
                for q in range(4):
                    pe.wait_ge(normed, TPB * b + 2 * q + 2)
                    if q == 0:
                        passed(pe, d1_done, 4 * (b - 1))
                    pe.matmul(ps[:, 4 * s + q, 0:2 * C], fwd_w[:, :],
                              xn[s][:, 2 * q:2 * q + 2, :].rearrange("p t c -> p (t c)"),
                              start=True, stop=True).then_inc(rows_done, 1)

            for s in range(2):
                rows(0, s)
            with pe.Fori(1, B // 2) as i:
                for s in range(2):
                    rows(i, s)

            def columns(u, s, g):
                if s == 0:
                    pe.wait_ge(d2_in, 16 * (g + 1))
                for q in range(2):
                    if isinstance(g, int) and g == 0:
                        table = fwd_h0[:, 0:4 * H]
                        passed(pe, k16_done, 7 * s)
                    else:
                        table = fwd_h[:, :]
                        pe.wait_ge(xh_done, 4 * (u - 1) + 2 * q + 2)
                    for b in range(4):
                        mm = pe.matmul(ps[0:HALF, 4 + q, P * b:P * b + P],
                                       d2[:, 4 * q + b, HALF * s:HALF * s + HALF], table, start=True, stop=True)
                    mm.then_inc(hdft, 1)

            pe.wait_ge(d1_done, 4 * B)
            for s in range(2):
                columns(s, s, 0)
                for b in range(B):
                    mm = pe.matmul(ps[0:HALF, 6 + s, 2 * H * b:2 * H * b + 2 * H],
                                   d2[:, b, HALF * s:HALF * s + HALF], fwd_h0[:, 4 * H:], start=True, stop=True)
                mm.then_inc(k16_dft, 1)

            def products(u, s, g, bins=2):
                pe.wait_ge(s_in[s], 16 * NH * (g + 1) if bins == 2 else 16 * NH * (NG + 2))
                pe.wait_ge(w_in[s], 64 * (g + 1) if bins == 2 else 64 * NG + 32)
                if isinstance(g, int) and g == 0:
                    pe.wait_ge(ones_in, 32)
                for j in range(4):
                    passed(pe, summed, 4 * (u - 1) + j + 1)
                    for hl in range(8):
                        for k in range(bins):
                            h = 8 * j + hl
                            mm = pe.matmul(ps[2 * H * k:2 * H * k + 2 * H, j, 48 * hl:48 * hl + 48],
                                           S[s][:, :, k * H + h], Wt[s][:, k, h, :], start=True, stop=True)
                    mm.then_inc(mixed, 1)

            def inverse(g, rows=P, width=P):
                pe.wait_ge(relu, 2 * (g + 1))
                z = Z[0:rows].rearrange("p b s c -> p (b s c)")
                for j in range(4):
                    passed(pe, d3_done, 4 * g + j - 1)
                    pe.matmul(ps[0:width, 6 + j % 2, 0:384], inv_h[0:rows, 0:width], z[:, 384 * j:384 * j + 384],
                              start=True, stop=True).then_inc(inv_done, 1)

            def group(g):
                for s in range(2):
                    products(2 * g + s, s, g)
                    if not (isinstance(g, int) and g == NG - 1):
                        columns(2 * (g + 1) + s, s, g + 1)
                    if s == 0 and not (isinstance(g, int) and g == 0):
                        inverse(g - 1)

            pe.wait_ge(k16_done, 13)
            group(0)
            group(1)
            with pe.Fori(2, NG - 1) as g:
                group(g)
            group(NG - 1)
            inverse(NG - 1)
            for s in range(2):
                products(2 * NG + s, s, NG, 1)
            inverse(NG, 2 * H, H)


def inverse_rows(nc, t, X, XS, mv, ident, F2):
    with ExitStack() as ctx:
        def sb(name, shape, dt=F32):
            return ctx.enter_context(nc.sbuf_tensor(name, shape, dt))

        def sem(name):
            return ctx.enter_context(nc.semaphore(name))

        inv_w = sb("inv_w", [P, P])
        d4 = [sb(f"d4{s}", [P, TPB, C]) for s in range(2)]
        st = sb("st2", [P, TPB, 6])
        mvb = sb("mvb2", [P, TPB, 2])
        scratch = words(sb("scratch2", [P, 16]))
        filed = sem("i_filed")
        ps = ctx.enter_context(nc.psum_tensor("psI", [P, 8, 512], F32))
        consts = sem("i_consts")
        d4_in = [sem(f"d4_in{s}") for s in range(2)]
        rows_done, xs_done, stats, aggr, added = (sem(n) for n in ("i_rows", "i_xs", "i_stats", "i_aggr", "i_added"))
        f2_v = F2.rearrange("b (t hh) k c -> b (hh k) t c", hh=HH)
        block = ctx.enter_context(nc.Block())

        @block.sync
        def _(sp):
            sp.dma_start(inv_w[:, :], t["inv_w"]).then_inc(consts, 16)
            sp.dma_start(ident[:, :], t["ident"]).then_inc(consts, 16)

            def image(i, s):
                passed(sp, rows_done, 4 * (2 * i + s - 1))
                sp.dma_start(d4[s][:, :, :], f2_v[2 * i + s]).then_inc(d4_in[s], 16)

            for s in range(2):
                image(0, s)
            with sp.Fori(1, B // 2) as i:
                for s in range(2):
                    image(i, s)
            sp.wait_ge(consts, 32)

        @block.tensor
        def _(pe):
            pe.wait_ge(consts, 32)

            def image(i, s):
                pe.wait_ge(d4_in[s], 16 * (i + 1))
                passed(pe, xs_done, 4 * (2 * i + s - 1))
                for q in range(4):
                    pe.matmul(ps[:, 4 * s + q, 0:2 * C], inv_w[:, :],
                              d4[s][:, 2 * q:2 * q + 2, :].rearrange("p t c -> p (t c)"),
                              start=True, stop=True).then_inc(rows_done, 1)

            for s in range(2):
                image(0, s)
            with pe.Fori(1, B // 2) as i:
                for s in range(2):
                    image(i, s)

        @block.scalar
        def _(act):
            with act.Fori(0, B // 2) as i:
                for s in range(2):
                    b = 2 * i + s
                    for q in range(4):
                        act.wait_ge(rows_done, 4 * b + q + 1)
                        nc.scalar.activation(XS[:, bass.ds(b * TPB + 2 * q, 2), :],
                                             ps[:, 4 * s + q, 0:2 * C].rearrange("p (t c) -> p t c", t=2),
                                             ACT.Copy).then_inc(xs_done, 1)

        @block.vector
        def _(dve):
            dve.wait_ge(consts, 32)

            def image(b):
                passed(dve, aggr, TPB * b)
                for k in range(TPB):
                    if k % 2 == 0:
                        held(nc, dve, scratch, xs_done, 4 * b + k // 2 + 1)
                    nc.vector.bn_stats(st[:, k, :], XS[:, b * TPB + k, :]).then_inc(stats, 1)
                passed(dve, filed, b)
                held(nc, dve, scratch, stats, TPB * (b + 1))
                for k in range(TPB):
                    nc.vector.bn_aggr(mvb[:, k, :], st[:, k, :]).then_inc(aggr, 1)
                dve.wait_ge(aggr, TPB * (b + 1))
                nc.vector.tensor_scalar(mv[:, bass.ds(b * TPB, TPB), :], mvb[:, :, :], 1.0, None,
                                        ALU.mult).then_inc(filed, 1)

            image(0)
            with dve.Fori(1, B) as b:
                image(b)

        @block.gpsimd
        def _(pool):
            with pool.Fori(0, B) as b:
                pool.wait_ge(xs_done, 4 * (b + 1))
                nc.gpsimd.tensor_tensor(X[:, bass.ds(b * TPB, TPB), :], X[:, bass.ds(b * TPB, TPB), :],
                                        XS[:, bass.ds(b * TPB, TPB), :], ALU.add).then_inc(added, 1)


def split_weights(nc, act, dve_side, raw_hi_lo, loaded, count, hi_done, lo_done):
    eng, side = act, dve_side
    for n, (raw, hi, lo) in enumerate(raw_hi_lo):
        if side == "hi":
            if n == 0:
                eng.wait_ge(loaded, count)
            nc.scalar.activation(hi, raw, ACT.Copy).then_inc(hi_done, 1)
        else:
            eng.wait_ge(hi_done, n + 1)
            nc.vector.tensor_tensor(lo, raw, hi.bitcast(F32), ALU.subtract).then_inc(lo_done, 1)


def mlp(nc, t, pre, wname, bname, gelu, eps, SRC, X, mv, ident, out):
    with ExitStack() as ctx:
        def sb(name, shape, dt=F32):
            return ctx.enter_context(nc.sbuf_tensor(pre + name, shape, dt))

        def sem(name):
            return ctx.enter_context(nc.semaphore(pre + name))

        raw1 = sb("raw1", [P, 2, HID])
        raw2 = sb("raw2", [P, MT, C])
        w1h, w1l = sb("w1h", [P, 2, HID], F32R), sb("w1l", [P, 2, HID], F32R)
        w2hl = sb("w2hl", [P, MT, 2, C], F32R)
        b1 = sb("b1", [P, MT])
        b2 = sb("b2", [P, C])
        gam, bet = sb("gam", [P, 2]), sb("bet", [P, 2])
        sd, rs = sb("sd", [P, NT]), sb("rs", [P, NT])
        xn = sb("xn", [P, GT, 2 * P])
        y = sb("y", [P, 2, GTOK])
        thi, tlo = sb("thi", [P, GTOK], F32R), sb("tlo", [P, GTOK], F32R)
        tst = sb("tst", [P, GTOK], F32R)
        hf = sb("hf", [P, 3, GTOK])
        hhi, hlo = sb("hhi", [P, MT, GTOK], F32R), sb("hlo", [P, MT, GTOK], F32R)
        part = sb("part", [P, 2, C])
        st = sb("st", [P, GT, 6])
        mvb = sb("mvb", [P, GT, 2])
        scratch = words(sb("scratch", [P, 16]))
        filed = sem("filed")
        ps = ctx.enter_context(nc.psum_tensor(pre + "ps", [P, 8, 512], F32))
        TB, RB, AB = 0, 2, 4

        (loaded, w_hi, w_lo, eps_in, rooted, recip, normed, tposed, y_done, t_hi, t_lo, fc1, act1, h_hi, h_lo, fc2,
         parted, x_done, stats, aggr, biased) = (sem(n) for n in (
             "loaded", "w_hi", "w_lo", "eps_in", "rooted", "recip", "normed", "tposed", "y_done", "t_hi", "t_lo",
             "fc1", "act1", "h_hi", "h_lo", "fc2", "parted", "x_done", "stats", "aggr", "biased"))
        stored = sem("stored")
        N = NGRP
        col = lambda v, a, b: t[v][a:b].rearrange("(c o) -> c o", o=1)
        loads = [
            (raw1[:, 0, :], t[pre + "mlp_w1"][0:P]),
            (raw1[0:C1, 1, :], t[pre + "mlp_w1"][P:C]),
            (raw1[C1:P, 1, :], t[pre + "mlp_w1"][P:C]),
            (raw2[:, :, :], t[pre + "mlp_w2"].rearrange("(m p) c -> p m c", p=P)),
            (b1[:, :], t[pre + "mlp_b1"].rearrange("(m p) -> p m", p=P)),
            (b2[:, :], t[pre + "mlp_b2"].rearrange("(o c) -> o c", o=1).to_broadcast([P, C])),
        ]
        for tile_, name in ((gam, wname), (bet, bname)):
            loads += [(tile_[:, 0:1], col(pre + name, 0, P)), (tile_[0:C1, 1:2], col(pre + name, P, C)),
                      (tile_[C1:P, 1:2], col(pre + name, P, C))]
        splits = [(raw1[:, 0, :], w1h[:, 0, :], w1l[:, 0, :]), (raw1[:, 1, :], w1h[:, 1, :], w1l[:, 1, :]),
                  (raw2[:, :, :], w2hl[:, :, 0, :], w2hl[:, :, 1, :])]

        block = ctx.enter_context(nc.Block())

        @block.sync
        def _(sp):
            with nc.allow_non_contiguous_dma(reason="bias columns"):
                for dst, src in loads:
                    sp.dma_start(dst, src).then_inc(loaded, 16)
            if out is not None:
                o_v = out.rearrange("b (t hh) w c -> (hh w) (b t) c", hh=HH)

                def store(i):
                    sp.wait_ge(x_done, GT * (i + 1))
                    sp.dma_start(o_v[:, bass.ds(GT * i, GT), :], X[:, bass.ds(GT * i, GT), :]).then_inc(stored, 16)

                with sp.Fori(0, N) as i:
                    store(i)
                sp.wait_ge(stored, 16 * N)
            sp.wait_ge(loaded, 16 * len(loads))

        @block.gpsimd
        def _(pool):
            pool.wait_ge(loaded, 16 * len(loads))
            with pool.Fori(0, N) as i:
                pool.wait_ge(normed, GT * (i + 1))
                for k in range(GT):
                    nc.gpsimd.tensor_tensor(X[:, GT * i + k, :], X[:, GT * i + k, :], b2[:, :],
                                            ALU.add).then_inc(biased, 1)

        @block.scalar
        def _(act):
            act.wait_ge(eps_in, 1)
            nc.scalar.activation(sd[:, :], sd[:, :], ACT.Sqrt).then_inc(rooted, 1)
            split_weights(nc, act, "hi", splits, loaded, 16 * len(loads), w_hi, w_lo)

            def channels(i):
                for k in range(2):
                    act.wait_ge(tposed, 2 * i + k + 1)
                    passed(act, t_lo, 2 * (i - 1) + k + 1)
                    nc.scalar.activation(y[:, k, :], ps[:, TB + k, :], ACT.Identity, bias=bet[:, k:k + 1],
                                         scale=gam[:, k:k + 1]).then_inc(y_done, 1)
                for k, dst in enumerate((thi, tst)):
                    act.wait_ge(y_done, 2 * i + k + 1)
                    passed(act, fc1, MT * i)
                    nc.scalar.activation(dst[:, :], y[:, k, :], ACT.Copy).then_inc(t_hi, 1)

            def hidden(i, m):
                n = MT * i + m
                act.wait_ge(fc1, n + 1)
                passed(act, h_lo, n - 2)
                nc.scalar.activation(hf[:, m % 3, :], ps[:, RB + m % 2, :], gelu,
                                     bias=b1[:, m:m + 1]).then_inc(act1, 1)

            def high(i, m):
                n = MT * i + m
                act.wait_ge(act1, n + 1)
                if m == 0:
                    passed(act, fc2, GT * i)
                nc.scalar.activation(hhi[:, m, :], hf[:, m % 3, :], ACT.Copy).then_inc(h_hi, 1)

            def group(i):
                channels(i)
                for m in range(MT):
                    hidden(i, m)
                    if m:
                        high(i, m - 1)
                high(i, MT - 1)

            rolled(act, N, group, 1, 0)

        @block.vector
        def _(dve):
            nc.vector.tensor_scalar(sd[:, :], mv[:, :, 1], eps, None, ALU.add).then_inc(eps_in, 1)
            dve.wait_ge(rooted, 1)
            nc.vector.reciprocal(rs[:, :], sd[:, :]).then_inc(recip, 1)
            dve.wait_ge(recip, 1)

            def normalise(i):
                passed(dve, tposed, 2 * i)
                for k in range(GT):
                    n = GT * i + k
                    for to, fr in ((slice(0, C), slice(0, C)), (slice(C, 2 * P), slice(P, C))):
                        ins = nc.vector.tensor_scalar(xn[:, k, to], SRC[:, n, fr], mv[:, n, 0:1],
                                                      rs[:, bass.ds(n, 1)], ALU.subtract, ALU.mult)
                    ins.then_inc(normed, 1)

            normalise(0)
            split_weights(nc, dve, "lo", splits, loaded, 16 * len(loads), w_hi, w_lo)

            def low_channels(i):
                dve.wait_ge(t_hi, 2 * i + 1)
                nc.vector.tensor_tensor(tlo[:, :], y[:, 0, :], thi[:, :].bitcast(F32), ALU.subtract).then_inc(t_lo, 1)
                dve.wait_ge(t_hi, 2 * i + 2)
                nc.vector.tensor_tensor(tst[C1:P, :], y[C1:P, 1, :], tst[C1:P, :].bitcast(F32),
                                        ALU.subtract).then_inc(t_lo, 1)

            def low_hidden(i, m):
                dve.wait_ge(h_hi, MT * i + m + 1)
                nc.vector.tensor_tensor(hlo[:, m, :], hf[:, m % 3, :], hhi[:, m, :].bitcast(F32),
                                        ALU.subtract).then_inc(h_lo, 1)

            def output(i, k):
                n = GT * i + k
                dve.wait_ge(fc2, n + 1)
                dve.wait_ge(biased, n + 1)
                passed(dve, x_done, n - 1)
                nc.vector.tensor_tensor(part[:, k % 2, :], ps[:, AB + k, 0:C], X[:, n, :], ALU.add).then_inc(parted, 1)
                dve.wait_ge(parted, n + 1)
                nc.vector.tensor_tensor(X[:, n, :], ps[:, AB + k, C:2 * C], part[:, k % 2, :],
                                        ALU.add).then_inc(x_done, 1)

            def measure(i, k):
                if out is None:
                    n = GT * i + k
                    if k == 0:
                        passed(dve, aggr, GT * i)
                    held(nc, dve, scratch, x_done, n + 1)
                    nc.vector.bn_stats(st[:, k, :], X[:, n, :]).then_inc(stats, 1)

            def collect(i):
                if out is None:
                    passed(dve, filed, i)
                    held(nc, dve, scratch, stats, GT * (i + 1))
                    for k in range(GT):
                        nc.vector.bn_aggr(mvb[:, k, :], st[:, k, :]).then_inc(aggr, 1)
                    dve.wait_ge(aggr, GT * (i + 1))
                    nc.vector.tensor_scalar(mv[:, bass.ds(GT * i, GT), :], mvb[:, :, :], 1.0, None,
                                            ALU.mult).then_inc(filed, 1)

            def group(i):
                head = isinstance(i, int) and i == 0
                low_channels(i)
                if not (isinstance(i, int) and i == N - 1):
                    normalise(i + 1)
                for m in range(MT):
                    if not head and m < GT:
                        output(i - 1, m)
                    if not head and 1 <= m <= GT:
                        measure(i - 1, m - 1)
                    low_hidden(i, m)
                if not head:
                    collect(i - 1)

            rolled(dve, N, group, 2, 1)
            for k in range(GT):
                output(N - 1, k)
            for k in range(GT):
                measure(N - 1, k)
            collect(N - 1)

        @block.tensor
        def _(pe):
            pe.wait_ge(w_hi, len(splits))

            def turn(i):
                for k in range(2):
                    passed(pe, y_done, 2 * (i - 1) + k + 1)
                    for j in range(GT):
                        if k == 0:
                            pe.wait_ge(normed, GT * i + j + 1)
                            src = xn[:, j, 0:P]
                        else:
                            src = xn[:, j, P:2 * P]
                        mm = pe.transpose(ps[:, TB + k, P * j:P * j + P], src, ident[:, :])
                    mm.then_inc(tposed, 1)

            def first(i):
                for m in range(MT):
                    n = MT * i + m
                    cut = slice(P * m, P * m + P)
                    passed(pe, act1, n - 1)
                    terms = [(w1h[:, 0, cut], thi), (w1l[:, 0, cut], thi), (w1h[:, 1, cut], tst),
                             (w1l[:, 1, cut], tst), (w1h[:, 0, cut], tlo)]
                    if m == 0:
                        pe.wait_ge(t_hi, 2 * i + 1)
                    for q, (w, x) in enumerate(terms):
                        if m == 0 and q == 2:
                            pe.wait_ge(t_lo, 2 * i + 2)
                        mm = pe.matmul(ps[:, RB + m % 2, :], w, x[:, :], start=(q == 0), stop=(q == 4))
                    mm.then_inc(fc1, 1)

            def second(i):
                passed(pe, x_done, GT * i)
                for m in range(MT):
                    pe.wait_ge(h_lo, MT * i + m + 1)
                    for k in range(GT):
                        cut = slice(P * k, P * k + P)
                        full = (hhi[:, m, cut], w2hl[:, m].rearrange("p a c -> p (a c)"), ps[:, AB + k, 0:2 * C])
                        low = (hlo[:, m, cut], w2hl[:, m, 0, :], ps[:, AB + k, C:2 * C])
                        for n, (x, w, o) in enumerate((full, low) if m == 0 else (low, full)):
                            mm = pe.matmul(o, x, w, start=(m == 0 and n == 0), stop=(m == MT - 1 and n == 1),
                                           skip_group_check=True)
                        if m == MT - 1:
                            mm.then_inc(fc2, 1)

            turn(0)
            pe.wait_ge(w_lo, len(splits))
            first(0)

            def group(i):
                turn(i + 1)
                second(i)
                first(i + 1)

            rolled(pe, N - 1, group, 1, 0)
            second(N - 1)


def gated_scan(nc, t, X, mv, ident):
    pre = "L1_conv_"
    with ExitStack() as ctx:
        def sb(name, shape, dt=F32):
            return ctx.enter_context(nc.sbuf_tensor("sc_" + name, shape, dt))

        def sem(name):
            return ctx.enter_context(nc.semaphore("sc_" + name))

        NSET = NT // (2 * GT)
        raw = sb("raw", [P, 3, 6, P])
        wh, wl = sb("wh", [P, 3, 6, P], F32R), sb("wl", [P, 3, 6, P], F32R)
        U, G, A = 0, 1, 2
        W00, W10A, W10B, W01A, W01B, W11 = range(6)
        gam, bet, bu, bg = (sb(n, [P, 2]) for n in ("gam", "bet", "bu", "bg"))
        sd, rs = sb("sd", [P, NT]), sb("rs", [P, NT])
        xn = [sb(f"xn{c}", [P, GT, 3 * P]) for c in range(2)]
        gate = [sb(f"gate{c}", [P, 3, GTOK]) for c in range(2)]
        nfix = [sb(f"nfix{c}", [P, 3, GTOK]) for c in range(2)]
        prod = [sb(f"prod{c}", [P, 3, GTOK]) for c in range(2)]
        hid = [sb(f"hid{c}", [P, 3, GTOK]) for c in range(2)]
        hi = [sb(f"hi{c}", [P, 3, GTOK], F32R) for c in range(2)]
        lo = [sb(f"lo{c}", [P, 3, GTOK], F32R) for c in range(2)]
        st = sb("st", [P, 2 * GT, 6])
        mvb = sb("mvb", [P, 2 * GT, 2])
        scratch = words(sb("scratch", [P, 16]))
        filed = sem("filed")
        ps = ctx.enter_context(nc.psum_tensor("sc_ps", [P, 8, 512], F32))
        loaded, zeroed, w_hi, w_lo, eps_in, rooted, recip, stats, aggr, turned_back = (sem(n) for n in (
            "loaded", "zeroed", "w_hi", "w_lo", "eps_in", "rooted", "recip", "stats", "aggr", "turned_back"))
        x_done = sem("x_done")
        names = ("normed", "tposed", "y_done", "y_hi", "y_lo", "mm", "u_out", "g_out", "fixed", "mult", "h_done",
                 "h_hi", "h_lo")
        Q = [{n: sem(f"{n}{c}") for n in names} for c in range(2)]
        col = lambda v, a, b: t[pre + v][a:b].rearrange("(c o) -> c o", o=1)
        loads = []
        for j, v in ((U, "Wu"), (G, "Wg"), (A, "A")):
            w = t[pre + v]
            loads += [
                (raw[:, j, W00, :], w[0:P, 0:P]),
                (raw[0:C1, j, W10A, :], w[P:C, 0:P]), (raw[C1:P, j, W10B, :], w[P:C, 0:P]),
                (raw[:, j, W01A, 0:C1], w[0:P, P:C]), (raw[:, j, W01B, C1:P], w[0:P, P:C]),
                (raw[0:C1, j, W11, 0:C1], w[P:C, P:C]), (raw[C1:P, j, W11, C1:P], w[P:C, P:C])]
        for tile_, v in ((gam, "norm1_scale"), (bet, "norm1_bias"), (bu, "bu"), (bg, "bg")):
            loads += [(tile_[:, 0:1], col(v, 0, P)), (tile_[0:C1, 1:2], col(v, P, C)), (tile_[C1:P, 1:2], col(v, P, C))]
        splits = [(raw[:, j].rearrange("p a b -> p (a b)"), wh[:, j].rearrange("p a b -> p (a b)"),
                   wl[:, j].rearrange("p a b -> p (a b)")) for j in range(3)]
        MM = 3 * (2 + STEPS - 1)
        HL = 3 * (STEPS - 1)

        block = ctx.enter_context(nc.Block())

        @block.sync
        def _(sp):
            sp.wait_ge(zeroed, 1)
            for dst, src in loads:
                sp.dma_start(dst, src).then_inc(loaded, 16)
            sp.wait_ge(loaded, 16 * len(loads))

        @block.gpsimd
        def _(pool):
            nc.gpsimd.memset(raw[:, :, :, :], 0.0).then_inc(zeroed, 1)

        def tile_of(j):
            return 0 if j < 2 else 1

        @block.scalar
        def _(act):
            act.wait_ge(eps_in, 1)
            nc.scalar.activation(sd[:, :], sd[:, :], ACT.Sqrt).then_inc(rooted, 1)
            split_weights(nc, act, "hi", splits, loaded, 16 * len(loads), w_hi, w_lo)

            def channels(i, c):
                q = Q[c]
                for j in range(3):
                    act.wait_ge(q["tposed"], 3 * i + j + 1)
                    k = tile_of(j)
                    nc.scalar.activation(hid[c][:, j, :], ps[:, 3 * c + j, :], ACT.Identity, bias=bet[:, k:k + 1],
                                         scale=gam[:, k:k + 1]).then_inc(q["y_done"], 1)
                for j in range(3):
                    act.wait_ge(q["y_done"], 3 * i + j + 1)
                    nc.scalar.activation(hi[c][:, j, :], hid[c][:, j, :], ACT.Copy).then_inc(q["y_hi"], 1)

            def branch(i, c, dst, bias, func, base, done):
                q = Q[c]
                for j in range(3):
                    act.wait_ge(q["mm"], MM * i + base + j + 1)
                    k = tile_of(j)
                    nc.scalar.activation(dst[c][:, j, :], ps[:, 3 * c + j, :], func,
                                         bias=bias[:, k:k + 1]).then_inc(q[done], 1)

            def high(i, c, s):
                q = Q[c]
                act.wait_ge(q["mm"], MM * i + 3 * (s + 2))
                for j in range(3):
                    if s == 0:
                        act.wait_ge(q["fixed"], 3 * i + j + 1)
                        nc.scalar.activation(hi[c][:, j, :], nfix[c][:, j, :], ACT.Copy,
                                             scale=-1.0).then_inc(q["h_hi"], 1)
                    else:
                        act.wait_ge(q["h_done"], HL * i + 3 * (s - 1) + j + 1)
                        nc.scalar.activation(hi[c][:, j, :], hid[c][:, j, :], ACT.Copy).then_inc(q["h_hi"], 1)

            with act.Fori(0, NSET // 2) as i:
                for c in range(2):
                    channels(i, c)
                for c in range(2):
                    branch(i, c, prod, bu, ACT.Identity, 0, "u_out")
                for c in range(2):
                    branch(i, c, gate, bg, ACT.Sigmoid, 3, "g_out")
                    high(i, c, 0)
                for s in range(1, STEPS - 1):
                    for c in range(2):
                        high(i, c, s)

        @block.vector
        def _(dve):
            nc.vector.tensor_scalar(sd[:, :], mv[:, :, 1], EPS1, None, ALU.add).then_inc(eps_in, 1)
            dve.wait_ge(rooted, 1)
            nc.vector.reciprocal(rs[:, :], sd[:, :]).then_inc(recip, 1)
            dve.wait_ge(recip, 1)

            def normalise(i, c):
                q = Q[c]
                passed(dve, q["tposed"], 3 * i)
                for j in range(GT):
                    for k in range(2):
                        n = (2 * i + c) * 2 * GT + GT * k + j
                        for to, fr in ((slice(P * k, P * k + P), slice(0, P)),
                                       (slice(2 * P + C1 * k, 2 * P + C1 * k + C1), slice(P, C))):
                            ins = nc.vector.tensor_scalar(xn[c][:, j, to], X[:, n, fr], mv[:, n, 0:1],
                                                          rs[:, bass.ds(n, 1)], ALU.subtract, ALU.mult)
                        ins.then_inc(q["normed"], 1)

            for c in range(2):
                normalise(0, c)
            split_weights(nc, dve, "lo", splits, loaded, 16 * len(loads), w_hi, w_lo)

            def low_channels(i, c):
                q = Q[c]
                for j in range(3):
                    dve.wait_ge(q["y_hi"], 3 * i + j + 1)
                    nc.vector.tensor_tensor(lo[c][:, j, :], hid[c][:, j, :], hi[c][:, j, :].bitcast(F32),
                                            ALU.subtract).then_inc(q["y_lo"], 1)

            def fix(i, c):
                q = Q[c]
                for j in range(3):
                    dve.wait_ge(q["u_out"], 3 * i + j + 1)
                    dve.wait_ge(q["g_out"], 3 * i + j + 1)
                    nc.vector.scalar_tensor_tensor(nfix[c][:, j, :], gate[c][:, j, :], 1.0, prod[c][:, j, :],
                                                   ALU.subtract, ALU.mult).then_inc(q["fixed"], 1)
                for j in range(3):
                    dve.wait_ge(q["h_hi"], HL * i + j + 1)
                    nc.vector.scalar_tensor_tensor(lo[c][:, j, :], nfix[c][:, j, :], -1.0, hi[c][:, j, :].bitcast(F32),
                                                   ALU.mult, ALU.subtract).then_inc(q["h_lo"], 1)

            def step(i, c, s):
                q = Q[c]

                def update(j):
                    n = HL * i + 3 * (s - 1) + j + 1
                    dve.wait_ge(q["mm"], MM * i + 3 * (s + 1) + j + 1)
                    nc.vector.tensor_tensor(prod[c][:, j, :], ps[:, 3 * c + j, :], gate[c][:, j, :],
                                            ALU.mult).then_inc(q["mult"], 1)
                    dve.wait_ge(q["mult"], n)
                    nc.vector.tensor_tensor(hid[c][:, j, :], prod[c][:, j, :], nfix[c][:, j, :],
                                            ALU.subtract).then_inc(q["h_done"], 1)

                def low(j):
                    dve.wait_ge(q["h_hi"], HL * i + 3 * s + j + 1)
                    nc.vector.tensor_tensor(lo[c][:, j, :], hid[c][:, j, :], hi[c][:, j, :].bitcast(F32),
                                            ALU.subtract).then_inc(q["h_lo"], 1)

                update(0)
                update(1)
                if s < STEPS - 1:
                    low(0)
                    update(2)
                    low(1)
                    low(2)
                else:
                    update(2)

            def finish(i, c):
                m = 2 * i + c
                for j in range(GT):
                    dve.wait_ge(turned_back, GT * m + j + 1)
                    tile0 = m * 2 * GT + j
                    v = ps[:, 6 + j % 2, 0:3 * P]
                    for a, (lo_c, hi_c, part) in enumerate(((0, P, v[:, 0:2 * P]), (P, C, v[:, 2 * P:]))):
                        dst = X[:, bass.ds(m * 2 * GT, 2 * GT), lo_c:hi_c].rearrange("p (k j) c -> p k j c", k=2)[:, :, j]
                        nc.vector.tensor_tensor(dst, dst, part.rearrange("p (k c) -> p k c", k=2),
                                                ALU.add).then_inc(x_done, 1)
                passed(dve, aggr, 2 * GT * m)
                for j in range(GT):
                    held(nc, dve, scratch, x_done, 2 * GT * m + 2 * j + 2)
                    for k in range(2):
                        nc.vector.bn_stats(st[:, GT * k + j, :], X[:, m * 2 * GT + GT * k + j, :]).then_inc(stats, 1)
                passed(dve, filed, m)
                held(nc, dve, scratch, stats, 2 * GT * (m + 1))
                for k in range(2 * GT):
                    nc.vector.bn_aggr(mvb[:, k, :], st[:, k, :]).then_inc(aggr, 1)
                dve.wait_ge(aggr, 2 * GT * (m + 1))
                nc.vector.tensor_scalar(mv[:, bass.ds(m * 2 * GT, 2 * GT), :], mvb[:, :, :], 1.0, None,
                                        ALU.mult).then_inc(filed, 1)

            def both(i):
                last = isinstance(i, int) and i == NSET // 2 - 1
                for c in range(2):
                    low_channels(i, c)
                if not last:
                    for c in range(2):
                        normalise(i + 1, c)
                for c in range(2):
                    fix(i, c)
                for s in range(1, STEPS):
                    for c in range(2):
                        step(i, c, s)
                for c in range(2):
                    finish(i, c)

            rolled(dve, NSET // 2, both, 1, 1)

        @block.tensor
        def _(pe):
            pe.wait_ge(w_hi, 3)

            def turn(i, c):
                q = Q[c]
                for j in range(3):
                    for k in range(GT):
                        if j == 0:
                            pe.wait_ge(q["normed"], 2 * GT * i + 2 * k + 2)
                        mm = pe.transpose(ps[:, 3 * c + j, P * k:P * k + P], xn[c][:, k, P * j:P * j + P], ident[:, :])
                    mm.then_inc(q["tposed"], 1)

            def product(c, w, before):
                q = Q[c]
                h, l = hi[c], lo[c]
                for j in range(3):
                    if j < 2:
                        cross = W10A if j == 0 else W10B
                        terms = [(wh, W00, h, j), (wl, W00, h, j), (wh, cross, h, 2), (wl, cross, h, 2),
                                 (wh, W00, l, j), (wh, cross, l, 2)]
                    else:
                        terms = [(wh, W01A, h, 0), (wl, W01A, h, 0), (wh, W01A, l, 0), (wh, W01B, h, 1),
                                 (wl, W01B, h, 1), (wh, W01B, l, 1), (wh, W11, h, 2), (wl, W11, h, 2), (wh, W11, l, 2)]
                    for n, (ww, cut, x, xj) in enumerate(terms):
                        if n == 0:
                            before(j)
                        mm = pe.matmul(ps[:, 3 * c + j, :], ww[:, w, cut, :], x[:, xj, :], start=(n == 0),
                                       stop=(n == len(terms) - 1))
                    mm.then_inc(q["mm"], 1)

            def turn_back(i, c):
                m = 2 * i + c
                q = Q[c]
                for k in range(GT):
                    passed(pe, x_done, 2 * (GT * m + k - 1) if isinstance(m, int) else 2 * GT * m + 2 * (k - 1))
                    for j in range(3):
                        if k == 0:
                            pe.wait_ge(q["h_done"], HL * i + 3 * (STEPS - 2) + j + 1)
                        mm = pe.transpose(ps[:, 6 + k % 2, P * j:P * j + P], hid[c][:, j, P * k:P * k + P], ident[:, :])
                    mm.then_inc(turned_back, 1)

            def both(i):
                for c in range(2):
                    turn(i, c)
                if isinstance(i, int):
                    pe.wait_ge(w_lo, 3)
                for c in range(2):
                    q = Q[c]

                    def ready(j, q=q):
                        if j == 0:
                            pe.wait_ge(q["y_lo"], 3 * i + 3)
                    product(c, U, ready)
                for c in range(2):
                    q = Q[c]

                    def ready(j, q=q):
                        pe.wait_ge(q["u_out"], 3 * i + j + 1)
                    product(c, G, ready)
                for s in range(1, STEPS):
                    for c in range(2):
                        q = Q[c]

                        def ready(j, q=q):
                            if j == 0:
                                pe.wait_ge(q["h_lo"], HL * i + 3 * s)
                        product(c, A, ready)
                for c in range(2):
                    turn_back(i, c)

            rolled(pe, NSET // 2, both, 1, 0)


_OUT = (B, H, W, C)


def kernel(**inputs):
    import concourse.bacc as _bacc
    from concourse.bass_utils import run_bass_kernel_spmd as _run

    nc = _bacc.Bacc("TRN2", target_bir_lowering=False, num_devices=1)
    arrays = {k: np.ascontiguousarray(v) for k, v in inputs.items()}
    arrays |= dict(zip(("fwd_w", "inv_w", "fwd_h", "fwd_h0", "inv_h"), dft_tables()))
    arrays |= {"block_ones": block_ones(), "ident": np.eye(P, dtype=np.float32)}
    t = {k: nc.dram_tensor(f"in_{k}", a.shape, mybir.dt.from_np(a.dtype), kind="ExternalInput").ap()
         for k, a in arrays.items()}
    out = nc.dram_tensor("out_0", _OUT, F32, kind="ExternalOutput").ap()
    build(nc, t, out)
    r = _run(nc, [{f"in_{k}": a for k, a in arrays.items()}], core_ids=[0])
    return r.results[0]["out_0"]
```

```python
import itertools
from contextlib import ExitStack

import numpy as np

import concourse.bass as bass
from concourse import mybir

F32 = mybir.dt.float32
F32R = mybir.dt.float32r
ALU = mybir.AluOpType
ACT = mybir.ActivationFunctionType

P = 128
B, H, W, C = 8, 32, 32, 192
WF = W // 2 + 1
NB, BS = 8, 24
HID = 4 * C
TOK = B * H * W
NT = TOK // P
TPB = NT // B
HH = P // W
HALF = C // 2
NH = NB // 2
NG = WF // 2
GT = 4
NGRP = NT // GT
GTOK = GT * P
MT = HID // P
C1 = C - P
STEPS = 8
EPS0, EPS1 = 1e-5, 1e-6


def dft_tables():
    h = np.arange(H)
    th = 2 * np.pi * np.outer(h, h) / H
    co, si = np.cos(th) / np.sqrt(H), np.sin(th) / np.sqrt(H)
    fw, iw = np.zeros((W, W)), np.zeros((W, W))
    for k in range(W // 2):
        fw[:, 2 * k] = co[:, k]
        iw[2 * k, :] = co[k] * (1 if k == 0 else 2)
        if k:
            fw[:, 2 * k + 1] = -si[:, k]
            iw[2 * k + 1, :] = -2 * si[k]
    fw[:, 1], iw[1, :] = co[:, W // 2], co[W // 2]
    eye = np.eye(HH)
    fwd_w, inv_w = np.kron(eye, fw), np.kron(eye, iw)
    fc = np.block([[co, -si], [si, co]])
    ic = np.block([[co, si], [-si, co]])
    z = np.zeros((2 * H, 2 * H))
    fwd_h = np.block([[fc, z], [z, fc]])
    inv_h = np.block([[ic, z], [z, ic]])
    fwd_h0 = np.zeros((P, 3 * 2 * H))
    fwd_h0[0:H, 0:2 * H] = fc[0:H]
    fwd_h0[2 * H:, 2 * H:4 * H] = fc
    fwd_h0[H:2 * H, 4 * H:] = fc[0:H]
    return [a.astype(np.float32) for a in (fwd_w, inv_w, fwd_h, fwd_h0, inv_h)]


def block_ones():
    s = np.zeros((NH, 2, NH, B, 2 * H))
    for n in range(NH):
        s[n, 0, n] = 1
    return s.reshape(NH, -1).astype(np.float32)


def passed(eng, sem, value):
    if not isinstance(value, int) or value > 0:
        eng.wait_ge(sem, value)


def words(tile_):
    return itertools.cycle([tile_[:, k:k + 1] for k in range(tile_.shape[1])])


def held(nc, dve, scratch, sem, value):
    passed(dve, sem, value)
    nc.vector.memset(next(scratch), 0.0)


def rolled(eng, count, body, head=1, tail=2):
    for i in range(head):
        body(i)
    with eng.Fori(head, count - tail) as i:
        body(i)
    for i in range(count - tail, count):
        body(i)


class Shared:

    def __init__(self, nc, ctx, t):
        sb = lambda name, shape, dt=F32: ctx.enter_context(nc.sbuf_tensor(name, shape, dt))
        self.nc, self.t = nc, t
        self.X = sb("X", [P, NT, C])
        self.mv = sb("mv", [P, NT, 2])
        self.ident = sb("ident", [P, P])
        self.inv_w = sb("inv_w", [P, P])
        self.sem = lambda name: ctx.enter_context(nc.semaphore(name))
        self.columns = {}
        for pre, names in (("L0_conv_", ("norm2_w", "norm2_b")),
                           ("L1_conv_", ("norm1_scale", "norm1_bias", "bu", "bg", "norm2_scale", "norm2_bias"))):
            for name in names:
                self.columns[pre + name] = sb("v_" + pre + name, [P, 2])
        self.b1 = {pre: sb(pre + "b1", [P, MT]) for pre in ("L0_conv_", "L1_conv_")}
        self.b2 = {pre: sb(pre + "b2", [P, C]) for pre in ("L0_conv_", "L1_conv_")}
        self.vectors_in = self.sem("vectors_in")

    def load_vectors(self, eng):
        t, n = self.t, 0
        loads = [(self.ident[:, :], t["ident"]), (self.inv_w[:, :], t["inv_w"])]
        for name, tile_ in self.columns.items():
            col = lambda a, b: t[name][a:b].rearrange("(c o) -> c o", o=1)
            loads += [(tile_[:, 0:1], col(0, P)), (tile_[0:C1, 1:2], col(P, C)), (tile_[C1:P, 1:2], col(P, C))]
        for pre in self.b1:
            loads += [(self.b1[pre][:, :], t[pre + "mlp_b1"].rearrange("(m p) -> p m", p=P)),
                      (self.b2[pre][:, :], t[pre + "mlp_b2"].rearrange("(o c) -> o c", o=1).to_broadcast([P, C]))]
        with self.nc.allow_non_contiguous_dma(reason="vectors as columns"):
            for dst, src in loads:
                eng.dma_start(dst, src).then_inc(self.vectors_in, 16)
        return len(loads)

    def weights(self, ctx):
        sb = lambda name, shape, dt=F32: ctx.enter_context(self.nc.sbuf_tensor(name, shape, dt))
        self.raw = sb("raw", [P, 2 * HID + MT * C])
        self.w1h, self.w1l = sb("w1h", [P, 2, HID], F32R), sb("w1l", [P, 2, HID], F32R)
        self.w2hl = sb("w2hl", [P, MT, 2, C], F32R)
        self.wh, self.wl = (sb(n, [P, 3, SCAN_W], F32R) for n in ("wh", "wl"))

    def mlp_loads(self, pre):
        t = self.t
        raw1 = self.raw[:, 0:2 * HID].rearrange("p (k f) -> p k f", k=2)
        raw2 = self.raw[:, 2 * HID:].rearrange("p (m c) -> p m c", m=MT)
        return [(raw1[:, 0, :], t[pre + "mlp_w1"][0:P]),
                (raw1[0:C1, 1, :], t[pre + "mlp_w1"][P:C]),
                (raw1[C1:P, 1, :], t[pre + "mlp_w1"][P:C]),
                (raw2, t[pre + "mlp_w2"].rearrange("(m p) c -> p m c", p=P))]

    def mlp_splits(self):
        raw1 = self.raw[:, 0:2 * HID].rearrange("p (k f) -> p k f", k=2)
        raw2 = self.raw[:, 2 * HID:].rearrange("p (m c) -> p m c", m=MT)
        return [(raw1[:, 0, :], self.w1h[:, 0, :], self.w1l[:, 0, :]),
                (raw1[:, 1, :], self.w1h[:, 1, :], self.w1l[:, 1, :]),
                (raw2, self.w2hl[:, :, 0, :], self.w2hl[:, :, 1, :])]

    def scan_loads(self):
        loads = []
        for j, name in enumerate(("Wu", "Wg", "A")):
            raw, w = self.raw[:, j * SCAN_W:(j + 1) * SCAN_W], self.t["L1_conv_" + name]
            loads += [(raw[:, W00], w[0:P, 0:P]), (raw[0:C1, W10], w[P:C, 0:P]), (raw[C1:P, W10], w[P:C, 0:P]),
                      (raw[:, W01_LOWER.start:W01_UPPER.stop], w[0:P, P:C]), (raw[0:C1, W11.start:W11.start + C1], w[P:C, P:C]),
                      (raw[C1:P, W11.start + C1:W11.stop], w[P:C, P:C])]
        return loads

    def scan_splits(self):
        return [(self.raw[:, j * SCAN_W:(j + 1) * SCAN_W], self.wh[:, j, :], self.wl[:, j, :]) for j in range(3)]


W00, W10 = slice(0, P), slice(P, 2 * P)
W01_UPPER, W01_LOWER = slice(2 * P, 3 * P), slice(2 * P + C1, 3 * P + C1)
W11 = slice(3 * P + C1, 4 * P + C1)
SCAN_W = W11.stop


def build(nc, t, out):
    with ExitStack() as ctx:
        sh = Shared(nc, ctx, t)
        F1 = nc.dram_tensor("rows_spectrum", [W, H, B, C], F32, kind="Internal").ap()
        F2 = nc.dram_tensor("rows_mixed", [B, H, W, C], F32, kind="Internal").ap()
        fourier(nc, t, sh, F1, F2)
        sh.weights(ctx)
        with nc.sbuf_tensor("XS", [P, NT, C], F32) as XS:
            inverse_rows(nc, t, sh, XS, F2)
            mlp(nc, t, sh, "L0_conv_", "norm2_w", "norm2_b", ACT.Gelu, EPS0, XS, None)
        gated_scan(nc, t, sh)
        mlp(nc, t, sh, "L1_conv_", "norm2_scale", "norm2_bias", ACT.Gelu_apprx_tanh, EPS1, None, out)


def fourier(nc, t, sh, F1, F2):
    X = sh.X
    with ExitStack() as ctx:
        def sb(name, shape, dt=F32):
            return ctx.enter_context(nc.sbuf_tensor(name, shape, dt))

        def sem(name):
            return ctx.enter_context(nc.semaphore(name))

        fwd_w = sb("fwd_w", [P, P])
        fwd_h = sb("fwd_h", [P, P])
        fwd_h0 = sb("fwd_h0", [P, 6 * H])
        inv_h = sb("inv_h", [P, P])
        gamma = sb("gamma", [HALF, 2])
        beta = sb("beta", [HALF, 2])
        dc = sb("dc", [HALF, 2])
        st = sb("st", [P, TPB, 6])
        mvb = [sb(f"mvb{s}", [P, TPB, 2]) for s in range(2)]
        scratch = words(sb("scratch", [P, 16]))
        sd, rs, shift = ([sb(f"{n}{s}", [P, TPB]) for s in range(2)] for n in ("sd", "rs", "shift"))
        row_bufs = [sb(f"row_bufs{s}", [P, 2, TPB, C]) for s in range(2)]
        xn = [row_bufs[0][:, s] for s in range(2)]
        d1 = [row_bufs[1][:, s] for s in range(2)]
        d2 = sb("d2", [P, B, C])
        xh = [sb(f"xh{s}", [HALF, 2, B, 2 * H]) for s in range(2)]
        x16 = [sb(f"x16{s}", [HALF, 2, B, H]) for s in range(2)]
        S = [sb(f"S{s}", [HALF + NH, 2 * NH * B, 2 * H]) for s in range(2)]
        Wt = [[sb(f"Wt{s}", [HALF + NH, 2, H, 2 * BS]) for s in range(2)],
              [row_bufs[s][0:HALF + NH].rearrange("p a t c -> p (a t c)").rearrange("p (k h c) -> p k h c", k=2, h=H)
               for s in range(2)]]
        cross = [sb(f"cross{s}", [P, 8, BS]) for s in range(2)]
        Y = sb("Y", [P, H, BS])
        Yt = sb("Yt", [P, BS, H])
        Z = sb("Z", [P, B, 2, HALF])
        d3 = sb("d3", [P, B * C])
        ps = ctx.enter_context(nc.psum_tensor("psF", [P, 8, 512], F32))

        consts, zeroed, ones_in, row_table = sem("consts"), sem("zeroed"), sem("ones_in"), sem("row_table")
        x_in = [sem(f"x_in{s}") for s in range(2)]
        stats, aggr, eps_in, rooted, recip, normed = (sem(n) for n in ("stats", "aggr", "eps_in", "rooted", "recip", "normed"))
        rows_done, d1_done, dc_done = sem("rows_done"), sem("d1_done"), sem("dc_done")
        f1_out = [sem(f"f1_out{s}") for s in range(2)]
        d2_in, hdft, xh_done, k16_dft, k16_done = sem("d2_in"), sem("hdft"), sem("xh_done"), sem("k16_dft"), sem("k16_done")
        s_in = [sem(f"s_in{s}") for s in range(2)]
        w_in = [[sem(f"w_in{p}{s}") for s in range(2)] for p in range(2)]
        normed_a, x_biased = sem("normed_a"), sem("x_biased")
        mixed, crossed, summed, turned, relu = sem("mixed"), sem("crossed"), sem("summed"), sem("turned"), sem("relu")
        inv_done, d3_done, f2_out = sem("inv_done"), sem("d3_done"), sem("f2_out")

        x_v = t["x"].rearrange("b (t hh) w c -> b (hh w) t c", hh=HH)
        f1_w = F1.rearrange("k (t hh) b c -> hh b k t c", hh=HH)
        f1_r = F1.rearrange("(g q) h b c -> g (q h) (b c)", q=4)
        f2_w = F2.rearrange("b h k c -> k h b c")
        w_v = t["L0_conv_w1"].rearrange("h k (s n) i o r -> s k (n i) h (o r)", s=2)
        b_v = t["L0_conv_b1"].rearrange("h k (s n) o r -> s k n h (o r)", s=2)
        N_CONST = 3 + 4
        UNITS = 2 * (NG + 1)

        block = ctx.enter_context(nc.Block())

        def load_weights(eng, g, p, s, bins=2):
            for k in range(bins):
                eng.dma_start(Wt[p][s][0:HALF, k], w_v[s, 2 * g + k]).then_inc(w_in[p][s], 16)
                eng.dma_start(Wt[p][s][HALF:HALF + NH, k], b_v[s, 2 * g + k]).then_inc(w_in[p][s], 16)

        def expand(eng, s, src, bins=2):
            for n in range(NH):
                rows = slice(n * BS, (n + 1) * BS)
                dst = S[s][rows].rearrange("p (r n b) f -> p r n b f", r=2, n=NH)[:, :, n, :, 0:bins * H]
                if bins == 2:
                    eng.dma_start(dst, src[rows]).then_inc(s_in[s], 16)
                else:
                    for r in range(2):
                        eng.dma_start(dst[:, r], src[rows, r]).then_inc(s_in[s], 16)

        @block.sync
        def _(sp):
            sp.dma_start(fwd_w[:, :], t["fwd_w"]).then_inc(row_table, 16)

            def store_rows(i, s):
                b = 2 * i + s
                sp.wait_ge(d1_done, (b + 1) * 4)
                for hh in range(HH):
                    sp.dma_start(f1_w[hh, b], d1[s][hh * W:(hh + 1) * W]).then_inc(f1_out[s], 16)

            with sp.Fori(0, B // 2 - 1) as i:
                for s in range(2):
                    store_rows(i, s)
            for s in range(2):
                store_rows(B // 2 - 1, s)
            for s in range(2):
                sp.wait_ge(f1_out[s], 16 * HH * B // 2)

            def spectrum_rows(g):
                sp.dma_start(d2[:, :, :], f1_r[g]).then_inc(d2_in, 16)

            spectrum_rows(0)
            sp.wait_ge(zeroed, 3)
            for s in range(2):
                sp.dma_start(S[s][HALF:HALF + NH].rearrange("p a f -> p (a f)"), t["block_ones"]).then_inc(ones_in, 16)
            sp.wait_ge(k16_dft, 2)
            spectrum_rows(1)
            for s in range(2):
                load_weights(sp, 1, 1, s)

            def group(g, p):
                for s in range(2):
                    if s == 1 and not (isinstance(g, int) and g >= NG - 2):
                        sp.wait_ge(hdft, 2 * 2 * (g + 2))
                        spectrum_rows(g + 2)
                    sp.wait_ge(mixed, 4 * (2 * g + s + 1))
                    if isinstance(g, int) and g == NG - 2:
                        load_weights(sp, NG, p, s, 1)
                    elif not (isinstance(g, int) and g == NG - 1):
                        load_weights(sp, g + 2, p, s)

            for g in range(2):
                group(g, g)
            with sp.Fori(1, NG // 2 - 1) as gg:
                for p in range(2):
                    group(2 * gg + p, p)
            for g in range(NG - 2, NG):
                group(g, g % 2)
            expand(sp, 1, x16[1], 1)

        @block.gpsimd
        def _(pool):
            def image(i, s):
                b = 2 * i + s
                passed(pool, x_in[s], 16 * i)
                pool.dma_start(X[:, bass.ds(b * TPB, TPB), :], x_v[b]).then_inc(x_in[s], 16)

            for s in range(2):
                image(0, s)
            with pool.Fori(1, B // 2) as i:
                for s in range(2):
                    image(i, s)
            for s in range(2):
                nc.gpsimd.memset(S[s][:, :, :], 0.0).then_inc(zeroed, 1)
            nc.gpsimd.memset(Y[:, :, :], 0.0).then_inc(zeroed, 1)
            n_vectors = sh.load_vectors(pool)
            pool.wait_ge(sh.vectors_in, 16 * n_vectors)
            pool.wait_ge(normed, TPB // 2 * B)
            pool.wait_ge(normed_a, TPB // 2 * B)
            with pool.Fori(0, B) as b:
                for k in range(TPB):
                    nc.gpsimd.tensor_tensor(X[:, b * TPB + k, :], X[:, b * TPB + k, :], sh.b2["L0_conv_"][:, :],
                                            ALU.add).then_inc(x_biased, 1)

            def store_mixed(g):
                pool.wait_ge(d3_done, 4 * (g + 1))
                for q in range(4):
                    if not (isinstance(g, int) and g == 0 and q == 1):
                        pool.dma_start(f2_w[4 * g + q], d3[q * H:(q + 1) * H, :].rearrange("p (b c) -> p b c", b=B)).then_inc(f2_out, 16)

            rolled(pool, NG, store_mixed, 1, 0)
            pool.wait_ge(d3_done, 4 * (NG + 1))
            pool.dma_start(f2_w[1], d3[0:H, :].rearrange("p (b c) -> p b c", b=B)).then_inc(f2_out, 16)
            pool.wait_ge(f2_out, 16 * 4 * NG)

        @block.scalar
        def _(act):
            act.dma_start(fwd_h[:, :], t["fwd_h"]).then_inc(consts, 16)
            act.dma_start(fwd_h0[:, :], t["fwd_h0"]).then_inc(consts, 16)
            act.dma_start(inv_h[:, :], t["inv_h"]).then_inc(consts, 16)
            for s in range(2):
                act.dma_start(gamma[:, s:s + 1], t["L0_conv_norm1_w"].rearrange("(s c o) -> s c o", s=2, o=1)[s]).then_inc(consts, 16)
                act.dma_start(beta[:, s:s + 1], t["L0_conv_norm1_b"].rearrange("(s c o) -> s c o", s=2, o=1)[s]).then_inc(consts, 16)

            def root(b, s):
                act.wait_ge(eps_in, b + 1)
                nc.scalar.activation(sd[s][:, :], mvb[s][:, :, 1], ACT.Sqrt).then_inc(rooted, 1)

            def normalise(b, s):
                act.wait_ge(recip, 2 * b + 2)
                passed(act, rows_done, 4 * (b - 1))
                for k in range(TPB // 2, TPB):
                    nc.scalar.activation(xn[s][:, k, :], X[:, b * TPB + k, :], ACT.Identity, bias=shift[s][:, k:k + 1],
                                         scale=rs[s][:, k:k + 1]).then_inc(normed_a, 1)

            def rows_out(i, s):
                b = 2 * i + s
                for q in range(4):
                    act.wait_ge(rows_done, 4 * b + q + 1)
                    if q == 0:
                        passed(act, f1_out[s], 16 * HH * i)
                    nc.scalar.activation(d1[s][:, 2 * q:2 * q + 2, :],
                                         ps[:, 4 * s + q, 0:2 * C].rearrange("p (t c) -> p t c", t=2),
                                         ACT.Copy).then_inc(d1_done, 1)

            def pair(i, last=False):
                normalise(2 * i, 0)
                root(2 * i + 1, 1)
                rows_out(i, 0)
                normalise(2 * i + 1, 1)
                if not last:
                    root(2 * i + 2, 0)
                rows_out(i, 1)

            root(0, 0)
            pair(0)
            load_weights(act, 0, 0, 0)
            with act.Fori(1, B // 2 - 1) as i:
                pair(i)
            load_weights(act, 0, 0, 1)
            pair(B // 2 - 1, True)

            def unit(u, bins=2):
                for j in range(4):
                    act.wait_ge(mixed, 4 * u + j + 1)
                    passed(act, summed, 4 * u + j - 1)
                    v = ps[:, j, 0:8 * 2 * BS].rearrange("p (h o r) -> p h o r", h=8, r=2)
                    for k in range(bins):
                        re, im = 2 * k * H, (2 * k + 1) * H
                        nc.scalar.activation(cross[j % 2][re:re + H], v[im:im + H, :, :, 1], ACT.Copy,
                                             scale=-1.0).then_inc(crossed, 1)
                        nc.scalar.activation(cross[j % 2][im:im + H], v[re:re + H, :, :, 1],
                                             ACT.Copy).then_inc(crossed, 1)

            act.wait_ge(zeroed, 3)
            for s in range(2):
                act.wait_ge(xh_done, 4 * (s + 1))
                expand(act, s, xh[s])

            def group(g):
                for s in range(2):
                    unit(2 * g + s)
                    if isinstance(g, int) and g == NG - 1:
                        if s == 0:
                            expand(act, s, x16[s], 1)
                    else:
                        act.wait_ge(xh_done, 4 * (2 * (g + 1) + s + 1))
                        expand(act, s, xh[s])

            rolled(act, NG, group, 1, 1)
            for u in range(2 * NG, UNITS):
                unit(u, 1)

        @block.vector
        def _(dve):

            def measure(i, s):
                b = 2 * i + s
                dve.wait_ge(x_in[s], 16 * (i + 1))
                held(nc, dve, scratch, aggr, TPB * b)
                for k in range(TPB):
                    nc.vector.bn_stats(st[:, k, :], X[:, b * TPB + k, :]).then_inc(stats, 1)
                passed(dve, normed, TPB // 2 * (b - 1))
                held(nc, dve, scratch, normed_a, TPB // 2 * (b - 1))
                held(nc, dve, scratch, stats, TPB * (b + 1))
                for k in range(TPB):
                    nc.vector.bn_aggr(mvb[s][:, k, :], st[:, k, :]).then_inc(aggr, 1)
                dve.wait_ge(aggr, TPB * (b + 1))
                nc.vector.tensor_scalar(mvb[s][:, :, 1], mvb[s][:, :, 1], EPS0, None, ALU.add).then_inc(eps_in, 1)

            def scales(b, s):
                dve.wait_ge(rooted, b + 1)
                nc.vector.reciprocal(rs[s][:, :], sd[s][:, :]).then_inc(recip, 1)
                dve.wait_ge(recip, 2 * b + 1)
                nc.vector.scalar_tensor_tensor(shift[s][:, :], mvb[s][:, :, 0], -1.0, rs[s][:, :], ALU.mult,
                                               ALU.mult).then_inc(recip, 1)

            def normalise(b, s):
                passed(dve, rows_done, 4 * (b - 1))
                for k in range(TPB // 2):
                    nc.vector.tensor_scalar(xn[s][:, k, :], X[:, b * TPB + k, :], mvb[s][:, k, 0:1], rs[s][:, k:k + 1],
                                            ALU.subtract, ALU.mult).then_inc(normed, 1)

            def pair(i, last=False):
                scales(2 * i, 0)
                measure(i, 1)
                normalise(2 * i, 0)
                scales(2 * i + 1, 1)
                if not last:
                    measure(i + 1, 0)
                normalise(2 * i + 1, 1)

            measure(0, 0)
            pair(0)
            with dve.Fori(1, B // 2 - 1) as i:
                pair(i)
            pair(B // 2 - 1, True)
            dve.wait_ge(consts, 16 * N_CONST)
            nc.vector.tensor_scalar(dc[:, :], beta[:, :], float(np.sqrt(H * W)), None, ALU.mult).then_inc(dc_done, 1)

            def channels_out(u, s, g0=False):
                for q in range(2):
                    dve.wait_ge(hdft, 2 * u + q + 1)
                    if q == 0 and not g0:
                        dve.wait_ge(s_in[s], 16 * NH * (u // 2 if isinstance(u, int) else (u - s) // 2))
                    v = ps[0:HALF, 4 + q, :].rearrange("p (b k r h) -> p r b k h", b=4, k=2, r=2)
                    for r in range(2):
                        nc.vector.tensor_scalar(
                            xh[s][:, r, 4 * q:4 * q + 4, :].rearrange("p b (k h) -> p b k h", k=2),
                            v[:, r], gamma[:, s:s + 1], None, ALU.mult).then_inc(xh_done if not g0 else k16_done, 1)

            for s in range(2):
                channels_out(s, s, True)
                dve.wait_ge(k16_done, 7 * s + 4)
                dve.wait_ge(dc_done, 1)
                nc.vector.tensor_scalar(xh[s][:, 0, :, 0], xh[s][:, 0, :, 0], dc[:, s:s + 1], None,
                                        ALU.add).then_inc(xh_done, 4)
                dve.wait_ge(k16_dft, s + 1)
                v = ps[0:HALF, 6 + s, :].rearrange("p (b r h) -> p r b h", b=B, r=2)
                for r in range(2):
                    nc.vector.tensor_scalar(x16[s][:, r], v[:, r], gamma[:, s:s + 1], None,
                                            ALU.mult).then_inc(k16_done, 1)
                if s == 0:
                    nc.vector.tensor_scalar(dc[:, 0:1], dc[:, 0:1], 1.0, None, ALU.mult).then_inc(k16_done, 1)

            def sums(u, s, bins=2):
                for j in range(4):
                    dve.wait_ge(crossed, (16 * u + 4 * (j + 1)) if bins == 2 else
                                16 * 2 * NG + 8 * (u - 2 * NG) + 2 * (j + 1))
                    if j == 0:
                        passed(dve, turned, u)
                    v = ps[:, j, 0:8 * 2 * BS].rearrange("p (h o r) -> p h o r", h=8, r=2)
                    n = 2 * H * bins
                    nc.vector.tensor_tensor(Y[0:n, 8 * j:8 * j + 8, :], v[0:n, :, :, 0], cross[j % 2][0:n],
                                            ALU.add).then_inc(summed, 1)

            def rectify(u, s, g):
                dve.wait_ge(summed, 4 * (u + 1))
                passed(dve, relu, u)
                nc.vector.transpose(Yt[:, :, :], Y[:, :, :].rearrange("p h o -> p o h")).then_inc(turned, 1)
                dve.wait_ge(turned, u + 1)
                passed(dve, inv_done, 4 * g)
                nc.vector.tensor_scalar(
                    Z[:, :, s, :].rearrange("p b (n o) -> p b n o", n=NH),
                    Yt[:, :, :].rearrange("p o (n b) -> p b n o", n=NH), 0.0, None, ALU.max).then_inc(relu, 1)

            def inverse_out(g):
                for j in range(4):
                    dve.wait_ge(inv_done, 4 * g + j + 1)
                    if j == 0:
                        passed(dve, f2_out, 16 * (4 * g - 1))
                    nc.vector.tensor_copy(d3[:, 384 * j:384 * j + 384], ps[:, 6 + j % 2, 0:384]).then_inc(d3_done, 1)

            def group(g):
                for s in range(2):
                    sums(2 * g + s, s)
                    if not (isinstance(g, int) and g == NG - 1):
                        channels_out(2 * (g + 1) + s, s)
                    if s == 0 and not (isinstance(g, int) and g == 0):
                        inverse_out(g - 1)
                    rectify(2 * g + s, s, g)

            group(0)
            group(1)
            with dve.Fori(2, NG - 1) as g:
                group(g)
            group(NG - 1)
            inverse_out(NG - 1)
            for s in range(2):
                sums(2 * NG + s, s, 1)
                rectify(2 * NG + s, s, NG)
            for j in range(4):
                dve.wait_ge(inv_done, 4 * NG + j + 1)
                if j == 0:
                    dve.wait_ge(f2_out, 16 * (4 * NG - 1))
                nc.vector.tensor_copy(d3[0:H, 384 * j:384 * j + 384], ps[0:H, 6 + j % 2, 0:384]).then_inc(d3_done, 1)

        @block.tensor
        def _(pe):
            pe.wait_ge(row_table, 16)

            def rows(i, s):
                b = 2 * i + s
                for q in range(4):
                    pe.wait_ge(normed if q < 2 else normed_a, TPB // 2 * b + 2 * (q % 2) + 2)
                    if q == 0:
                        passed(pe, d1_done, 4 * (b - 1))
                    pe.matmul(ps[:, 4 * s + q, 0:2 * C], fwd_w[:, :],
                              xn[s][:, 2 * q:2 * q + 2, :].rearrange("p t c -> p (t c)"),
                              start=True, stop=True).then_inc(rows_done, 1)

            for s in range(2):
                rows(0, s)
            with pe.Fori(1, B // 2) as i:
                for s in range(2):
                    rows(i, s)

            def columns(u, s, g):
                if s == 0:
                    pe.wait_ge(d2_in, 16 * (g + 1))
                for q in range(2):
                    if isinstance(g, int) and g == 0:
                        table = fwd_h0[:, 0:4 * H]
                        passed(pe, k16_done, 7 * s)
                    else:
                        table = fwd_h[:, :]
                        pe.wait_ge(xh_done, 4 * (u - 1) + 2 * q + 2)
                    for b in range(4):
                        mm = pe.matmul(ps[0:HALF, 4 + q, P * b:P * b + P],
                                       d2[:, 4 * q + b, HALF * s:HALF * s + HALF], table, start=True, stop=True)
                    mm.then_inc(hdft, 1)

            pe.wait_ge(d1_done, 4 * B)
            pe.wait_ge(consts, 16 * N_CONST)
            for s in range(2):
                columns(s, s, 0)
                for b in range(B):
                    mm = pe.matmul(ps[0:HALF, 6 + s, 2 * H * b:2 * H * b + 2 * H],
                                   d2[:, b, HALF * s:HALF * s + HALF], fwd_h0[:, 4 * H:], start=True, stop=True)
                mm.then_inc(k16_dft, 1)

            def products(u, s, g, p, times, bins=2):
                pe.wait_ge(s_in[s], 16 * NH * (g + 1) if bins == 2 else 16 * NH * (NG + 2))
                pe.wait_ge(w_in[p][s], 64 * times if bins == 2 else 64 * (times - 1) + 32)
                if isinstance(g, int) and g == 0:
                    pe.wait_ge(ones_in, 32)
                for j in range(4):
                    passed(pe, summed, 4 * (u - 1) + j + 1)
                    for hl in range(8):
                        for k in range(bins):
                            h = 8 * j + hl
                            mm = pe.matmul(ps[2 * H * k:2 * H * k + 2 * H, j, 48 * hl:48 * hl + 48],
                                           S[s][:, :, k * H + h], Wt[p][s][:, k, h, :], start=True, stop=True)
                    mm.then_inc(mixed, 1)

            def inverse(g, rows=P, width=P):
                pe.wait_ge(relu, 2 * (g + 1))
                z = Z[0:rows].rearrange("p b s c -> p (b s c)")
                for j in range(4):
                    passed(pe, d3_done, 4 * g + j - 1)
                    pe.matmul(ps[0:width, 6 + j % 2, 0:384], inv_h[0:rows, 0:width], z[:, 384 * j:384 * j + 384],
                              start=True, stop=True).then_inc(inv_done, 1)

            def group(g, p, times):
                for s in range(2):
                    products(2 * g + s, s, g, p, times)
                    if not (isinstance(g, int) and g == NG - 1):
                        columns(2 * (g + 1) + s, s, g + 1)
                    if s == 0 and not (isinstance(g, int) and g == 0):
                        inverse(g - 1)

            pe.wait_ge(k16_done, 13)
            for g in range(2):
                group(g, g, 1)
            with pe.Fori(1, NG // 2 - 1) as gg:
                for p in range(2):
                    group(2 * gg + p, p, gg + 1)
            for g in range(NG - 2, NG):
                group(g, g % 2, NG // 2)
            inverse(NG - 1)
            for s in range(2):
                products(2 * NG + s, s, NG, 0, NG // 2 + 1, 1)
            inverse(NG, 2 * H, H)


def inverse_rows(nc, t, sh, XS, F2):
    mv = sh.mv
    with ExitStack() as ctx:
        def sb(name, shape, dt=F32):
            return ctx.enter_context(nc.sbuf_tensor(name, shape, dt))

        def sem(name):
            return ctx.enter_context(nc.semaphore(name))

        DEPTH = 4
        inv_w = sh.inv_w
        d4 = [sb(f"d4{s}", [P, TPB, C]) for s in range(DEPTH)]
        st = sb("st2", [P, TPB, 6])
        mvb = sb("mvb2", [P, TPB, 2])
        scratch = words(sb("scratch2", [P, 16]))
        filed = sem("i_filed")
        ps = ctx.enter_context(nc.psum_tensor("psI", [P, 8, 512], F32))
        d4_in = [sem(f"d4_in{s}") for s in range(DEPTH)]
        rows_done, xs_done, stats, aggr = (sem(n) for n in ("i_rows", "i_xs", "i_stats", "i_aggr"))
        w_loaded, w_hi, w_lo = sem("i_w_loaded"), sem("i_w_hi"), sem("i_w_lo")
        loads, splits = sh.mlp_loads("L0_conv_"), sh.mlp_splits()
        f2_v = F2.rearrange("b (t hh) k c -> b (hh k) t c", hh=HH)
        block = ctx.enter_context(nc.Block())

        @block.sync
        def _(sp):
            def image(i, s):
                passed(sp, rows_done, 4 * (DEPTH * (i - 1) + s + 1))
                sp.dma_start(d4[s][:, :, :], f2_v[DEPTH * i + s]).then_inc(d4_in[s], 16)

            for s in range(DEPTH):
                image(0, s)
            for dst, src in loads:
                sp.dma_start(dst, src).then_inc(w_loaded, 16)
            for i in range(1, B // DEPTH):
                for s in range(DEPTH):
                    image(i, s)

        @block.tensor
        def _(pe):
            def image(i, s):
                pe.wait_ge(d4_in[s], 16 * (i + 1))
                passed(pe, xs_done, 4 * (DEPTH * i + s - 1))
                for q in range(4):
                    pe.matmul(ps[:, 4 * (s % 2) + q, 0:2 * C], inv_w[:, :],
                              d4[s][:, 2 * q:2 * q + 2, :].rearrange("p t c -> p (t c)"),
                              start=True, stop=True).then_inc(rows_done, 1)

            for i in range(B // DEPTH):
                for s in range(DEPTH):
                    image(i, s)

        @block.scalar
        def _(act):
            def pair(i):
                for s in range(2):
                    b = 2 * i + s
                    for q in range(4):
                        act.wait_ge(rows_done, 4 * b + q + 1)
                        nc.scalar.activation(XS[:, bass.ds(b * TPB + 2 * q, 2), :],
                                             ps[:, 4 * s + q, 0:2 * C].rearrange("p (t c) -> p t c", t=2),
                                             ACT.Copy).then_inc(xs_done, 1)

            for i in range(2):
                pair(i)
            high_parts(nc.scalar, act, splits, w_loaded, 16 * len(loads), w_hi)
            with act.Fori(2, B // 2) as i:
                pair(i)

        @block.vector
        def _(dve):

            def image(b):
                passed(dve, aggr, TPB * b)
                for k in range(TPB):
                    if k % 2 == 0:
                        held(nc, dve, scratch, xs_done, 4 * b + k // 2 + 1)
                    nc.vector.bn_stats(st[:, k, :], XS[:, b * TPB + k, :]).then_inc(stats, 1)
                passed(dve, filed, b)
                held(nc, dve, scratch, stats, TPB * (b + 1))
                for k in range(TPB):
                    nc.vector.bn_aggr(mvb[:, k, :], st[:, k, :]).then_inc(aggr, 1)
                dve.wait_ge(aggr, TPB * (b + 1))
                nc.vector.tensor_scalar(mv[:, bass.ds(b * TPB, TPB), :], mvb[:, :, :], 1.0, None,
                                        ALU.mult).then_inc(filed, 1)

            image(0)
            with dve.Fori(1, B) as b:
                image(b)

        @block.gpsimd
        def _(pool):
            low_parts(nc, pool, splits, w_hi, w_lo)


def high_parts(scalar, act, splits, loaded, count, done):
    act.wait_ge(loaded, count)
    for raw, hi, lo in splits:
        scalar.activation(hi, raw, ACT.Copy).then_inc(done, 1)


def low_parts(nc, pool, splits, hi_done, lo_done):
    for n, (raw, hi, lo) in enumerate(splits):
        pool.wait_ge(hi_done, n + 1)
        nc.gpsimd.tensor_tensor(lo, raw, hi.bitcast(F32), ALU.subtract).then_inc(lo_done, 1)


def mlp(nc, t, sh, pre, wname, bname, gelu, eps, XS, out):
    X, mv, ident = sh.X, sh.mv, sh.ident
    SRC = X if XS is None else XS
    w1h, w1l, w2hl = sh.w1h, sh.w1l, sh.w2hl
    b1, b2 = sh.b1[pre], sh.b2[pre]
    gam, bet = sh.columns[pre + wname], sh.columns[pre + bname]
    with ExitStack() as ctx:
        def sb(name, shape, dt=F32):
            return ctx.enter_context(nc.sbuf_tensor(pre + name, shape, dt))

        def sem(name):
            return ctx.enter_context(nc.semaphore(pre + name))

        sd, rs = sb("sd", [P, NT]), sb("rs", [P, NT])
        xn = sb("xn", [P, GT, 2 * P])
        y = sb("y", [P, 2, GTOK])
        thi, tlo = sb("thi", [P, GTOK], F32R), sb("tlo", [P, GTOK], F32R)
        tst = sb("tst", [P, GTOK], F32R)
        hf = sb("hf", [P, 3, GTOK])
        hhi, hlo = sb("hhi", [P, MT, GTOK], F32R), sb("hlo", [P, MT, GTOK], F32R)
        part = sb("part", [P, 2, C])
        st = sb("st", [P, GT, 6])
        mvb = sb("mvb", [P, GT, 2])
        scratch = words(sb("scratch", [P, 16]))
        filed = sem("filed")
        ps = ctx.enter_context(nc.psum_tensor(pre + "ps", [P, 8, 512], F32))
        TB, RB, AB = 0, 2, 4

        (loaded, w_hi, w_lo, eps_in, rooted, recip, normed, tposed, y_done, t_hi, t_lo, fc1, act1, h_hi, h_lo, fc2,
         parted, x_done, stats, aggr, biased) = (sem(n) for n in (
             "loaded", "w_hi", "w_lo", "eps_in", "rooted", "recip", "normed", "tposed", "y_done", "t_hi", "t_lo",
             "fc1", "act1", "h_hi", "h_lo", "fc2", "parted", "x_done", "stats", "aggr", "biased"))
        stored = sem("stored")
        N = NGRP
        loads, splits = (sh.scan_loads(), sh.scan_splits()) if out is None else ([], [])
        zeroed = sem("zeroed")

        block = ctx.enter_context(nc.Block())

        @block.sync
        def _(sp):
            if loads:
                sp.wait_ge(zeroed, 1)
                for dst, src in loads:
                    sp.dma_start(dst, src).then_inc(loaded, 16)
            if out is not None:
                o_v = out.rearrange("b (t hh) w c -> (hh w) (b t) c", hh=HH)

                def store(i):
                    sp.wait_ge(x_done, GT * (i + 1))
                    sp.dma_start(o_v[:, bass.ds(GT * i, GT), :], X[:, bass.ds(GT * i, GT), :]).then_inc(stored, 16)

                with sp.Fori(0, N) as i:
                    store(i)
                sp.wait_ge(stored, 16 * N)

        @block.gpsimd
        def _(pool):
            if loads:
                nc.gpsimd.memset(sh.raw[:, 0:3 * SCAN_W], 0.0).then_inc(zeroed, 1)

            def group(i):
                if XS is None:
                    pool.wait_ge(normed, GT * (i + 1))
                if XS is None:
                    for k in range(GT):
                        nc.gpsimd.tensor_tensor(X[:, GT * i + k, :], X[:, GT * i + k, :], b2[:, :],
                                                ALU.add).then_inc(biased, 1)
                else:
                    tiles = bass.ds(GT * i, GT)
                    nc.gpsimd.tensor_tensor(X[:, tiles, :], X[:, tiles, :], XS[:, tiles, :], ALU.add).then_inc(biased, GT)

            with pool.Fori(0, N) as i:
                group(i)
            if loads:
                low_parts(nc, pool, splits, w_hi, w_lo)

        @block.scalar
        def _(act):
            act.wait_ge(eps_in, 1)
            nc.scalar.activation(sd[:, :], sd[:, :], ACT.Sqrt).then_inc(rooted, 1)

            def channels(i):
                for k in range(2):
                    act.wait_ge(tposed, 2 * i + k + 1)
                    passed(act, t_lo, 2 * (i - 1) + k + 1)
                    nc.scalar.activation(y[:, k, :], ps[:, TB + k, :], ACT.Identity, bias=bet[:, k:k + 1],
                                         scale=gam[:, k:k + 1]).then_inc(y_done, 1)
                for k, dst in enumerate((thi, tst)):
                    act.wait_ge(y_done, 2 * i + k + 1)
                    passed(act, fc1, MT * i)
                    nc.scalar.activation(dst[:, :], y[:, k, :], ACT.Copy).then_inc(t_hi, 1)

            def hidden(i, m):
                n = MT * i + m
                act.wait_ge(fc1, n + 1)
                passed(act, h_lo, n - 2)
                nc.scalar.activation(hf[:, m % 3, :], ps[:, RB + m % 2, :], gelu,
                                     bias=b1[:, m:m + 1]).then_inc(act1, 1)

            def high(i, m):
                n = MT * i + m
                act.wait_ge(act1, n + 1)
                if m == 0:
                    passed(act, fc2, GT * i)
                nc.scalar.activation(hhi[:, m, :], hf[:, m % 3, :], ACT.Copy).then_inc(h_hi, 1)

            def group(i):
                channels(i)
                for m in range(MT):
                    hidden(i, m)
                    if m:
                        high(i, m - 1)
                high(i, MT - 1)

            rolled(act, N, group, 1, 0)
            if loads:
                high_parts(nc.scalar, act, splits, loaded, 16 * len(loads), w_hi)

        @block.vector
        def _(dve):
            nc.vector.tensor_scalar(sd[:, :], mv[:, :, 1], eps, None, ALU.add).then_inc(eps_in, 1)
            dve.wait_ge(rooted, 1)
            nc.vector.reciprocal(rs[:, :], sd[:, :]).then_inc(recip, 1)
            dve.wait_ge(recip, 1)

            def normalise(i):
                passed(dve, tposed, 2 * i)
                for k in range(GT):
                    n = GT * i + k
                    for to, fr in ((slice(0, C), slice(0, C)), (slice(C, 2 * P), slice(P, C))):
                        ins = nc.vector.tensor_scalar(xn[:, k, to], SRC[:, n, fr], mv[:, n, 0:1],
                                                      rs[:, bass.ds(n, 1)], ALU.subtract, ALU.mult)
                    ins.then_inc(normed, 1)

            normalise(0)

            def low_channels(i):
                dve.wait_ge(t_hi, 2 * i + 1)
                nc.vector.tensor_tensor(tlo[:, :], y[:, 0, :], thi[:, :].bitcast(F32), ALU.subtract).then_inc(t_lo, 1)
                dve.wait_ge(t_hi, 2 * i + 2)
                nc.vector.tensor_tensor(tst[C1:P, :], y[C1:P, 1, :], tst[C1:P, :].bitcast(F32),
                                        ALU.subtract).then_inc(t_lo, 1)

            def low_hidden(i, m):
                dve.wait_ge(h_hi, MT * i + m + 1)
                nc.vector.tensor_tensor(hlo[:, m, :], hf[:, m % 3, :], hhi[:, m, :].bitcast(F32),
                                        ALU.subtract).then_inc(h_lo, 1)

            def output(i, k):
                n = GT * i + k
                dve.wait_ge(fc2, n + 1)
                dve.wait_ge(biased, n + 1)
                passed(dve, x_done, n - 1)
                nc.vector.tensor_tensor(part[:, k % 2, :], ps[:, AB + k, 0:C], X[:, n, :], ALU.add).then_inc(parted, 1)
                dve.wait_ge(parted, n + 1)
                nc.vector.tensor_tensor(X[:, n, :], ps[:, AB + k, C:2 * C], part[:, k % 2, :],
                                        ALU.add).then_inc(x_done, 1)

            def measure(i, k):
                if out is None:
                    n = GT * i + k
                    if k == 0:
                        passed(dve, aggr, GT * i)
                    held(nc, dve, scratch, x_done, n + 1)
                    nc.vector.bn_stats(st[:, k, :], X[:, n, :]).then_inc(stats, 1)

            def collect(i):
                if out is None:
                    passed(dve, filed, i)
                    held(nc, dve, scratch, stats, GT * (i + 1))
                    for k in range(GT):
                        nc.vector.bn_aggr(mvb[:, k, :], st[:, k, :]).then_inc(aggr, 1)
                    dve.wait_ge(aggr, GT * (i + 1))
                    nc.vector.tensor_scalar(mv[:, bass.ds(GT * i, GT), :], mvb[:, :, :], 1.0, None,
                                            ALU.mult).then_inc(filed, 1)

            def group(i):
                head = isinstance(i, int) and i == 0
                low_channels(i)
                if not (isinstance(i, int) and i == N - 1):
                    normalise(i + 1)
                for m in range(MT):
                    if not head and m < GT:
                        output(i - 1, m)
                    low_hidden(i, m)
                if not head:
                    for k in range(GT):
                        measure(i - 1, k)
                    collect(i - 1)

            rolled(dve, N, group, 2, 1)
            for k in range(GT):
                output(N - 1, k)
            for k in range(GT):
                measure(N - 1, k)
            collect(N - 1)

        @block.tensor
        def _(pe):
            def turn(i):
                for k in range(2):
                    passed(pe, y_done, 2 * (i - 1) + k + 1)
                    for j in range(GT):
                        if k == 0:
                            pe.wait_ge(normed, GT * i + j + 1)
                            src = xn[:, j, 0:P]
                        else:
                            src = xn[:, j, P:2 * P]
                        mm = pe.transpose(ps[:, TB + k, P * j:P * j + P], src, ident[:, :])
                    mm.then_inc(tposed, 1)

            def first(i):
                for m in range(MT):
                    n = MT * i + m
                    cut = slice(P * m, P * m + P)
                    passed(pe, act1, n - 1)
                    terms = [(w1h[:, 0, cut], thi), (w1l[:, 0, cut], thi), (w1h[:, 1, cut], tst),
                             (w1l[:, 1, cut], tst), (w1h[:, 0, cut], tlo)]
                    if m == 0:
                        pe.wait_ge(t_hi, 2 * i + 1)
                    for q, (w, x) in enumerate(terms):
                        if m == 0 and q == 2:
                            pe.wait_ge(t_lo, 2 * i + 2)
                        mm = pe.matmul(ps[:, RB + m % 2, :], w, x[:, :], start=(q == 0), stop=(q == 4))
                    mm.then_inc(fc1, 1)

            def second(i):
                passed(pe, x_done, GT * i)
                for m in range(MT):
                    pe.wait_ge(h_lo, MT * i + m + 1)
                    for k in range(GT):
                        cut = slice(P * k, P * k + P)
                        full = (hhi[:, m, cut], w2hl[:, m].rearrange("p a c -> p (a c)"), ps[:, AB + k, 0:2 * C])
                        low = (hlo[:, m, cut], w2hl[:, m, 0, :], ps[:, AB + k, C:2 * C])
                        for n, (x, w, o) in enumerate((full, low) if m == 0 else (low, full)):
                            mm = pe.matmul(o, x, w, start=(m == 0 and n == 0), stop=(m == MT - 1 and n == 1),
                                           skip_group_check=True)
                        if m == MT - 1:
                            mm.then_inc(fc2, 1)

            turn(0)
            first(0)

            def group(i):
                turn(i + 1)
                second(i)
                first(i + 1)

            rolled(pe, N - 1, group, 1, 0)
            second(N - 1)


def gated_scan(nc, t, sh):
    X, mv, ident, wh, wl = sh.X, sh.mv, sh.ident, sh.wh, sh.wl
    pre = "L1_conv_"
    gam, bet, bu, bg = (sh.columns[pre + n] for n in ("norm1_scale", "norm1_bias", "bu", "bg"))
    with ExitStack() as ctx:
        def sb(name, shape, dt=F32):
            return ctx.enter_context(nc.sbuf_tensor("sc_" + name, shape, dt))

        def sem(name):
            return ctx.enter_context(nc.semaphore("sc_" + name))

        NP = NT // (4 * GT)
        ST = 2 * GT
        U, G, A = 0, 1, 2
        sd, rs, shift = sb("sd", [P, NT]), sb("rs", [P, NT]), sb("shift", [P, NT])
        xn = sb("xn", [P, GT, 3 * P])
        y = sb("y", [P, 2, GTOK])
        yh, yl = sb("yh", [P, 3, GTOK], F32R), sb("yl", [P, 3, GTOK], F32R)
        gate, nfix, prod, hid = ([sb(f"{n}{c}", [P, 3, GTOK]) for c in range(2)] for n in ("gate", "nfix", "prod", "hid"))
        hi, lo = ([sb(f"{n}{c}", [P, 3, GTOK], F32R) for c in range(2)] for n in ("hi", "lo"))
        ych, ycl = [yh, hi[1]], [yl, lo[1]]
        st = sb("st", [P, 2 * ST, 6])
        mvb = sb("mvb", [P, 2 * ST, 2])
        scratch = words(sb("scratch", [P, 16]))
        ps = ctx.enter_context(nc.psum_tensor("sc_ps", [P, 8, 512], F32))
        loaded, w_hi, w_lo = sem("loaded"), sem("w_hi"), sem("w_lo")
        eps_in, rooted, recip, stats, aggr, filed = (sem(n) for n in ("eps_in", "rooted", "recip", "stats", "aggr", "filed"))
        normed, tposed, y_done, y_hi, y_lo = (sem(n) for n in ("normed", "tposed", "y_done", "y_hi", "y_lo"))
        turned_back, x_done = sem("turned_back"), sem("x_done")
        names = ("mm", "u_out", "g_out", "fixed", "mult", "h_done", "h_hi", "h_lo")
        Q = [{n: sem(f"{n}{c}") for n in names} for c in range(2)]
        loads, splits = sh.mlp_loads("L1_conv_"), sh.mlp_splits()
        MM = 3 * (2 + STEPS - 1)
        HL = 3 * (STEPS - 1)
        ROUNDS = [("back", 0, 0), ("back", 0, 1), ("back", 0, 2), ("back", 0, 3), ("turn", 1, 0), ("turn", 1, 1),
                  ("turn", 1, 2), ("back", 1, 0), ("back", 1, 1), ("back", 1, 2), ("back", 1, 3),
                  ("turn", 0, 0), ("turn", 0, 1), ("turn", 0, 2)]
        BRING = {(3, 0): 0, (3, 1): 1, (4, 0): 2}
        NORM0 = {(1, 0): 0, (1, 1): 1, (2, 0): 2, (2, 1): 3}
        NORM1 = {(4, 1): 0, (5, 0): 1, (5, 1): 2, (6, 0): 3}
        LAST_BANKS = [6, 7, 0, 1, 2, 3, 4, 5]
        bank_of = {r: 6 + n % 2 for n, r in enumerate(ROUNDS)}

        block = ctx.enter_context(nc.Block())

        @block.sync
        def _(sp):
            for dst, src in loads:
                sp.dma_start(dst, src).then_inc(loaded, 16)

        def column(j):
            return slice(0, 1) if j < 2 else slice(1, 2)

        @block.gpsimd
        def _(pool):
            def low_channels(m, c, tiles=range(3)):
                for j in tiles:
                    pool.wait_ge(y_hi, 3 * m + j + 1)
                    nc.gpsimd.tensor_tensor(ycl[c][:, j, :], y[:, (3 * c + j) % 2, :], ych[c][:, j, :].bitcast(F32),
                                            ALU.subtract).then_inc(y_lo, 1)

            def low(i, c, s):
                q = Q[c]
                for j in range(3):
                    pool.wait_ge(q["h_hi"], HL * i + 3 * s + j + 1)
                    pool.wait_ge(q["mm"], MM * i + 3 * (s + 2))
                    nc.gpsimd.tensor_tensor(lo[c][:, j, :], hid[c][:, j, :], hi[c][:, j, :].bitcast(F32),
                                            ALU.subtract).then_inc(q["h_lo"], 1)

            def pair(i):
                low_channels(2 * i + 1, 1)
                for s in range(1, STEPS - 1):
                    for c in range(2):
                        low(i, c, s)
                        if (s, c) in BRING and not (isinstance(i, int) and i == NP - 1):
                            low_channels(2 * i + 2, 0, [BRING[s, c]])

            low_channels(0, 0)
            rolled(pool, NP, pair, 0, 1)
            low_parts(nc, pool, splits, w_hi, w_lo)

        @block.scalar
        def _(act):
            act.wait_ge(eps_in, 1)
            nc.scalar.activation(sd[:, :], sd[:, :], ACT.Sqrt).then_inc(rooted, 1)
            act.wait_ge(recip, 2)

            def normalise(m, quarters=range(GT)):
                for j in quarters:
                    for k in range(2):
                        n = m * ST + GT * k + j
                        for to, fr in ((slice(P * k, P * k + P), slice(0, P)),
                                       (slice(2 * P + C1 * k, 2 * P + C1 * k + C1), slice(P, C))):
                            ins = nc.scalar.activation(xn[:, j, to], X[:, n, fr], ACT.Identity,
                                                       bias=shift[:, bass.ds(n, 1)], scale=rs[:, bass.ds(n, 1)])
                    ins.then_inc(normed, 1)

            def channels(m, c, tiles=range(3)):
                for j in tiles:
                    act.wait_ge(tposed, 3 * m + j + 1)
                    passed(act, y_lo, 3 * m + j - 1)
                    nc.scalar.activation(y[:, (3 * c + j) % 2, :], ps[:, bank_of["turn", c, j], :], ACT.Identity,
                                         bias=bet[:, column(j)], scale=gam[:, column(j)]).then_inc(y_done, 1)
                    act.wait_ge(y_done, 3 * m + j + 1)
                    nc.scalar.activation(ych[c][:, j, :], y[:, (3 * c + j) % 2, :], ACT.Copy).then_inc(y_hi, 1)

            def branch(i, c, dst, bias, func, base, done):
                q = Q[c]
                for j in range(3):
                    act.wait_ge(q["mm"], MM * i + base + j + 1)
                    nc.scalar.activation(dst[c][:, j, :], ps[:, 3 * c + j, :], func,
                                         bias=bias[:, column(j)]).then_inc(q[done], 1)

            def high(i, c, s):
                q = Q[c]
                for j in range(3):
                    if s == 0:
                        act.wait_ge(q["fixed"], 3 * i + j + 1)
                        nc.scalar.activation(hi[c][:, j, :], nfix[c][:, j, :], ACT.Copy,
                                             scale=-1.0).then_inc(q["h_hi"], 1)
                    else:
                        act.wait_ge(q["h_done"], HL * i + 3 * (s - 1) + j + 1)
                        nc.scalar.activation(hi[c][:, j, :], hid[c][:, j, :], ACT.Copy).then_inc(q["h_hi"], 1)

            def pair(i):
                branch(i, 0, prod, bu, ACT.Identity, 0, "u_out")
                channels(2 * i + 1, 1)
                branch(i, 0, gate, bg, ACT.Sigmoid, 3, "g_out")
                high(i, 0, 0)
                branch(i, 1, prod, bu, ACT.Identity, 0, "u_out")
                branch(i, 1, gate, bg, ACT.Sigmoid, 3, "g_out")
                high(i, 1, 0)
                for s in range(1, STEPS - 1):
                    for c in range(2):
                        high(i, c, s)
                        if isinstance(i, int) and i == NP - 1:
                            continue
                        if (s, c) in NORM0:
                            normalise(2 * i + 2, [NORM0[s, c]])
                        if (s, c) in BRING:
                            channels(2 * i + 2, 0, [BRING[s, c]])
                        if (s, c) in NORM1:
                            normalise(2 * i + 3, [NORM1[s, c]])

            normalise(0)
            channels(0, 0)
            normalise(1)
            rolled(act, NP, pair, 0, 1)
            high_parts(nc.scalar, act, splits, loaded, 16 * len(loads), w_hi)

        @block.vector
        def _(dve):
            nc.vector.tensor_scalar(sd[:, :], mv[:, :, 1], EPS1, None, ALU.add).then_inc(eps_in, 1)
            dve.wait_ge(rooted, 1)
            nc.vector.reciprocal(rs[:, :], sd[:, :]).then_inc(recip, 1)
            dve.wait_ge(recip, 1)
            nc.vector.scalar_tensor_tensor(shift[:, :], mv[:, :, 0], -1.0, rs[:, :], ALU.mult,
                                           ALU.mult).then_inc(recip, 1)

            def fix(i, c):
                q = Q[c]
                for j in range(3):
                    dve.wait_ge(q["u_out"], 3 * i + j + 1)
                    dve.wait_ge(q["g_out"], 3 * i + j + 1)
                    nc.vector.scalar_tensor_tensor(nfix[c][:, j, :], gate[c][:, j, :], 1.0, prod[c][:, j, :],
                                                   ALU.subtract, ALU.mult).then_inc(q["fixed"], 1)
                for j in range(3):
                    dve.wait_ge(q["h_hi"], HL * i + j + 1)
                    nc.vector.scalar_tensor_tensor(lo[c][:, j, :], nfix[c][:, j, :], -1.0, hi[c][:, j, :].bitcast(F32),
                                                   ALU.mult, ALU.subtract).then_inc(q["h_lo"], 1)

            def step(i, c, s):
                q = Q[c]
                for j in range(3):
                    dve.wait_ge(q["mm"], MM * i + 3 * (s + 1) + j + 1)
                    nc.vector.tensor_tensor(prod[c][:, j, :], ps[:, 3 * c + j, :], gate[c][:, j, :],
                                            ALU.mult).then_inc(q["mult"], 1)
                    dve.wait_ge(q["mult"], HL * i + 3 * (s - 1) + j + 1)
                    if j == 0 and s > 1:
                        dve.wait_ge(q["h_lo"], HL * i + 3 * s)
                    nc.vector.tensor_tensor(hid[c][:, j, :], prod[c][:, j, :], nfix[c][:, j, :],
                                            ALU.subtract).then_inc(q["h_done"], 1)

            def add_back(i, c, k, bank):
                m = 2 * i + c
                dve.wait_ge(turned_back, GT * m + k + 1)
                v = ps[:, bank, 0:3 * P]
                for a, b, part in ((0, P, v[:, 0:2 * P]), (P, C, v[:, 2 * P:])):
                    dst = X[:, bass.ds(m * ST, ST), a:b].rearrange("p (h j) c -> p h j c", h=2)[:, :, k]
                    nc.vector.tensor_tensor(dst, dst, part.rearrange("p (h c) -> p h c", h=2), ALU.add).then_inc(x_done, 1)

            def measure(i, n):
                if n == 0:
                    passed(dve, aggr, 2 * ST * i)
                    held(nc, dve, scratch, x_done, 2 * 2 * GT * (i + 1))
                nc.vector.bn_stats(st[:, n, :], X[:, i * 2 * ST + n, :]).then_inc(stats, 1)

            def collect(i):
                passed(dve, filed, i)
                held(nc, dve, scratch, stats, 2 * ST * (i + 1))
                for k in range(2 * ST):
                    nc.vector.bn_aggr(mvb[:, k, :], st[:, k, :]).then_inc(aggr, 1)
                dve.wait_ge(aggr, 2 * ST * (i + 1))
                nc.vector.tensor_scalar(mv[:, bass.ds(i * 2 * ST, 2 * ST), :], mvb[:, :, :], 1.0, None,
                                        ALU.mult).then_inc(filed, 1)

            def pair(i):
                back = not (isinstance(i, int) and i == 0)
                for c in range(2):
                    for k in range(GT):
                        if back:
                            add_back(i - 1, c, k, bank_of["back", c, k])
                        if (c, k) == (0, GT - 1):
                            fix(i, 0)
                        if (c, k) == (1, GT - 2):
                            fix(i, 1)
                for s in range(1, STEPS):
                    for c in range(2):
                        step(i, c, s)
                        n = 2 * (s - 1) + c
                        if back and 2 <= n:
                            measure(i - 1, n - 2)
                if back:
                    for n in range(2 * STEPS - 4, 2 * ST):
                        measure(i - 1, n)
                    collect(i - 1)

            rolled(dve, NP, pair, 2, 1)
            for c in range(2):
                for k in range(GT):
                    add_back(NP - 1, c, k, LAST_BANKS[GT * c + k])
            for n in range(2 * ST):
                measure(NP - 1, n)
            collect(NP - 1)

        @block.tensor
        def _(pe):
            def turn(m, c, j):
                for k in range(GT):
                    if j == 0:
                        pe.wait_ge(normed, GT * m + k + 1)
                    mm = pe.transpose(ps[:, bank_of["turn", c, j], P * k:P * k + P], xn[:, k, P * j:P * j + P], ident[:, :])
                mm.then_inc(tposed, 1)

            def turn_back(i, c, k, bank):
                q = Q[c]
                for j in range(3):
                    if k == 0:
                        pe.wait_ge(q["h_done"], HL * i + 3 * (STEPS - 2) + j + 1)
                    mm = pe.transpose(ps[:, bank, P * j:P * j + P], hid[c][:, j, P * k:P * k + P], ident[:, :])
                mm.then_inc(turned_back, 1)

            def bank_free(i, kind, c, j):
                n = ROUNDS.index((kind, c, j)) - 2
                at = i
                if n < 0:
                    n, at = n + len(ROUNDS), i - 1
                k2, c2, j2 = ROUNDS[n]
                if k2 == "back":
                    passed(pe, x_done, 4 * GT * (at - 1) + 2 * (GT * c2 + j2) + 2)
                else:
                    passed(pe, y_done, 3 * (2 * (at + 1 - c2) + c2) + j2 + 1)

            def back_round(i, c, k):
                if not (isinstance(i, int) and i == 0):
                    bank_free(i, "back", c, k)
                    turn_back(i - 1, c, k, bank_of["back", c, k])

            def turn_round(i, c, j):
                bank_free(i, "turn", c, j)
                turn(2 * i + 1 if c else 2 * i + 2, c, j)

            def product(c, w, h, l, high_in, low_in):
                def bank(b):
                    return ps[:, 3 * c + b, :]

                def term(out, ww, rows, cols, x, j, first=False, last=False):
                    return pe.matmul(out, ww[rows, w, cols], x[rows, j, :], start=first, stop=last, skip_group_check=True)

                every, lower, upper = slice(0, P), slice(0, C1), slice(C1, P)
                for j in range(2):
                    high_in(j)
                    term(bank(j), wh, every, W00, h, j, first=True)
                    term(bank(j), wl, every, W00, h, j)
                high_in(2)
                for ww in (wh, wl):
                    for j, rows in enumerate((lower, upper)):
                        term(bank(j), ww, rows, W10, h, 2)
                for n, ww in enumerate((wh, wl)):
                    term(bank(2), ww, every, W11, h, 2, first=(n == 0))
                for ww in (wh, wl):
                    for j, cols in enumerate((W01_LOWER, W01_UPPER)):
                        term(bank(2), ww, every, cols, h, j)
                for j in range(2):
                    low_in(j)
                    term(bank(j), wh, every, W00, l, j)
                low_in(2)
                for j, rows in enumerate((lower, upper)):
                    term(bank(j), wh, rows, W10, l, 2, last=True).then_inc(Q[c]["mm"], 1)
                for j, cols in enumerate((W01_LOWER, W01_UPPER)):
                    term(bank(2), wh, every, cols, l, j)
                term(bank(2), wh, every, W11, l, 2, last=True).then_inc(Q[c]["mm"], 1)

            def project(i, c, w):
                q = Q[c]
                m = 2 * i + c

                def high_in(j):
                    pe.wait_ge(y_hi, 3 * m + j + 1)
                    if w == U:
                        passed(pe, q["h_done"], HL * (i - 1) + 3 * (STEPS - 2) + j + 1)
                    else:
                        pe.wait_ge(q["u_out"], 3 * i + j + 1)

                def low_in(j):
                    pe.wait_ge(y_lo, 3 * m + j + 1)

                product(c, w, ych[c], ycl[c], high_in, low_in)

            def advance(i, c, s):
                q = Q[c]
                product(c, A, hi[c], lo[c], lambda j: pe.wait_ge(q["h_hi"], HL * i + 3 * (s - 1) + j + 1),
                        lambda j: pe.wait_ge(q["h_lo"], HL * i + 3 * (s - 1) + j + 1))

            def pair(i):
                back_round(i, 0, 0)
                back_round(i, 0, 1)
                project(i, 0, U)
                back_round(i, 0, 2)
                back_round(i, 0, 3)
                turn_round(i, 1, 0)
                turn_round(i, 1, 1)
                project(i, 0, G)
                turn_round(i, 1, 2)
                back_round(i, 1, 0)
                project(i, 1, U)
                back_round(i, 1, 1)
                back_round(i, 1, 2)
                project(i, 1, G)
                back_round(i, 1, 3)
                for s in range(1, STEPS):
                    for c in range(2):
                        advance(i, c, s)
                        if (s, c) in BRING and not (isinstance(i, int) and i == NP - 1):
                            turn_round(i, 0, BRING[s, c])

            for j in range(3):
                if j == 2:
                    pe.wait_ge(y_done, 1)
                turn(0, 0, j)
            rolled(pe, NP, pair, 2, 1)
            for c in range(2):
                for k in range(GT):
                    turn_back(NP - 1, c, k, LAST_BANKS[GT * c + k])


_OUT = (B, H, W, C)


def kernel(**inputs):
    import concourse.bacc as _bacc
    from concourse.bass_utils import run_bass_kernel_spmd as _run

    nc = _bacc.Bacc("TRN2", target_bir_lowering=False, num_devices=1)
    arrays = {k: np.ascontiguousarray(v) for k, v in inputs.items()}
    arrays |= dict(zip(("fwd_w", "inv_w", "fwd_h", "fwd_h0", "inv_h"), dft_tables()))
    arrays |= {"block_ones": block_ones(), "ident": np.eye(P, dtype=np.float32)}
    t = {k: nc.dram_tensor(f"in_{k}", a.shape, mybir.dt.from_np(a.dtype), kind="ExternalInput").ap()
         for k, a in arrays.items()}
    out = nc.dram_tensor("out_0", _OUT, F32, kind="ExternalOutput").ap()
    build(nc, t, out)
    r = _run(nc, [{f"in_{k}": a for k, a in arrays.items()}], core_ids=[0])
    return r.results[0]["out_0"]
```

```python
import itertools
from contextlib import ExitStack

import numpy as np

import concourse.bass as bass
from concourse import mybir

F32 = mybir.dt.float32
F32R = mybir.dt.float32r
ALU = mybir.AluOpType
ACT = mybir.ActivationFunctionType

P = 128
B, H, W, C = 8, 32, 32, 192
WF = W // 2 + 1
NB, BS = 8, 24
HID = 4 * C
TOK = B * H * W
NT = TOK // P
TPB = NT // B
HH = P // W
HALF = C // 2
NH = NB // 2
NG = WF // 2
GT = 4
NGRP = NT // GT
LATE = 5 * TPB
GTOK = GT * P
MT = HID // P
C1 = C - P
STEPS = 8
EPS0, EPS1 = 1e-5, 1e-6


def dft_tables():
    h = np.arange(H)
    th = 2 * np.pi * np.outer(h, h) / H
    co, si = np.cos(th) / np.sqrt(H), np.sin(th) / np.sqrt(H)
    fw, iw = np.zeros((W, W)), np.zeros((W, W))
    for k in range(W // 2):
        fw[:, 2 * k] = co[:, k]
        iw[2 * k, :] = co[k] * (1 if k == 0 else 2)
        if k:
            fw[:, 2 * k + 1] = -si[:, k]
            iw[2 * k + 1, :] = -2 * si[k]
    fw[:, 1], iw[1, :] = co[:, W // 2], co[W // 2]
    eye = np.eye(HH)
    fwd_w, inv_w = np.kron(eye, fw), np.kron(eye, iw)
    fc = np.block([[co, -si], [si, co]])
    ic = np.block([[co, si], [-si, co]])
    z = np.zeros((2 * H, 2 * H))
    fwd_h = np.block([[fc, z], [z, fc]])
    inv_h = np.block([[ic, z], [z, ic]])
    fwd_h0 = np.zeros((P, 3 * 2 * H))
    fwd_h0[0:H, 0:2 * H] = fc[0:H]
    fwd_h0[2 * H:, 2 * H:4 * H] = fc
    fwd_h0[H:2 * H, 4 * H:] = fc[0:H]
    return [a.astype(np.float32) for a in (fwd_w, inv_w, fwd_h, fwd_h0, inv_h)]


def block_ones():
    s = np.zeros((NH, 2, NH, B, 2 * H))
    for n in range(NH):
        s[n, 0, n] = 1
    return s.reshape(NH, -1).astype(np.float32)


def passed(eng, sem, value):
    if not isinstance(value, int) or value > 0:
        eng.wait_ge(sem, value)


def words(tile_):
    return itertools.cycle([tile_[:, k:k + 1] for k in range(tile_.shape[1])])


def held(nc, dve, scratch, sem, value):
    passed(dve, sem, value)
    nc.vector.memset(next(scratch), 0.0)


def rolled(eng, count, body, head=1, tail=2):
    for i in range(head):
        body(i)
    with eng.Fori(head, count - tail) as i:
        body(i)
    for i in range(count - tail, count):
        body(i)


class Shared:

    def __init__(self, nc, ctx, t):
        sb = lambda name, shape, dt=F32: ctx.enter_context(nc.sbuf_tensor(name, shape, dt))
        self.nc, self.t = nc, t
        self.X = sb("X", [P, NT, C])
        self.mv = sb("mv", [P, NT, 2])
        self.ident = sb("ident", [P, P])
        self.inv_w = sb("inv_w", [P, P])
        self.tables = sb("tables", [P, 3])
        self.sem = lambda name: ctx.enter_context(nc.semaphore(name))
        self.columns = {}
        for pre, names in (("L0_conv_", ("norm2_w", "norm2_b")),
                           ("L1_conv_", ("norm1_scale", "norm1_bias", "bu", "bg", "norm2_scale", "norm2_bias"))):
            for name in names:
                self.columns[pre + name] = sb("v_" + pre + name, [P, 2])
        self.b1 = {pre: sb(pre + "b1", [P, MT]) for pre in ("L0_conv_", "L1_conv_")}
        self.b2 = {pre: sb(pre + "b2", [P, C]) for pre in ("L0_conv_", "L1_conv_")}
        self.vectors_in = self.sem("vectors_in")

    def load_table(self, n, func):
        self.nc.scalar.activation(self.tables[:, n:n + 1], self.ident[:, 0:1], func)

    def load_vectors(self, eng):
        t, n = self.t, 0
        loads = [(self.ident[:, :], t["ident"]), (self.inv_w[:, :], t["inv_w"])]
        for name, tile_ in self.columns.items():
            col = lambda a, b: t[name][a:b].rearrange("(c o) -> c o", o=1)
            loads += [(tile_[:, 0:1], col(0, P)), (tile_[0:C1, 1:2], col(P, C)), (tile_[C1:P, 1:2], col(P, C))]
        for pre in self.b1:
            loads += [(self.b1[pre][:, :], t[pre + "mlp_b1"].rearrange("(m p) -> p m", p=P)),
                      (self.b2[pre][:, :], t[pre + "mlp_b2"].rearrange("(o c) -> o c", o=1).to_broadcast([P, C]))]
        with self.nc.allow_non_contiguous_dma(reason="vectors as columns"):
            for dst, src in loads:
                eng.dma_start(dst, src).then_inc(self.vectors_in, 16)
        return len(loads)

    def weights(self, ctx):
        sb = lambda name, shape, dt=F32: ctx.enter_context(self.nc.sbuf_tensor(name, shape, dt))
        self.raw = sb("raw", [P, 2 * HID + MT * C])
        self.w1h, self.w1l = sb("w1h", [P, 2, HID], F32R), sb("w1l", [P, 2, HID], F32R)
        self.w2hl = sb("w2hl", [P, MT, 2, C], F32R)
        self.wh, self.wl = (sb(n, [P, SCAN_W], F32R) for n in ("wh", "wl"))

    def mlp_loads(self, pre):
        t = self.t
        raw1 = self.raw[:, 0:2 * HID].rearrange("p (k f) -> p k f", k=2)
        raw2 = self.raw[:, 2 * HID:].rearrange("p (m c) -> p m c", m=MT)
        return [(raw1[:, 0, :], t[pre + "mlp_w1"][0:P]),
                (raw1[0:C1, 1, :], t[pre + "mlp_w1"][P:C]),
                (raw1[C1:P, 1, :], t[pre + "mlp_w1"][P:C]),
                (raw2, t[pre + "mlp_w2"].rearrange("(m p) c -> p m c", p=P))]

    def mlp_splits(self):
        raw1 = self.raw[:, 0:2 * HID].rearrange("p (k f) -> p k f", k=2)
        raw2 = self.raw[:, 2 * HID:].rearrange("p (m c) -> p m c", m=MT)
        return [(raw1[:, 0, :], self.w1h[:, 0, :], self.w1l[:, 0, :]),
                (raw1[:, 1, :], self.w1h[:, 1, :], self.w1l[:, 1, :]),
                (raw2, self.w2hl[:, :, 0, :], self.w2hl[:, :, 1, :])]

    def scan_loads(self):
        raw, loads = self.raw, []
        ws = {k: self.t["L1_conv_" + name] for k, name in (("U", "Wu"), ("G", "Wg"), ("A", "A"))}
        for k, w in ws.items():
            loads += [(raw[:, W00[k]], w[0:P, 0:P]), (raw[0:C1, W10[k]], w[P:C, 0:P]), (raw[C1:P, W10[k]], w[P:C, 0:P])]
        loads += [(raw[:, A01_LOWER.start:A01_UPPER.stop], ws["A"][0:P, P:C])]
        for rows, order, diagonal in ((slice(0, C1), "UG", 0), (slice(C1, P), "GU", 1)):
            at = A11.start + C1 * diagonal
            loads += [(raw[rows, at:at + C1], ws["A"][P:C, P:C])]
            loads += [(raw[rows, UG11.start + C1 * n:UG11.start + C1 * (n + 1)], ws[k][P:C, P:C])
                      for n, k in enumerate(order)]
        loads += [(raw[:, UG01[0].start + C1 * n:UG01[0].start + C1 * (n + 1)], ws[k][0:P, P:C])
                  for n, k in enumerate("UGU")]
        return loads

    def scan_splits(self):
        cuts = [slice(0, SCAN_W // 2), slice(SCAN_W // 2, SCAN_W)]
        return [(self.raw[:, cut], self.wh[:, cut], self.wl[:, cut]) for cut in cuts]


W00, W10 = ({w: slice(2 * P * n + P * k, 2 * P * n + P * (k + 1)) for n, w in enumerate("UGA")} for k in range(2))
A01_UPPER, A01_LOWER = slice(6 * P, 7 * P), slice(6 * P + C1, 7 * P + C1)
A11 = slice(7 * P + C1, 8 * P + C1)
UG01 = [slice(8 * P + C1 * (k + 1), 9 * P + C1 * (k + 1)) for k in range(2)]
UG11 = slice(9 * P + 2 * C1, 10 * P + 2 * C1)
SCAN_W = UG11.stop


def build(nc, t, out):
    with ExitStack() as ctx:
        sh = Shared(nc, ctx, t)
        F1 = nc.dram_tensor("rows_spectrum", [W, H, B, C], F32, kind="Internal").ap()
        F2 = nc.dram_tensor("rows_mixed", [B, H, W, C], F32, kind="Internal").ap()
        fourier(nc, t, sh, F1, F2)
        sh.weights(ctx)
        with nc.sbuf_tensor("XS", [P, NT, C], F32) as XS:
            inverse_rows(nc, t, sh, XS, F2)
            mlp(nc, t, sh, "L0_conv_", "norm2_w", "norm2_b", ACT.Gelu, EPS0, XS, None)
        gated_scan(nc, t, sh)
        mlp(nc, t, sh, "L1_conv_", "norm2_scale", "norm2_bias", ACT.Gelu_apprx_tanh, EPS1, None, out)


def fourier(nc, t, sh, F1, F2):
    X = sh.X
    with ExitStack() as ctx:
        def sb(name, shape, dt=F32):
            return ctx.enter_context(nc.sbuf_tensor(name, shape, dt))

        def sem(name):
            return ctx.enter_context(nc.semaphore(name))

        fwd_w = sb("fwd_w", [P, P])
        fwd_h = sb("fwd_h", [P, P])
        fwd_h0 = sb("fwd_h0", [P, 6 * H])
        inv_h = sb("inv_h", [P, P])
        gamma = sb("gamma", [HALF, 2])
        beta = sb("beta", [HALF, 2])
        dc = sb("dc", [HALF, 2])
        st = sb("st", [P, TPB, 6])
        mvb = [sb(f"mvb{s}", [P, TPB, 2]) for s in range(2)]
        scratch = words(sb("scratch", [P, 16]))
        sd, rs, shift = ([sb(f"{n}{s}", [P, TPB]) for s in range(2)] for n in ("sd", "rs", "shift"))
        row_bufs = [sb(f"row_bufs{s}", [P, 2, TPB, C]) for s in range(2)]
        xn = [row_bufs[0][:, s] for s in range(2)]
        d1 = [row_bufs[1][:, s] for s in range(2)]
        d2 = sb("d2", [P, B, C])
        xh = [sb(f"xh{s}", [HALF, 2, B, 2 * H]) for s in range(2)]
        x16 = [sb(f"x16{s}", [HALF, 2, B, H]) for s in range(2)]
        S = [sb(f"S{s}", [HALF + NH, 2 * NH * B, 2 * H]) for s in range(2)]
        Wt = [[sb(f"Wt{s}", [HALF + NH, 2, H, 2 * BS]) for s in range(2)],
              [row_bufs[s][0:HALF + NH].rearrange("p a t c -> p (a t c)").rearrange("p (k h c) -> p k h c", k=2, h=H)
               for s in range(2)]]
        cross = [sb(f"cross{s}", [P, 8, BS]) for s in range(2)]
        Y = sb("Y", [P, H, BS])
        Yt = sb("Yt", [P, BS, H])
        Z = sb("Z", [P, B, 2, HALF])
        d3 = sb("d3", [P, B * C])
        ps = ctx.enter_context(nc.psum_tensor("psF", [P, 8, 512], F32))

        consts, zeroed, ones_in, row_table = sem("consts"), sem("zeroed"), sem("ones_in"), sem("row_table")
        x_in = [sem(f"x_in{s}") for s in range(2)]
        stats, aggr, eps_in, rooted, recip, normed = (sem(n) for n in ("stats", "aggr", "eps_in", "rooted", "recip", "normed"))
        rows_done, d1_done, dc_done = sem("rows_done"), sem("d1_done"), sem("dc_done")
        f1_out = [sem(f"f1_out{s}") for s in range(2)]
        d2_in, hdft, xh_done, k16_dft, k16_done = sem("d2_in"), sem("hdft"), sem("xh_done"), sem("k16_dft"), sem("k16_done")
        s_in = [sem(f"s_in{s}") for s in range(2)]
        w_in = [[sem(f"w_in{p}{s}") for s in range(2)] for p in range(2)]
        normed_a, x_biased = sem("normed_a"), sem("x_biased")
        mixed, crossed, summed, turned, relu = sem("mixed"), sem("crossed"), sem("summed"), sem("turned"), sem("relu")
        inv_done, d3_done, f2_out = sem("inv_done"), sem("d3_done"), sem("f2_out")

        x_v = t["x"].rearrange("b (t hh) w c -> b (hh w) t c", hh=HH)
        f1_w = F1.rearrange("k (t hh) b c -> hh b k t c", hh=HH)
        f1_r = F1.rearrange("(g q) h b c -> g (q h) (b c)", q=4)
        f2_w = F2.rearrange("b h k c -> k h b c")
        w_v = t["L0_conv_w1"].rearrange("h k (s n) i o r -> s k (n i) h (o r)", s=2)
        b_v = t["L0_conv_b1"].rearrange("h k (s n) o r -> s k n h (o r)", s=2)
        N_CONST = 3 + 4
        UNITS = 2 * (NG + 1)

        block = ctx.enter_context(nc.Block())

        def load_weights(eng, g, p, s, bins=2):
            for k in range(bins):
                eng.dma_start(Wt[p][s][0:HALF, k], w_v[s, 2 * g + k]).then_inc(w_in[p][s], 16)
                eng.dma_start(Wt[p][s][HALF:HALF + NH, k], b_v[s, 2 * g + k]).then_inc(w_in[p][s], 16)

        def expand(eng, s, src, bins=2):
            for n in range(NH):
                rows = slice(n * BS, (n + 1) * BS)
                dst = S[s][rows].rearrange("p (r n b) f -> p r n b f", r=2, n=NH)[:, :, n, :, 0:bins * H]
                if bins == 2:
                    eng.dma_start(dst, src[rows]).then_inc(s_in[s], 16)
                else:
                    for r in range(2):
                        eng.dma_start(dst[:, r], src[rows, r]).then_inc(s_in[s], 16)

        @block.sync
        def _(sp):
            sp.dma_start(fwd_w[:, :], t["fwd_w"]).then_inc(row_table, 16)

            def store_rows(i, s):
                b = 2 * i + s
                sp.wait_ge(d1_done, (b + 1) * 4)
                for hh in range(HH):
                    sp.dma_start(f1_w[hh, b], d1[s][hh * W:(hh + 1) * W]).then_inc(f1_out[s], 16)

            with sp.Fori(0, B // 2 - 1) as i:
                for s in range(2):
                    store_rows(i, s)
            for s in range(2):
                store_rows(B // 2 - 1, s)
            for s in range(2):
                sp.wait_ge(f1_out[s], 16 * HH * B // 2)

            def spectrum_rows(g):
                sp.dma_start(d2[:, :, :], f1_r[g]).then_inc(d2_in, 16)

            spectrum_rows(0)
            sp.wait_ge(zeroed, 3)
            for s in range(2):
                sp.dma_start(S[s][HALF:HALF + NH].rearrange("p a f -> p (a f)"), t["block_ones"]).then_inc(ones_in, 16)
            sp.wait_ge(k16_dft, 2)
            spectrum_rows(1)
            for s in range(2):
                load_weights(sp, 1, 1, s)

            def group(g, p):
                for s in range(2):
                    if s == 1 and not (isinstance(g, int) and g >= NG - 2):
                        sp.wait_ge(hdft, 2 * 2 * (g + 2))
                        spectrum_rows(g + 2)
                    sp.wait_ge(mixed, 4 * (2 * g + s + 1))
                    if isinstance(g, int) and g == NG - 2:
                        load_weights(sp, NG, p, s, 1)
                    elif not (isinstance(g, int) and g == NG - 1):
                        load_weights(sp, g + 2, p, s)

            for g in range(2):
                group(g, g)
            with sp.Fori(1, NG // 2 - 1) as gg:
                for p in range(2):
                    group(2 * gg + p, p)
            for g in range(NG - 2, NG):
                group(g, g % 2)
            expand(sp, 1, x16[1], 1)

        @block.gpsimd
        def _(pool):
            def image(i, s):
                b = 2 * i + s
                passed(pool, x_in[s], 16 * i)
                pool.dma_start(X[:, bass.ds(b * TPB, TPB), :], x_v[b]).then_inc(x_in[s], 16)

            for s in range(2):
                image(0, s)
            with pool.Fori(1, B // 2) as i:
                for s in range(2):
                    image(i, s)
            for s in range(2):
                nc.gpsimd.memset(S[s][:, :, :], 0.0).then_inc(zeroed, 1)
            nc.gpsimd.memset(Y[:, :, :], 0.0).then_inc(zeroed, 1)
            n_vectors = sh.load_vectors(pool)
            pool.wait_ge(sh.vectors_in, 16 * n_vectors)
            pool.wait_ge(normed, TPB // 2 * B)
            pool.wait_ge(normed_a, TPB // 2 * B)
            with pool.Fori(0, B) as b:
                for k in range(TPB):
                    nc.gpsimd.tensor_tensor(X[:, b * TPB + k, :], X[:, b * TPB + k, :], sh.b2["L0_conv_"][:, :],
                                            ALU.add).then_inc(x_biased, 1)

            def store_mixed(g):
                pool.wait_ge(d3_done, 4 * (g + 1))
                for q in range(4):
                    if not (isinstance(g, int) and g == 0 and q == 1):
                        pool.dma_start(f2_w[4 * g + q], d3[q * H:(q + 1) * H, :].rearrange("p (b c) -> p b c", b=B)).then_inc(f2_out, 16)

            rolled(pool, NG, store_mixed, 1, 0)
            pool.wait_ge(d3_done, 4 * (NG + 1))
            pool.dma_start(f2_w[1], d3[0:H, :].rearrange("p (b c) -> p b c", b=B)).then_inc(f2_out, 16)
            pool.wait_ge(f2_out, 16 * 4 * NG)

        @block.scalar
        def _(act):
            act.dma_start(fwd_h[:, :], t["fwd_h"]).then_inc(consts, 16)
            act.dma_start(fwd_h0[:, :], t["fwd_h0"]).then_inc(consts, 16)
            act.dma_start(inv_h[:, :], t["inv_h"]).then_inc(consts, 16)
            for s in range(2):
                act.dma_start(gamma[:, s:s + 1], t["L0_conv_norm1_w"].rearrange("(s c o) -> s c o", s=2, o=1)[s]).then_inc(consts, 16)
                act.dma_start(beta[:, s:s + 1], t["L0_conv_norm1_b"].rearrange("(s c o) -> s c o", s=2, o=1)[s]).then_inc(consts, 16)

            def root(b, s):
                act.wait_ge(eps_in, b + 1)
                nc.scalar.activation(sd[s][:, :], mvb[s][:, :, 1], ACT.Sqrt).then_inc(rooted, 1)

            def normalise(b, s):
                act.wait_ge(recip, 2 * b + 2)
                passed(act, rows_done, 4 * (b - 1))
                for k in range(TPB // 2, TPB):
                    nc.scalar.activation(xn[s][:, k, :], X[:, b * TPB + k, :], ACT.Identity, bias=shift[s][:, k:k + 1],
                                         scale=rs[s][:, k:k + 1]).then_inc(normed_a, 1)

            def rows_out(i, s):
                b = 2 * i + s
                for q in range(4):
                    act.wait_ge(rows_done, 4 * b + q + 1)
                    if q == 0:
                        passed(act, f1_out[s], 16 * HH * i)
                    nc.scalar.activation(d1[s][:, 2 * q:2 * q + 2, :],
                                         ps[:, 4 * s + q, 0:2 * C].rearrange("p (t c) -> p t c", t=2),
                                         ACT.Copy).then_inc(d1_done, 1)

            def pair(i, last=False):
                normalise(2 * i, 0)
                root(2 * i + 1, 1)
                rows_out(i, 0)
                normalise(2 * i + 1, 1)
                if not last:
                    root(2 * i + 2, 0)
                rows_out(i, 1)

            root(0, 0)
            pair(0)
            load_weights(act, 0, 0, 0)
            with act.Fori(1, B // 2 - 1) as i:
                pair(i)
            load_weights(act, 0, 0, 1)
            pair(B // 2 - 1, True)

            def unit(u, bins=2):
                for j in range(4):
                    act.wait_ge(mixed, 4 * u + j + 1)
                    passed(act, summed, 4 * u + j - 1)
                    v = ps[:, j, 0:8 * 2 * BS].rearrange("p (h o r) -> p h o r", h=8, r=2)
                    for k in range(bins):
                        re, im = 2 * k * H, (2 * k + 1) * H
                        nc.scalar.activation(cross[j % 2][re:re + H], v[im:im + H, :, :, 1], ACT.Copy,
                                             scale=-1.0).then_inc(crossed, 1)
                        nc.scalar.activation(cross[j % 2][im:im + H], v[re:re + H, :, :, 1],
                                             ACT.Copy).then_inc(crossed, 1)

            act.wait_ge(zeroed, 3)
            for s in range(2):
                act.wait_ge(xh_done, 4 * (s + 1))
                expand(act, s, xh[s])

            def group(g):
                for s in range(2):
                    unit(2 * g + s)
                    if isinstance(g, int) and g == NG - 1:
                        if s == 0:
                            expand(act, s, x16[s], 1)
                    else:
                        act.wait_ge(xh_done, 4 * (2 * (g + 1) + s + 1))
                        expand(act, s, xh[s])

            rolled(act, NG, group, 1, 1)
            for u in range(2 * NG, UNITS):
                unit(u, 1)

        @block.vector
        def _(dve):

            def measure(i, s):
                b = 2 * i + s
                dve.wait_ge(x_in[s], 16 * (i + 1))
                held(nc, dve, scratch, aggr, TPB * b)
                for k in range(TPB):
                    nc.vector.bn_stats(st[:, k, :], X[:, b * TPB + k, :]).then_inc(stats, 1)
                passed(dve, normed, TPB // 2 * (b - 1))
                held(nc, dve, scratch, normed_a, TPB // 2 * (b - 1))
                held(nc, dve, scratch, stats, TPB * (b + 1))
                for k in range(TPB):
                    nc.vector.bn_aggr(mvb[s][:, k, :], st[:, k, :]).then_inc(aggr, 1)
                dve.wait_ge(aggr, TPB * (b + 1))
                nc.vector.tensor_scalar(mvb[s][:, :, 1], mvb[s][:, :, 1], EPS0, None, ALU.add).then_inc(eps_in, 1)

            def scales(b, s):
                dve.wait_ge(rooted, b + 1)
                nc.vector.reciprocal(rs[s][:, :], sd[s][:, :]).then_inc(recip, 1)
                dve.wait_ge(recip, 2 * b + 1)
                nc.vector.scalar_tensor_tensor(shift[s][:, :], mvb[s][:, :, 0], -1.0, rs[s][:, :], ALU.mult,
                                               ALU.mult).then_inc(recip, 1)

            def normalise(b, s):
                passed(dve, rows_done, 4 * (b - 1))
                for k in range(TPB // 2):
                    nc.vector.tensor_scalar(xn[s][:, k, :], X[:, b * TPB + k, :], mvb[s][:, k, 0:1], rs[s][:, k:k + 1],
                                            ALU.subtract, ALU.mult).then_inc(normed, 1)

            def pair(i, last=False):
                scales(2 * i, 0)
                measure(i, 1)
                normalise(2 * i, 0)
                scales(2 * i + 1, 1)
                if not last:
                    measure(i + 1, 0)
                normalise(2 * i + 1, 1)

            measure(0, 0)
            pair(0)
            with dve.Fori(1, B // 2 - 1) as i:
                pair(i)
            pair(B // 2 - 1, True)
            dve.wait_ge(consts, 16 * N_CONST)
            nc.vector.tensor_scalar(dc[:, :], beta[:, :], float(np.sqrt(H * W)), None, ALU.mult).then_inc(dc_done, 1)

            def channels_out(u, s, g0=False):
                for q in range(2):
                    dve.wait_ge(hdft, 2 * u + q + 1)
                    if q == 0 and not g0:
                        dve.wait_ge(s_in[s], 16 * NH * (u // 2 if isinstance(u, int) else (u - s) // 2))
                    v = ps[0:HALF, 4 + q, :].rearrange("p (b k r h) -> p r b k h", b=4, k=2, r=2)
                    for r in range(2):
                        nc.vector.tensor_scalar(
                            xh[s][:, r, 4 * q:4 * q + 4, :].rearrange("p b (k h) -> p b k h", k=2),
                            v[:, r], gamma[:, s:s + 1], None, ALU.mult).then_inc(xh_done if not g0 else k16_done, 1)

            for s in range(2):
                channels_out(s, s, True)
                dve.wait_ge(k16_done, 7 * s + 4)
                dve.wait_ge(dc_done, 1)
                nc.vector.tensor_scalar(xh[s][:, 0, :, 0], xh[s][:, 0, :, 0], dc[:, s:s + 1], None,
                                        ALU.add).then_inc(xh_done, 4)
                dve.wait_ge(k16_dft, s + 1)
                v = ps[0:HALF, 6 + s, :].rearrange("p (b r h) -> p r b h", b=B, r=2)
                for r in range(2):
                    nc.vector.tensor_scalar(x16[s][:, r], v[:, r], gamma[:, s:s + 1], None,
                                            ALU.mult).then_inc(k16_done, 1)
                if s == 0:
                    nc.vector.tensor_scalar(dc[:, 0:1], dc[:, 0:1], 1.0, None, ALU.mult).then_inc(k16_done, 1)

            def sums(u, s, bins=2):
                for j in range(4):
                    dve.wait_ge(crossed, (16 * u + 4 * (j + 1)) if bins == 2 else
                                16 * 2 * NG + 8 * (u - 2 * NG) + 2 * (j + 1))
                    if j == 0:
                        passed(dve, turned, u)
                    v = ps[:, j, 0:8 * 2 * BS].rearrange("p (h o r) -> p h o r", h=8, r=2)
                    n = 2 * H * bins
                    nc.vector.tensor_tensor(Y[0:n, 8 * j:8 * j + 8, :], v[0:n, :, :, 0], cross[j % 2][0:n],
                                            ALU.add).then_inc(summed, 1)

            def rectify(u, s, g):
                dve.wait_ge(summed, 4 * (u + 1))
                passed(dve, relu, u)
                nc.vector.transpose(Yt[:, :, :], Y[:, :, :].rearrange("p h o -> p o h")).then_inc(turned, 1)
                dve.wait_ge(turned, u + 1)
                passed(dve, inv_done, 4 * g)
                nc.vector.tensor_scalar(
                    Z[:, :, s, :].rearrange("p b (n o) -> p b n o", n=NH),
                    Yt[:, :, :].rearrange("p o (n b) -> p b n o", n=NH), 0.0, None, ALU.max).then_inc(relu, 1)

            def inverse_out(g):
                for j in range(4):
                    dve.wait_ge(inv_done, 4 * g + j + 1)
                    if j == 0:
                        passed(dve, f2_out, 16 * (4 * g - 1))
                    nc.vector.tensor_copy(d3[:, 384 * j:384 * j + 384], ps[:, 6 + j % 2, 0:384]).then_inc(d3_done, 1)

            def group(g):
                for s in range(2):
                    sums(2 * g + s, s)
                    if not (isinstance(g, int) and g == NG - 1):
                        channels_out(2 * (g + 1) + s, s)
                    if s == 0 and not (isinstance(g, int) and g == 0):
                        inverse_out(g - 1)
                    rectify(2 * g + s, s, g)

            group(0)
            group(1)
            with dve.Fori(2, NG - 1) as g:
                group(g)
            group(NG - 1)
            inverse_out(NG - 1)
            for s in range(2):
                sums(2 * NG + s, s, 1)
                rectify(2 * NG + s, s, NG)
            for j in range(4):
                dve.wait_ge(inv_done, 4 * NG + j + 1)
                if j == 0:
                    dve.wait_ge(f2_out, 16 * (4 * NG - 1))
                nc.vector.tensor_copy(d3[0:H, 384 * j:384 * j + 384], ps[0:H, 6 + j % 2, 0:384]).then_inc(d3_done, 1)

        @block.tensor
        def _(pe):
            pe.wait_ge(row_table, 16)

            def rows(i, s):
                b = 2 * i + s
                for q in range(4):
                    pe.wait_ge(normed if q < 2 else normed_a, TPB // 2 * b + 2 * (q % 2) + 2)
                    if q == 0:
                        passed(pe, d1_done, 4 * (b - 1))
                    pe.matmul(ps[:, 4 * s + q, 0:2 * C], fwd_w[:, :],
                              xn[s][:, 2 * q:2 * q + 2, :].rearrange("p t c -> p (t c)"),
                              start=True, stop=True).then_inc(rows_done, 1)

            for s in range(2):
                rows(0, s)
            with pe.Fori(1, B // 2) as i:
                for s in range(2):
                    rows(i, s)

            def columns(u, s, g):
                if s == 0:
                    pe.wait_ge(d2_in, 16 * (g + 1))
                for q in range(2):
                    if isinstance(g, int) and g == 0:
                        table = fwd_h0[:, 0:4 * H]
                        passed(pe, k16_done, 7 * s)
                    else:
                        table = fwd_h[:, :]
                        pe.wait_ge(xh_done, 4 * (u - 1) + 2 * q + 2)
                    for b in range(4):
                        mm = pe.matmul(ps[0:HALF, 4 + q, P * b:P * b + P],
                                       d2[:, 4 * q + b, HALF * s:HALF * s + HALF], table, start=True, stop=True)
                    mm.then_inc(hdft, 1)

            pe.wait_ge(d1_done, 4 * B)
            pe.wait_ge(consts, 16 * N_CONST)
            for s in range(2):
                columns(s, s, 0)
                for b in range(B):
                    mm = pe.matmul(ps[0:HALF, 6 + s, 2 * H * b:2 * H * b + 2 * H],
                                   d2[:, b, HALF * s:HALF * s + HALF], fwd_h0[:, 4 * H:], start=True, stop=True)
                mm.then_inc(k16_dft, 1)

            def products(u, s, g, p, times, bins=2):
                pe.wait_ge(s_in[s], 16 * NH * (g + 1) if bins == 2 else 16 * NH * (NG + 2))
                pe.wait_ge(w_in[p][s], 64 * times if bins == 2 else 64 * (times - 1) + 32)
                if isinstance(g, int) and g == 0:
                    pe.wait_ge(ones_in, 32)
                for j in range(4):
                    passed(pe, summed, 4 * (u - 1) + j + 1)
                    for hl in range(8):
                        for k in range(bins):
                            h = 8 * j + hl
                            mm = pe.matmul(ps[2 * H * k:2 * H * k + 2 * H, j, 48 * hl:48 * hl + 48],
                                           S[s][:, :, k * H + h], Wt[p][s][:, k, h, :], start=True, stop=True)
                    mm.then_inc(mixed, 1)

            def inverse(g, rows=P, width=P):
                pe.wait_ge(relu, 2 * (g + 1))
                z = Z[0:rows].rearrange("p b s c -> p (b s c)")
                for j in range(4):
                    passed(pe, d3_done, 4 * g + j - 1)
                    pe.matmul(ps[0:width, 6 + j % 2, 0:384], inv_h[0:rows, 0:width], z[:, 384 * j:384 * j + 384],
                              start=True, stop=True).then_inc(inv_done, 1)

            def group(g, p, times):
                for s in range(2):
                    products(2 * g + s, s, g, p, times)
                    if not (isinstance(g, int) and g == NG - 1):
                        columns(2 * (g + 1) + s, s, g + 1)
                    if s == 0 and not (isinstance(g, int) and g == 0):
                        inverse(g - 1)

            pe.wait_ge(k16_done, 13)
            for g in range(2):
                group(g, g, 1)
            with pe.Fori(1, NG // 2 - 1) as gg:
                for p in range(2):
                    group(2 * gg + p, p, gg + 1)
            for g in range(NG - 2, NG):
                group(g, g % 2, NG // 2)
            inverse(NG - 1)
            for s in range(2):
                products(2 * NG + s, s, NG, 0, NG // 2 + 1, 1)
            inverse(NG, 2 * H, H)


def inverse_rows(nc, t, sh, XS, F2):
    mv = sh.mv
    with ExitStack() as ctx:
        def sb(name, shape, dt=F32):
            return ctx.enter_context(nc.sbuf_tensor(name, shape, dt))

        def sem(name):
            return ctx.enter_context(nc.semaphore(name))

        DEPTH = 4
        inv_w = sh.inv_w
        d4 = [sb(f"d4{s}", [P, TPB, C]) for s in range(DEPTH)]
        st = sb("st2", [P, TPB, 6])
        mvb = sb("mvb2", [P, TPB, 2])
        scratch = words(sb("scratch2", [P, 16]))
        filed = sem("i_filed")
        ps = ctx.enter_context(nc.psum_tensor("psI", [P, 8, 512], F32))
        d4_in = [sem(f"d4_in{s}") for s in range(DEPTH)]
        rows_done, xs_done, stats, aggr = (sem(n) for n in ("i_rows", "i_xs", "i_stats", "i_aggr"))
        w_loaded, w_hi, w_lo = sem("i_w_loaded"), sem("i_w_hi"), sem("i_w_lo")
        loads, splits = sh.mlp_loads("L0_conv_"), sh.mlp_splits()
        f2_v = F2.rearrange("b (t hh) k c -> b (hh k) t c", hh=HH)
        block = ctx.enter_context(nc.Block())

        @block.sync
        def _(sp):
            def image(i, s):
                passed(sp, rows_done, 4 * (DEPTH * (i - 1) + s + 1))
                sp.dma_start(d4[s][:, :, :], f2_v[DEPTH * i + s]).then_inc(d4_in[s], 16)

            for s in range(DEPTH):
                image(0, s)
            for dst, src in loads:
                sp.dma_start(dst, src).then_inc(w_loaded, 16)
            for i in range(1, B // DEPTH):
                for s in range(DEPTH):
                    image(i, s)

        @block.tensor
        def _(pe):
            def image(i, s):
                pe.wait_ge(d4_in[s], 16 * (i + 1))
                passed(pe, xs_done, 4 * (DEPTH * i + s - 1))
                for q in range(4):
                    pe.matmul(ps[:, 4 * (s % 2) + q, 0:2 * C], inv_w[:, :],
                              d4[s][:, 2 * q:2 * q + 2, :].rearrange("p t c -> p (t c)"),
                              start=True, stop=True).then_inc(rows_done, 1)

            for i in range(B // DEPTH):
                for s in range(DEPTH):
                    image(i, s)

        @block.scalar
        def _(act):
            def pair(i):
                for s in range(2):
                    b = 2 * i + s
                    for q in range(4):
                        act.wait_ge(rows_done, 4 * b + q + 1)
                        nc.scalar.activation(XS[:, bass.ds(b * TPB + 2 * q, 2), :],
                                             ps[:, 4 * s + q, 0:2 * C].rearrange("p (t c) -> p t c", t=2),
                                             ACT.Copy).then_inc(xs_done, 1)

            for i in range(2):
                pair(i)
            high_parts(nc.scalar, act, splits, w_loaded, 16 * len(loads), w_hi)
            with act.Fori(2, B // 2) as i:
                pair(i)
            sh.load_table(0, ACT.Sqrt)

        @block.vector
        def _(dve):

            def image(b):
                passed(dve, aggr, TPB * b)
                for k in range(TPB):
                    if k % 2 == 0:
                        held(nc, dve, scratch, xs_done, 4 * b + k // 2 + 1)
                    nc.vector.bn_stats(st[:, k, :], XS[:, b * TPB + k, :]).then_inc(stats, 1)
                passed(dve, filed, b)
                held(nc, dve, scratch, stats, TPB * (b + 1))
                for k in range(TPB):
                    nc.vector.bn_aggr(mvb[:, k, :], st[:, k, :]).then_inc(aggr, 1)
                dve.wait_ge(aggr, TPB * (b + 1))
                nc.vector.tensor_scalar(mv[:, bass.ds(b * TPB, TPB), :], mvb[:, :, :], 1.0, None,
                                        ALU.mult).then_inc(filed, 1)

            image(0)
            with dve.Fori(1, LATE // TPB) as b:
                image(b)

        @block.gpsimd
        def _(pool):
            low_parts(nc, pool, splits, w_hi, w_lo)


def high_parts(scalar, act, splits, loaded, count, done):
    act.wait_ge(loaded, count)
    for raw, hi, lo in splits:
        scalar.activation(hi, raw, ACT.Copy).then_inc(done, 1)


def low_parts(nc, pool, splits, hi_done, lo_done):
    for n, (raw, hi, lo) in enumerate(splits):
        pool.wait_ge(hi_done, n + 1)
        nc.gpsimd.tensor_tensor(lo, raw, hi.bitcast(F32), ALU.subtract).then_inc(lo_done, 1)


def mlp(nc, t, sh, pre, wname, bname, gelu, eps, XS, out):
    X, mv, ident = sh.X, sh.mv, sh.ident
    SRC = X if XS is None else XS
    w1h, w1l, w2hl = sh.w1h, sh.w1l, sh.w2hl
    b1, b2 = sh.b1[pre], sh.b2[pre]
    gam, bet = sh.columns[pre + wname], sh.columns[pre + bname]
    with ExitStack() as ctx:
        def sb(name, shape, dt=F32):
            return ctx.enter_context(nc.sbuf_tensor(pre + name, shape, dt))

        def sem(name):
            return ctx.enter_context(nc.semaphore(pre + name))

        sd, rs = sb("sd", [P, NT]), sb("rs", [P, NT])
        xn = sb("xn", [P, GT, 2 * P])
        y = sb("y", [P, 2, GTOK])
        thi, tlo = sb("thi", [P, GTOK], F32R), sb("tlo", [P, GTOK], F32R)
        tst = sb("tst", [P, GTOK], F32R)
        hf = sb("hf", [P, 3, GTOK])
        hhi, hlo = sb("hhi", [P, MT, GTOK], F32R), sb("hlo", [P, MT, GTOK], F32R)
        part = sb("part", [P, 2, C])
        st = sb("st", [P, GT, 6])
        mvb = sb("mvb", [P, GT, 2])
        late = NT - 4 * GT if XS is None else LATE
        LT = GT
        LG = (NT - late) // LT
        st_x, mv_x = sb("st_x", [P, LT, 6]), sb("mv_x", [P, LT, 2])
        stats_x, aggr_x, filed_x = sem("stats_x"), sem("aggr_x"), sem("filed_x")
        first_tiles, late_tiles = slice(0, late), slice(late, NT)
        scratch = words(sb("scratch", [P, 16]))
        filed = sem("filed")
        ps = ctx.enter_context(nc.psum_tensor(pre + "ps", [P, 8, 512], F32))
        TB, RB, AB = 0, 2, 4

        (loaded, w_hi, w_lo, eps_in, rooted, recip, normed, tposed, y_done, t_hi, t_lo, fc1, act1, h_hi, h_lo, fc2,
         parted, x_done, stats, aggr, biased) = (sem(n) for n in (
             "loaded", "w_hi", "w_lo", "eps_in", "rooted", "recip", "normed", "tposed", "y_done", "t_hi", "t_lo",
             "fc1", "act1", "h_hi", "h_lo", "fc2", "parted", "x_done", "stats", "aggr", "biased"))
        stored = sem("stored")
        N = NGRP
        loads, splits = (sh.scan_loads(), sh.scan_splits()) if out is None else ([], [])
        zeroed = sem("zeroed")

        block = ctx.enter_context(nc.Block())

        @block.sync
        def _(sp):
            if loads:
                sp.wait_ge(zeroed, 1)
                for dst, src in loads:
                    sp.dma_start(dst, src).then_inc(loaded, 16)
            if out is not None:
                o_v = out.rearrange("b (t hh) w c -> (hh w) (b t) c", hh=HH)

                def store(i):
                    sp.wait_ge(x_done, GT * (i + 1))
                    sp.dma_start(o_v[:, bass.ds(GT * i, GT), :], X[:, bass.ds(GT * i, GT), :]).then_inc(stored, 16)

                with sp.Fori(0, N - 1) as i:
                    store(i)
                for n in range(GT * (N - 1), NT):
                    sp.wait_ge(x_done, n + 1)
                    sp.dma_start(o_v[:, n:n + 1, :], X[:, n:n + 1, :]).then_inc(stored, 16)
                sp.wait_ge(stored, 16 * (N - 1 + GT))

        @block.gpsimd
        def _(pool):
            if loads:
                nc.gpsimd.memset(sh.raw[:, A01_UPPER.start:A11.stop], 0.0).then_inc(zeroed, 1)

            def group(i):
                if XS is None:
                    pool.wait_ge(normed, GT * (i + 1))
                if XS is None:
                    for k in range(GT):
                        nc.gpsimd.tensor_tensor(X[:, GT * i + k, :], X[:, GT * i + k, :], b2[:, :],
                                                ALU.add).then_inc(biased, 1)
                else:
                    tiles = bass.ds(GT * i, GT)
                    nc.gpsimd.tensor_tensor(X[:, tiles, :], X[:, tiles, :], XS[:, tiles, :], ALU.add).then_inc(biased, GT)

            with pool.Fori(0, N) as i:
                group(i)
            if loads:
                low_parts(nc, pool, splits, w_hi, w_lo)

        @block.scalar
        def _(act):
            def root(n, tiles):
                act.wait_ge(eps_in, n)
                nc.scalar.activation(sd[:, tiles], sd[:, tiles], ACT.Sqrt).then_inc(rooted, 1)
                sh.load_table(n, gelu)

            root(1, first_tiles)

            def channels(i):
                for k in range(2):
                    act.wait_ge(tposed, 2 * i + k + 1)
                    passed(act, t_lo, 2 * (i - 1) + k + 1)
                    nc.scalar.activation(y[:, k, :], ps[:, TB + k, :], ACT.Identity, bias=bet[:, k:k + 1],
                                         scale=gam[:, k:k + 1]).then_inc(y_done, 1)
                for k, dst in enumerate((thi, tst)):
                    act.wait_ge(y_done, 2 * i + k + 1)
                    passed(act, fc1, MT * i)
                    nc.scalar.activation(dst[:, :], y[:, k, :], ACT.Copy).then_inc(t_hi, 1)

            def hidden(i, m):
                n = MT * i + m
                act.wait_ge(fc1, n + 1)
                passed(act, h_lo, n - 2)
                nc.scalar.activation(hf[:, m % 3, :], ps[:, RB + m % 2, :], gelu,
                                     bias=b1[:, m:m + 1]).then_inc(act1, 1)

            def high(i, m):
                n = MT * i + m
                act.wait_ge(act1, n + 1)
                if m == 0:
                    passed(act, fc2, GT * i)
                nc.scalar.activation(hhi[:, m, :], hf[:, m % 3, :], ACT.Copy).then_inc(h_hi, 1)

            def group(i):
                channels(i)
                for m in range(MT):
                    hidden(i, m)
                    if m:
                        high(i, m - 1)
                high(i, MT - 1)

            rolled(act, LG + 2, group, 1, 0)
            root(2, late_tiles)
            with act.Fori(LG + 2, N) as i:
                group(i)
            if loads:
                high_parts(nc.scalar, act, splits, loaded, 16 * len(loads), w_hi)
                sh.load_table(0, ACT.Sqrt)

        @block.vector
        def _(dve):
            def add_eps(tiles):
                nc.vector.tensor_scalar(sd[:, tiles], mv[:, tiles, 1], eps, None, ALU.add).then_inc(eps_in, 1)

            def invert(n, tiles):
                dve.wait_ge(rooted, n)
                nc.vector.reciprocal(rs[:, tiles], sd[:, tiles]).then_inc(recip, 1)
                dve.wait_ge(recip, n)

            add_eps(first_tiles)
            invert(1, first_tiles)

            def measure_source(n):
                at = late + LT * n
                for k in range(LT):
                    if k == 0:
                        held(nc, dve, scratch, aggr_x, LT * n)
                    nc.vector.bn_stats(st_x[:, k, :], SRC[:, at + k, :]).then_inc(stats_x, 1)
                passed(dve, filed_x, n)
                held(nc, dve, scratch, stats_x, LT * (n + 1))
                for k in range(LT):
                    nc.vector.bn_aggr(mv_x[:, k, :], st_x[:, k, :]).then_inc(aggr_x, 1)
                dve.wait_ge(aggr_x, LT * (n + 1))
                nc.vector.tensor_scalar(mv[:, bass.ds(at, LT), :], mv_x[:, :, :], 1.0, None, ALU.mult).then_inc(filed_x, 1)

            def normalise(i):
                passed(dve, tposed, 2 * i)
                for k in range(GT):
                    n = GT * i + k
                    for to, fr in ((slice(0, C), slice(0, C)), (slice(C, 2 * P), slice(P, C))):
                        ins = nc.vector.tensor_scalar(xn[:, k, to], SRC[:, n, fr], mv[:, n, 0:1],
                                                      rs[:, bass.ds(n, 1)], ALU.subtract, ALU.mult)
                    ins.then_inc(normed, 1)

            normalise(0)

            def low_channels(i):
                dve.wait_ge(t_hi, 2 * i + 1)
                nc.vector.tensor_tensor(tlo[:, :], y[:, 0, :], thi[:, :].bitcast(F32), ALU.subtract).then_inc(t_lo, 1)
                dve.wait_ge(t_hi, 2 * i + 2)
                nc.vector.tensor_tensor(tst[C1:P, :], y[C1:P, 1, :], tst[C1:P, :].bitcast(F32),
                                        ALU.subtract).then_inc(t_lo, 1)

            def low_hidden(i, m):
                dve.wait_ge(h_hi, MT * i + m + 1)
                nc.vector.tensor_tensor(hlo[:, m, :], hf[:, m % 3, :], hhi[:, m, :].bitcast(F32),
                                        ALU.subtract).then_inc(h_lo, 1)

            def output(i, k):
                n = GT * i + k
                dve.wait_ge(fc2, n + 1)
                dve.wait_ge(biased, n + 1)
                passed(dve, x_done, n - 1)
                nc.vector.tensor_tensor(part[:, k % 2, :], ps[:, AB + k, 0:C], X[:, n, :], ALU.add).then_inc(parted, 1)
                dve.wait_ge(parted, n + 1)
                nc.vector.tensor_tensor(X[:, n, :], ps[:, AB + k, C:2 * C], part[:, k % 2, :],
                                        ALU.add).then_inc(x_done, 1)

            def measure(i, k):
                if out is None:
                    n = GT * i + k
                    if k == 0:
                        passed(dve, aggr, GT * i)
                    held(nc, dve, scratch, x_done, n + 1)
                    nc.vector.bn_stats(st[:, k, :], X[:, n, :]).then_inc(stats, 1)

            def collect(i):
                if out is None:
                    passed(dve, filed, i)
                    held(nc, dve, scratch, stats, GT * (i + 1))
                    for k in range(GT):
                        nc.vector.bn_aggr(mvb[:, k, :], st[:, k, :]).then_inc(aggr, 1)
                    dve.wait_ge(aggr, GT * (i + 1))
                    nc.vector.tensor_scalar(mv[:, bass.ds(GT * i, GT), :], mvb[:, :, :], 1.0, None,
                                            ALU.mult).then_inc(filed, 1)

            def group(i):
                head = isinstance(i, int) and i == 0
                low_channels(i)
                if not (isinstance(i, int) and i == N - 1):
                    normalise(i + 1)
                for m in range(MT):
                    if not head and m < GT:
                        output(i - 1, m)
                    low_hidden(i, m)
                if not head:
                    for k in range(GT):
                        measure(i - 1, k)
                    collect(i - 1)

            group(0)
            group(1)
            measure_source(0)
            with dve.Fori(2, LG + 1) as i:
                group(i)
                measure_source(i - 1)
            dve.wait_ge(filed_x, LG)
            add_eps(late_tiles)
            with dve.Fori(LG + 1, LG + 3) as i:
                group(i)
            invert(2, late_tiles)
            with dve.Fori(LG + 3, N - 1) as i:
                group(i)
            group(N - 1)
            for k in range(GT):
                output(N - 1, k)
                measure(N - 1, k)
            collect(N - 1)

        @block.tensor
        def _(pe):
            def turn(i):
                for k in range(2):
                    passed(pe, y_done, 2 * (i - 1) + k + 1)
                    for j in range(GT):
                        if k == 0:
                            pe.wait_ge(normed, GT * i + j + 1)
                            src = xn[:, j, 0:P]
                        else:
                            src = xn[:, j, P:2 * P]
                        mm = pe.transpose(ps[:, TB + k, P * j:P * j + P], src, ident[:, :])
                    mm.then_inc(tposed, 1)

            def first(i):
                for m in range(MT):
                    n = MT * i + m
                    cut = slice(P * m, P * m + P)
                    passed(pe, act1, n - 1)
                    terms = [(w1h[:, 0, cut], thi), (w1l[:, 0, cut], thi), (w1h[:, 1, cut], tst),
                             (w1l[:, 1, cut], tst), (w1h[:, 0, cut], tlo)]
                    if m == 0:
                        pe.wait_ge(t_hi, 2 * i + 1)
                    for q, (w, x) in enumerate(terms):
                        if m == 0 and q == 2:
                            pe.wait_ge(t_lo, 2 * i + 2)
                        mm = pe.matmul(ps[:, RB + m % 2, :], w, x[:, :], start=(q == 0), stop=(q == 4))
                    mm.then_inc(fc1, 1)

            def second(i, by_tile=False):
                passed(pe, x_done, GT * i)
                order = [(m, k) for m in range(MT) for k in range(GT)]
                if by_tile:
                    early = GT * MT // 3
                    order[early:] = sorted(order[early:], key=lambda mk: mk[1])
                for m, k in order:
                    if k == 0:
                        pe.wait_ge(h_lo, MT * i + m + 1)
                    cut = slice(P * k, P * k + P)
                    full = (hhi[:, m, cut], w2hl[:, m].rearrange("p a c -> p (a c)"), ps[:, AB + k, 0:2 * C])
                    low = (hlo[:, m, cut], w2hl[:, m, 0, :], ps[:, AB + k, C:2 * C])
                    for n, (x, w, o) in enumerate((full, low) if m == 0 else (low, full)):
                        mm = pe.matmul(o, x, w, start=(m == 0 and n == 0), stop=(m == MT - 1 and n == 1),
                                       skip_group_check=True)
                    if m == MT - 1:
                        mm.then_inc(fc2, 1)

            turn(0)
            first(0)

            def group(i):
                turn(i + 1)
                second(i)
                first(i + 1)

            rolled(pe, N - 1, group, 1, 0)
            second(N - 1, True)


def gated_scan(nc, t, sh):
    X, mv, ident, wh, wl = sh.X, sh.mv, sh.ident, sh.wh, sh.wl
    pre = "L1_conv_"
    gam, bet, bu, bg = (sh.columns[pre + n] for n in ("norm1_scale", "norm1_bias", "bu", "bg"))
    with ExitStack() as ctx:
        def sb(name, shape, dt=F32):
            return ctx.enter_context(nc.sbuf_tensor("sc_" + name, shape, dt))

        def sem(name):
            return ctx.enter_context(nc.semaphore("sc_" + name))

        NP = NT // (4 * GT)
        ST = 2 * GT
        sd, rs, shift = sb("sd", [P, NT]), sb("rs", [P, NT]), sb("shift", [P, NT])
        xn = sb("xn", [P, GT, 3 * P])
        y = sb("y", [P, 2, GTOK])
        yh, yl = sb("yh", [P, 3, GTOK], F32R), sb("yl", [P, 3, GTOK], F32R)
        gate, nfix, prod, hid = ([sb(f"{n}{c}", [P, 3, GTOK]) for c in range(2)] for n in ("gate", "nfix", "prod", "hid"))
        hi, lo = ([sb(f"{n}{c}", [P, 3, GTOK], F32R) for c in range(2)] for n in ("hi", "lo"))
        ych, ycl = [yh, hi[1]], [yl, lo[1]]
        st = sb("st", [P, 2 * ST, 6])
        mvb = sb("mvb", [P, 2 * ST, 2])
        scratch = words(sb("scratch", [P, 16]))
        ps = ctx.enter_context(nc.psum_tensor("sc_ps", [P, 8, 512], F32))
        loaded, w_hi, w_lo = sem("loaded"), sem("w_hi"), sem("w_lo")
        eps_in, rooted, recip, stats, aggr, filed = (sem(n) for n in ("eps_in", "rooted", "recip", "stats", "aggr", "filed"))
        normed, tposed, y_done, y_hi, y_lo = (sem(n) for n in ("normed", "tposed", "y_done", "y_hi", "y_lo"))
        turned_back, x_done, normed_first = sem("turned_back"), sem("x_done"), sem("normed_first")
        names = ("mm", "u_out", "g_out", "fixed", "mult", "h_done", "h_hi", "h_lo")
        Q = [{n: sem(f"{n}{c}") for n in names} for c in range(2)]
        loads, splits = sh.mlp_loads("L1_conv_"), sh.mlp_splits()
        MM = 3 * (2 + STEPS - 1)
        HL = 3 * (STEPS - 1)
        ROUNDS = [("back", 0, 0), ("back", 0, 1), ("back", 0, 2), ("turn", 1, 0), ("turn", 1, 1), ("back", 0, 3),
                  ("turn", 1, 2), ("back", 1, 0), ("back", 1, 1), ("back", 1, 2), ("back", 1, 3),
                  ("turn", 0, 0), ("turn", 0, 1), ("turn", 0, 2)]
        BRING = {(3, 0): 0, (3, 1): 1, (4, 0): 2}
        NORM0 = {(1, 0): 0, (1, 1): 1, (2, 0): 2, (2, 1): 3}
        NORM1 = {(4, 1): 0, (5, 0): 1, (5, 1): 2, (6, 0): 3}
        LAST_BANKS = [6, 7, 0, 1, 2, 3, 4, 5]
        bank_of = {r: 6 + n % 2 for n, r in enumerate(ROUNDS)}

        block = ctx.enter_context(nc.Block())

        @block.sync
        def _(sp):
            for dst, src in loads:
                sp.dma_start(dst, src).then_inc(loaded, 16)

        def column(j):
            return slice(0, 1) if j < 2 else slice(1, 2)

        @block.gpsimd
        def _(pool):
            def low_channels(m, c, tiles=range(3)):
                for j in tiles:
                    pool.wait_ge(y_hi, 3 * m + j + 1)
                    nc.gpsimd.tensor_tensor(ycl[c][:, j, :], y[:, (3 * c + j) % 2, :], ych[c][:, j, :].bitcast(F32),
                                            ALU.subtract).then_inc(y_lo, 1)

            def low(i, c, s):
                q = Q[c]
                for j in range(3):
                    pool.wait_ge(q["h_hi"], HL * i + 3 * s + j + 1)
                    pool.wait_ge(q["mm"], MM * i + 3 * (s + 2))
                    nc.gpsimd.tensor_tensor(lo[c][:, j, :], hid[c][:, j, :], hi[c][:, j, :].bitcast(F32),
                                            ALU.subtract).then_inc(q["h_lo"], 1)

            def pair(i):
                low_channels(2 * i + 1, 1)
                for s in range(1, STEPS - 1):
                    for c in range(2):
                        low(i, c, s)
                        if (s, c) in BRING and not (isinstance(i, int) and i == NP - 1):
                            low_channels(2 * i + 2, 0, [BRING[s, c]])

            low_channels(0, 0)
            rolled(pool, NP, pair, 0, 1)
            low_parts(nc, pool, splits, w_hi, w_lo)

        @block.scalar
        def _(act):
            act.wait_ge(eps_in, 1)
            nc.scalar.activation(sd[:, :], sd[:, :], ACT.Sqrt).then_inc(rooted, 1)
            sh.load_table(2, ACT.Sigmoid)
            act.wait_ge(recip, 2)

            def normalise(m, quarters=range(GT)):
                for j in quarters:
                    for k in range(2):
                        n = m * ST + GT * k + j
                        for to, fr in ((slice(P * k, P * k + P), slice(0, P)),
                                       (slice(2 * P + C1 * k, 2 * P + C1 * k + C1), slice(P, C))):
                            ins = nc.scalar.activation(xn[:, j, to], X[:, n, fr], ACT.Identity,
                                                       bias=shift[:, bass.ds(n, 1)], scale=rs[:, bass.ds(n, 1)])
                    ins.then_inc(normed, 1)

            def channels(m, c, tiles=range(3)):
                for j in tiles:
                    act.wait_ge(tposed, 3 * m + j + 1)
                    passed(act, y_lo, 3 * m + j - 1)
                    nc.scalar.activation(y[:, (3 * c + j) % 2, :], ps[:, bank_of["turn", c, j], :], ACT.Identity,
                                         bias=bet[:, column(j)], scale=gam[:, column(j)]).then_inc(y_done, 1)
                    act.wait_ge(y_done, 3 * m + j + 1)
                    nc.scalar.activation(ych[c][:, j, :], y[:, (3 * c + j) % 2, :], ACT.Copy).then_inc(y_hi, 1)

            def branch(i, c, w):
                q = Q[c]
                lower, upper = slice(0, C1), slice(C1, P)
                u, g = (prod[c], bu, ACT.Identity), (gate[c], bg, ACT.Sigmoid)
                dst, bias, func = u if w == "U" else g
                base, done = (0, "u_out") if w == "U" else (3, "g_out")
                for j in range(2):
                    act.wait_ge(q["mm"], MM * i + base + j + 1)
                    nc.scalar.activation(dst[:, j, :], ps[:, 3 * c + j, :], func,
                                         bias=bias[:, column(j)]).then_inc(q[done], 1)
                act.wait_ge(q["mm"], MM * i + base + 3)
                to = lower if w == "U" else upper
                for (dst, bias, func), fr in ((u, to), (g, upper if w == "U" else lower)):
                    ins = nc.scalar.activation(dst[to, 2, :], ps[fr, 3 * c + 2, :], func, bias=bias[fr, column(2)])
                ins.then_inc(q[done], 1)

            def high(i, c, s):
                q = Q[c]
                for j in range(3):
                    if s == 0:
                        act.wait_ge(q["fixed"], 3 * i + j + 1)
                        nc.scalar.activation(hi[c][:, j, :], nfix[c][:, j, :], ACT.Copy,
                                             scale=-1.0).then_inc(q["h_hi"], 1)
                    else:
                        act.wait_ge(q["h_done"], HL * i + 3 * (s - 1) + j + 1)
                        nc.scalar.activation(hi[c][:, j, :], hid[c][:, j, :], ACT.Copy).then_inc(q["h_hi"], 1)

            def pair(i):
                branch(i, 0, "U")
                channels(2 * i + 1, 1)
                branch(i, 0, "G")
                branch(i, 1, "U")
                high(i, 0, 0)
                branch(i, 1, "G")
                high(i, 1, 0)
                for s in range(1, STEPS - 1):
                    for c in range(2):
                        high(i, c, s)
                        if isinstance(i, int) and i == NP - 1:
                            continue
                        if (s, c) in NORM0:
                            normalise(2 * i + 2, [NORM0[s, c]])
                        if (s, c) in BRING:
                            channels(2 * i + 2, 0, [BRING[s, c]])
                        if (s, c) in NORM1:
                            normalise(2 * i + 3, [NORM1[s, c]])

            normalise(0, [GT - 1])
            channels(0, 0)
            rolled(act, NP, pair, 0, 1)
            high_parts(nc.scalar, act, splits, loaded, 16 * len(loads), w_hi)
            sh.load_table(0, ACT.Sqrt)

        @block.vector
        def _(dve):
            nc.vector.tensor_scalar(sd[:, :], mv[:, :, 1], EPS1, None, ALU.add).then_inc(eps_in, 1)
            dve.wait_ge(rooted, 1)
            nc.vector.reciprocal(rs[:, :], sd[:, :]).then_inc(recip, 1)
            dve.wait_ge(recip, 1)
            nc.vector.scalar_tensor_tensor(shift[:, :], mv[:, :, 0], -1.0, rs[:, :], ALU.mult,
                                           ALU.mult).then_inc(recip, 1)

            def fix(i, c):
                q = Q[c]
                for j in range(3):
                    dve.wait_ge(q["u_out"], 3 * i + j + 1)
                    dve.wait_ge(q["g_out"], 3 * i + j + 1)
                    nc.vector.scalar_tensor_tensor(nfix[c][:, j, :], gate[c][:, j, :], 1.0, prod[c][:, j, :],
                                                   ALU.subtract, ALU.mult).then_inc(q["fixed"], 1)
                for j in range(3):
                    dve.wait_ge(q["h_hi"], HL * i + j + 1)
                    nc.vector.scalar_tensor_tensor(lo[c][:, j, :], nfix[c][:, j, :], -1.0, hi[c][:, j, :].bitcast(F32),
                                                   ALU.mult, ALU.subtract).then_inc(q["h_lo"], 1)

            def step(i, c, s):
                q = Q[c]
                for j in range(3):
                    dve.wait_ge(q["mm"], MM * i + 3 * (s + 1) + j + 1)
                    nc.vector.tensor_tensor(prod[c][:, j, :], ps[:, 3 * c + j, :], gate[c][:, j, :],
                                            ALU.mult).then_inc(q["mult"], 1)
                    dve.wait_ge(q["mult"], HL * i + 3 * (s - 1) + j + 1)
                    if j == 0 and s > 1:
                        dve.wait_ge(q["h_lo"], HL * i + 3 * s)
                    nc.vector.tensor_tensor(hid[c][:, j, :], prod[c][:, j, :], nfix[c][:, j, :],
                                            ALU.subtract).then_inc(q["h_done"], 1)

            def add_back(i, c, k, bank):
                m = 2 * i + c
                dve.wait_ge(turned_back, GT * m + k + 1)
                v = ps[:, bank, 0:3 * P]
                for a, b, part in ((0, P, v[:, 0:2 * P]), (P, C, v[:, 2 * P:])):
                    dst = X[:, bass.ds(m * ST, ST), a:b].rearrange("p (h j) c -> p h j c", h=2)[:, :, k]
                    nc.vector.tensor_tensor(dst, dst, part.rearrange("p (h c) -> p h c", h=2), ALU.add).then_inc(x_done, 1)

            def measure(i, n):
                if n % ST == 0:
                    passed(dve, aggr, 2 * ST * i)
                    held(nc, dve, scratch, x_done, 4 * GT * i + 2 * GT * (n // ST + 1))
                nc.vector.bn_stats(st[:, n, :], X[:, i * 2 * ST + n, :]).then_inc(stats, 1)

            def collect(i):
                passed(dve, filed, i)
                held(nc, dve, scratch, stats, 2 * ST * (i + 1))
                for k in range(2 * ST):
                    nc.vector.bn_aggr(mvb[:, k, :], st[:, k, :]).then_inc(aggr, 1)
                dve.wait_ge(aggr, 2 * ST * (i + 1))
                nc.vector.tensor_scalar(mv[:, bass.ds(i * 2 * ST, 2 * ST), :], mvb[:, :, :], 1.0, None,
                                        ALU.mult).then_inc(filed, 1)

            def pair(i):
                back = not (isinstance(i, int) and i == 0)
                last = isinstance(i, int) and i == NP - 1
                for c in range(2):
                    for k in range(GT):
                        if back:
                            add_back(i - 1, c, k, bank_of["back", c, k])
                        if (c, k) == (1, 0):
                            fix(i, 0)
                        if (c, k) == (1, 2):
                            fix(i, 1)
                            step(i, 0, 1)
                for s in range(1, STEPS):
                    for c in range(2):
                        if (s, c) != (1, 0):
                            step(i, c, s)
                        n = 2 * (2 * (s - 1) + c - 1)
                        if back and 0 <= n < 2 * ST:
                            measure(i - 1, n)
                            measure(i - 1, n + 1)
                        if back and n == 2 * ST:
                            collect(i - 1)
                        if last and (s, c) == (STEPS - 1, 0):
                            results(0)

            def results(c):
                for k in range(GT):
                    add_back(NP - 1, c, k, LAST_BANKS[GT * c + k])

            for m, j in [(0, j) for j in range(GT - 1)] + [(1, j) for j in range(GT)]:
                if (m, j) == (1, 0):
                    dve.wait_ge(tposed, 3)
                for k in range(2):
                    n = m * ST + GT * k + j
                    for to, fr in ((slice(P * k, P * k + P), slice(0, P)),
                                   (slice(2 * P + C1 * k, 2 * P + C1 * k + C1), slice(P, C))):
                        ins = nc.vector.tensor_scalar(xn[:, j, to], X[:, n, fr], mv[:, n, 0:1], rs[:, n:n + 1],
                                                      ALU.subtract, ALU.mult)
                ins.then_inc(normed_first, 1)
            rolled(dve, NP, pair, 2, 1)
            results(1)

        @block.tensor
        def _(pe):
            def turn(m, c, j):
                for k in range(GT):
                    if j == 0:
                        if isinstance(m, int) and m < 2:
                            if (m, k) == (0, GT - 1):
                                pe.wait_ge(normed, 1)
                            else:
                                pe.wait_ge(normed_first, (GT - 1) * m + k + 1)
                        else:
                            pe.wait_ge(normed, GT * (m - 2) + k + 2)
                    mm = pe.transpose(ps[:, bank_of["turn", c, j], P * k:P * k + P], xn[:, k, P * j:P * j + P], ident[:, :])
                mm.then_inc(tposed, 1)

            def turn_back(i, c, k, bank):
                q = Q[c]
                for j in range(3):
                    if k == 0:
                        pe.wait_ge(q["h_done"], HL * i + 3 * (STEPS - 2) + j + 1)
                    mm = pe.transpose(ps[:, bank, P * j:P * j + P], hid[c][:, j, P * k:P * k + P], ident[:, :])
                mm.then_inc(turned_back, 1)

            def bank_free(i, kind, c, j):
                n = ROUNDS.index((kind, c, j)) - 2
                at = i
                if n < 0:
                    n, at = n + len(ROUNDS), i - 1
                k2, c2, j2 = ROUNDS[n]
                if k2 == "back":
                    passed(pe, x_done, 4 * GT * (at - 1) + 2 * (GT * c2 + j2) + 2)
                else:
                    passed(pe, y_done, 3 * (2 * (at + 1 - c2) + c2) + j2 + 1)

            def back_round(i, c, k):
                if not (isinstance(i, int) and i == 0):
                    bank_free(i, "back", c, k)
                    turn_back(i - 1, c, k, bank_of["back", c, k])

            def turn_round(i, c, j):
                bank_free(i, "turn", c, j)
                turn(2 * i + 1 if c else 2 * i + 2, c, j)

            def product(c, w, h, l, high_in, low_in, midway=None, third_free=None):
                def bank(b):
                    return ps[:, 3 * c + b, :]

                def term(out, ww, rows, cols, x, j, first=False, last=False):
                    return pe.matmul(out, ww[rows, cols], x[rows, j, :], start=first, stop=last, skip_group_check=True)

                every, lower, upper = slice(0, P), slice(0, C1), slice(C1, P)
                if w == "A":
                    from_last, from_first = (every, A11), [(A01_LOWER, 0), (A01_UPPER, 1)]
                else:
                    half = 0 if w == "U" else 1
                    from_last, from_first = ((lower, upper)[half], UG11), [(UG01[half], half)]
                for j in range(2):
                    high_in(j)
                    term(bank(j), wh, every, W00[w], h, j, first=True)
                    term(bank(j), wl, every, W00[w], h, j)
                high_in(2)
                for ww in (wh, wl):
                    for j, rows in enumerate((lower, upper)):
                        term(bank(j), ww, rows, W10[w], h, 2)
                if third_free:
                    third_free()
                for n, ww in enumerate((wh, wl)):
                    term(bank(2), ww, *from_last, h, 2, first=(n == 0))
                for ww in (wh, wl):
                    for cols, j in from_first:
                        term(bank(2), ww, every, cols, h, j)
                if midway:
                    midway()
                for j in range(2):
                    low_in(j)
                    term(bank(j), wh, every, W00[w], l, j)
                low_in(2)
                for j, rows in enumerate((lower, upper)):
                    term(bank(j), wh, rows, W10[w], l, 2, last=True).then_inc(Q[c]["mm"], 1)
                for cols, j in from_first:
                    term(bank(2), wh, every, cols, l, j)
                term(bank(2), wh, *from_last, l, 2, last=True).then_inc(Q[c]["mm"], 1)

            def project(i, c, w, midway=None):
                q = Q[c]
                m = 2 * i + c

                def high_in(j):
                    pe.wait_ge(y_hi, 3 * m + j + 1)
                    if j < 2:
                        bank_read(j)

                def bank_read(j):
                    if w == "U":
                        passed(pe, q["h_done"], HL * (i - 1) + 3 * (STEPS - 2) + j + 1)
                    else:
                        pe.wait_ge(q["u_out"], 3 * i + j + 1)

                def low_in(j):
                    pe.wait_ge(y_lo, 3 * m + j + 1)

                product(c, w, ych[c], ycl[c], high_in, low_in, midway, lambda: bank_read(2))

            def advance(i, c, s):
                q = Q[c]
                last = isinstance(i, int) and (i, c, s) == (NP - 1, 1, STEPS - 1)
                product(c, "A", hi[c], lo[c], lambda j: pe.wait_ge(q["h_hi"], HL * i + 3 * (s - 1) + j + 1),
                        lambda j: pe.wait_ge(q["h_lo"], HL * i + 3 * (s - 1) + j + 1),
                        (lambda: last_back(0)) if last else None)

            def last_back(c):
                for k in range(GT):
                    turn_back(NP - 1, c, k, LAST_BANKS[GT * c + k])

            def pair(i):
                back_round(i, 0, 0)
                back_round(i, 0, 1)
                project(i, 0, "U")
                back_round(i, 0, 2)
                turn_round(i, 1, 0)
                turn_round(i, 1, 1)
                project(i, 0, "G", lambda: (back_round(i, 0, 3), turn_round(i, 1, 2)))
                back_round(i, 1, 0)
                project(i, 1, "U")
                back_round(i, 1, 1)
                project(i, 1, "G")
                back_round(i, 1, 2)
                for s in range(1, STEPS):
                    for c in range(2):
                        advance(i, c, s)
                        if (s, c) == (1, 0):
                            back_round(i, 1, 3)
                        if (s, c) in BRING and not (isinstance(i, int) and i == NP - 1):
                            turn_round(i, 0, BRING[s, c])

            for j in range(3):
                if j == 2:
                    pe.wait_ge(y_done, 1)
                turn(0, 0, j)
            rolled(pe, NP, pair, 2, 1)
            last_back(1)


_OUT = (B, H, W, C)


def kernel(**inputs):
    import concourse.bacc as _bacc
    from concourse.bass_utils import run_bass_kernel_spmd as _run

    nc = _bacc.Bacc("TRN2", target_bir_lowering=False, num_devices=1)
    arrays = {k: np.ascontiguousarray(v) for k, v in inputs.items()}
    arrays |= dict(zip(("fwd_w", "inv_w", "fwd_h", "fwd_h0", "inv_h"), dft_tables()))
    arrays |= {"block_ones": block_ones(), "ident": np.eye(P, dtype=np.float32)}
    t = {k: nc.dram_tensor(f"in_{k}", a.shape, mybir.dt.from_np(a.dtype), kind="ExternalInput").ap()
         for k, a in arrays.items()}
    out = nc.dram_tensor("out_0", _OUT, F32, kind="ExternalOutput").ap()
    build(nc, t, out)
    r = _run(nc, [{f"in_{k}": a for k, a in arrays.items()}], core_ids=[0])
    return r.results[0]["out_0"]
```
